# Optimizing a Trainium2 kernel written in Bass

```python
import numpy as np
import jax
import jax.numpy as jnp

def _softmax(x, axis=-1):
    return jax.nn.softmax(x, axis=axis)

def _gelu(x):
    return jax.nn.gelu(x, approximate=True)

def _silu(x):
    return jax.nn.silu(x)

def _sigmoid(x):
    return jax.nn.sigmoid(x)

def _layernorm(x, axis=-1, eps=1e-05):
    m = jnp.mean(x, axis=axis, keepdims=True)
    v = jnp.var(x, axis=axis, keepdims=True)
    return (x - m) / jnp.sqrt(v + eps)

def _scatter_add(tgt, idx, src, axis=0):
    return tgt.at[idx].add(src)

def _segment_sum(src, seg, n):
    return jax.ops.segment_sum(src, seg, n)
kernel_name = 'mk_seq_postln_d1_jaxref_r8_c1178c'

def setup_inputs(seed: int=0):
    np.random.seed(seed)
    _w = jnp.asarray

    def _L0_attn_setup():
        import jax, jax.numpy as jnp
        import numpy as np
        E = 128
        H = 16
        D = E // H
        K = 4
        MAX_SEQ = 1024
        ROPE_BASE = 10000.0
        SCALE = D ** (-0.5)

        def rotate_half(x):
            half = x.shape[-1] // 2
            return jnp.concatenate([-x[..., half:], x[..., :half]], axis=-1)

        def _rope_cache():
            inv_freq = 1.0 / ROPE_BASE ** (jnp.arange(0, D, 2, dtype=jnp.float32) / D)
            t = jnp.arange(MAX_SEQ, dtype=jnp.float32)
            freqs = jnp.outer(t, inv_freq)
            emb = jnp.concatenate([freqs, freqs], axis=-1)
            return (jnp.cos(emb), jnp.sin(emb))
        key = jax.random.key(seed)
        ks = jax.random.split(key, 6)
        B, S = (2, 256)
        w_scale = E ** (-0.5)
        return {'x': jax.random.normal(ks[0], (B, S, E), dtype=jnp.float32), 'Wq': jax.random.normal(ks[1], (E, E), dtype=jnp.float32) * w_scale, 'Wk': jax.random.normal(ks[2], (E, E), dtype=jnp.float32) * w_scale, 'Wv': jax.random.normal(ks[3], (E, E), dtype=jnp.float32) * w_scale, 'Wr': jax.random.normal(ks[4], (E, H * K), dtype=jnp.float32) * w_scale, 'Wo': jax.random.normal(ks[5], (E, E), dtype=jnp.float32) * w_scale}
    _L0_attn_in = _L0_attn_setup()

    def _L0_ffn_setup():
        import jax, jax.numpy as jnp
        import numpy as np
        DIM = 128
        DEPTH = 2
        HEADS = 8
        DIM_HEAD = 64
        WINDOW = 64
        INNER = HEADS * DIM_HEAD
        HID = int(DIM * 4 * 2 / 3)
        B, N = (2, 1024)
        QK_SCALE = 8.0

        def shift_token(t):
            t1, t2 = jnp.split(t, 2, axis=-1)
            t2 = jnp.pad(t2, ((0, 0), (1, 0), (0, 0)))[:, :-1]
            return jnp.concatenate([t1, t2], axis=-1)

        def l2norm(t):
            return t / jnp.clip(jnp.linalg.norm(t, axis=-1, keepdims=True), 1e-12)

        def rotate_half(x):
            x1, x2 = jnp.split(x, 2, axis=-1)
            return jnp.concatenate([-x2, x1], axis=-1)

        def rotary_xpos(q, k):
            n = q.shape[-2]
            half_idx = jnp.arange(0, DIM_HEAD, 2, dtype=jnp.float32)
            inv_freq = 1.0 / 10000.0 ** (half_idx / DIM_HEAD)
            t = jnp.arange(n, dtype=jnp.float32)
            freqs = t[:, None] * inv_freq[None, :]
            freqs = jnp.concatenate([freqs, freqs], axis=-1)
            base = (half_idx + 0.4 * DIM_HEAD) / (1.4 * DIM_HEAD)
            power = (t - n // 2) / float(WINDOW // 2)
            scale = base[None, :] ** power[:, None]
            scale = jnp.concatenate([scale, scale], axis=-1)
            cos, sin = (jnp.cos(freqs), jnp.sin(freqs))
            q = q * cos * scale + rotate_half(q) * sin * scale
            k = k * cos / scale + rotate_half(k) * sin / scale
            return (q, k)

        def local_attention(q, k, v):
            b, h, n, d = q.shape
            w = n // WINDOW
            bq = q.reshape(b, h, w, WINDOW, d) * QK_SCALE
            bk = k.reshape(b, h, w, WINDOW, d)
            bv = v.reshape(b, h, w, WINDOW, d)

            def look_around(t):
                p = jnp.pad(t, ((0, 0), (0, 0), (1, 0), (0, 0), (0, 0)))
                return jnp.concatenate([p[:, :, :w], p[:, :, 1:]], axis=3)
            bk, bv = (look_around(bk), look_around(bv))
            bt = jnp.arange(n).reshape(w, WINDOW)
            btp = jnp.pad(bt, ((1, 0), (0, 0)), constant_values=-1)
            btk = jnp.concatenate([btp[:w], btp[1:]], axis=1)
            sim = jnp.einsum('bhwid,bhwjd->bhwij', bq, bk)
            i = bt[:, :, None]
            j = btk[:, None, :]
            mask = (i < j) | (i > j + WINDOW) | (j == -1)
            sim = jnp.where(mask, -jnp.finfo(sim.dtype).max, sim)
            attn = jax.nn.softmax(sim, axis=-1)
            out = jnp.einsum('bhwij,bhwjd->bhwid', attn, bv)
            return out.reshape(b, h, n, d)

        def _layer(x, wqkv, qs, ksc, wo, lg, lb, w1, b1, w2, b2):
            b, n, _ = x.shape
            h = shift_token(x)
            qkv = h @ wqkv
            q, k, v = jnp.split(qkv, 3, axis=-1)
            to_heads = lambda t: t.reshape(b, n, HEADS, DIM_HEAD).transpose(0, 2, 1, 3)
            q, k, v = (to_heads(q), to_heads(k), to_heads(v))
            q = l2norm(q) * qs
            k = l2norm(k) * ksc
            q, k = rotary_xpos(q, k)
            o = local_attention(q, k, v)
            o = o.transpose(0, 2, 1, 3).reshape(b, n, INNER)
            x = x + o @ wo
            h = shift_token(x)
            mu = h.mean(-1, keepdims=True)
            var = h.var(-1, keepdims=True)
            h = (h - mu) / jnp.sqrt(var + 1e-05) * lg + lb
            h = h @ w1 + b1
            a, g = jnp.split(h, 2, axis=-1)
            h = a * jax.nn.gelu(g, approximate=False)
            x = x + h @ w2 + b2
            return x
        key = jax.random.key(seed)
        ks = jax.random.split(key, 6)
        return {'x': jax.random.normal(ks[0], (B, N, DIM), jnp.float32), 'wqkv': jax.random.normal(ks[1], (DEPTH, DIM, 3 * INNER), jnp.float32) * 0.02, 'q_scale': jnp.ones((DEPTH, DIM_HEAD), jnp.float32), 'k_scale': jnp.ones((DEPTH, DIM_HEAD), jnp.float32), 'wo': jax.random.normal(ks[2], (DEPTH, INNER, DIM), jnp.float32) * 0.02, 'ln_g': jnp.ones((DEPTH, DIM), jnp.float32), 'ln_b': jnp.zeros((DEPTH, DIM), jnp.float32), 'w1': jax.random.normal(ks[3], (DEPTH, DIM, 2 * HID), jnp.float32) * 0.02, 'b1': jnp.zeros((DEPTH, 2 * HID), jnp.float32), 'w2': jax.random.normal(ks[4], (DEPTH, HID, DIM), jnp.float32) * 0.02, 'b2': jnp.zeros((DEPTH, DIM), jnp.float32)}
    _L0_ffn_in = _L0_ffn_setup()
    _d = {'L0_attn_x': _L0_attn_in['x'], 'L0_attn_Wq': _L0_attn_in['Wq'], 'L0_attn_Wk': _L0_attn_in['Wk'], 'L0_attn_Wv': _L0_attn_in['Wv'], 'L0_attn_Wr': _L0_attn_in['Wr'], 'L0_attn_Wo': _L0_attn_in['Wo'], 'L0_ffn_wqkv': _L0_ffn_in['wqkv'], 'L0_ffn_q_scale': _L0_ffn_in['q_scale'], 'L0_ffn_k_scale': _L0_ffn_in['k_scale'], 'L0_ffn_wo': _L0_ffn_in['wo'], 'L0_ffn_ln_g': _L0_ffn_in['ln_g'], 'L0_ffn_ln_b': _L0_ffn_in['ln_b'], 'L0_ffn_w1': _L0_ffn_in['w1'], 'L0_ffn_b1': _L0_ffn_in['b1'], 'L0_ffn_w2': _L0_ffn_in['w2'], 'L0_ffn_b2': _L0_ffn_in['b2']}
    _x0 = _d['L0_attn_x']
    _d['L0_attn_x'] = jax.random.normal(jax.random.fold_in(jax.random.key(seed), 1), (8, 512, 128), dtype=_x0.dtype)
    del _x0
    return _d

def reference(L0_attn_x, L0_attn_Wq, L0_attn_Wk, L0_attn_Wv, L0_attn_Wr, L0_attn_Wo, L0_ffn_wqkv, L0_ffn_q_scale, L0_ffn_k_scale, L0_ffn_wo, L0_ffn_ln_g, L0_ffn_ln_b, L0_ffn_w1, L0_ffn_b1, L0_ffn_w2, L0_ffn_b2):

    def _L0_attn_ref(x, Wq, Wk, Wv, Wr, Wo):
        import jax, jax.numpy as jnp
        import numpy as np
        E = 128
        H = 16
        D = E // H
        K = 4
        MAX_SEQ = 1024
        ROPE_BASE = 10000.0
        SCALE = D ** (-0.5)

        def rotate_half(x):
            half = x.shape[-1] // 2
            return jnp.concatenate([-x[..., half:], x[..., :half]], axis=-1)

        def _rope_cache():
            inv_freq = 1.0 / ROPE_BASE ** (jnp.arange(0, D, 2, dtype=jnp.float32) / D)
            t = jnp.arange(MAX_SEQ, dtype=jnp.float32)
            freqs = jnp.outer(t, inv_freq)
            emb = jnp.concatenate([freqs, freqs], axis=-1)
            return (jnp.cos(emb), jnp.sin(emb))
        B, S, _ = x.shape
        q = (x @ Wq).reshape(B, S, H, D).transpose(0, 2, 1, 3)
        k = (x @ Wk).reshape(B, S, H, D).transpose(0, 2, 1, 3)
        v = (x @ Wv).reshape(B, S, H, D).transpose(0, 2, 1, 3)
        logits = (x @ Wr).reshape(B, S, H, K).transpose(0, 2, 1, 3)
        node_probs = jax.nn.softmax(logits, axis=-1)
        expected_pos = jnp.cumsum(node_probs, axis=2) - node_probs
        cos_c, sin_c = _rope_cache()
        pos = jnp.clip(expected_pos, 0.0, MAX_SEQ - 1)
        pf = pos.astype(jnp.int32)
        pc = jnp.minimum(pf + 1, MAX_SEQ - 1)
        frac = (pos - pf.astype(pos.dtype))[..., None]
        cos = cos_c[pf] + frac * (cos_c[pc] - cos_c[pf])
        sin = sin_c[pf] + frac * (sin_c[pc] - sin_c[pf])
        cos_w = jnp.einsum('bhsk,bhskd->bhsd', node_probs, cos)
        sin_w = jnp.einsum('bhsk,bhskd->bhsd', node_probs, sin)
        q_r = q * cos_w + rotate_half(q) * sin_w
        k_r = k * cos_w + rotate_half(k) * sin_w
        node_w = jnp.einsum('bhik,bhjk->bhij', node_probs, node_probs)
        scores = jnp.einsum('bhid,bhjd->bhij', q_r, k_r) * SCALE
        scores = scores + jnp.log(node_w + 1e-08)
        causal = jnp.tril(jnp.ones((S, S), dtype=bool))
        scores = jnp.where(causal[None, None], scores, -jnp.inf)
        attn = jax.nn.softmax(scores, axis=-1)
        out = jnp.einsum('bhij,bhjd->bhid', attn, v)
        out = out.transpose(0, 2, 1, 3).reshape(B, S, E)
        return out @ Wo

    def _L0_ffn_ref(x, wqkv, q_scale, k_scale, wo, ln_g, ln_b, w1, b1, w2, b2):
        import jax, jax.numpy as jnp
        import numpy as np
        DIM = 128
        DEPTH = 2
        HEADS = 8
        DIM_HEAD = 64
        WINDOW = 64
        INNER = HEADS * DIM_HEAD
        HID = int(DIM * 4 * 2 / 3)
        B, N = (2, 1024)
        QK_SCALE = 8.0

        def shift_token(t):
            t1, t2 = jnp.split(t, 2, axis=-1)
            t2 = jnp.pad(t2, ((0, 0), (1, 0), (0, 0)))[:, :-1]
            return jnp.concatenate([t1, t2], axis=-1)

        def l2norm(t):
            return t / jnp.clip(jnp.linalg.norm(t, axis=-1, keepdims=True), 1e-12)

        def rotate_half(x):
            x1, x2 = jnp.split(x, 2, axis=-1)
            return jnp.concatenate([-x2, x1], axis=-1)

        def rotary_xpos(q, k):
            n = q.shape[-2]
            half_idx = jnp.arange(0, DIM_HEAD, 2, dtype=jnp.float32)
            inv_freq = 1.0 / 10000.0 ** (half_idx / DIM_HEAD)
            t = jnp.arange(n, dtype=jnp.float32)
            freqs = t[:, None] * inv_freq[None, :]
            freqs = jnp.concatenate([freqs, freqs], axis=-1)
            base = (half_idx + 0.4 * DIM_HEAD) / (1.4 * DIM_HEAD)
            power = (t - n // 2) / float(WINDOW // 2)
            scale = base[None, :] ** power[:, None]
            scale = jnp.concatenate([scale, scale], axis=-1)
            cos, sin = (jnp.cos(freqs), jnp.sin(freqs))
            q = q * cos * scale + rotate_half(q) * sin * scale
            k = k * cos / scale + rotate_half(k) * sin / scale
            return (q, k)

        def local_attention(q, k, v):
            b, h, n, d = q.shape
            w = n // WINDOW
            bq = q.reshape(b, h, w, WINDOW, d) * QK_SCALE
            bk = k.reshape(b, h, w, WINDOW, d)
            bv = v.reshape(b, h, w, WINDOW, d)

            def look_around(t):
                p = jnp.pad(t, ((0, 0), (0, 0), (1, 0), (0, 0), (0, 0)))
                return jnp.concatenate([p[:, :, :w], p[:, :, 1:]], axis=3)
            bk, bv = (look_around(bk), look_around(bv))
            bt = jnp.arange(n).reshape(w, WINDOW)
            btp = jnp.pad(bt, ((1, 0), (0, 0)), constant_values=-1)
            btk = jnp.concatenate([btp[:w], btp[1:]], axis=1)
            sim = jnp.einsum('bhwid,bhwjd->bhwij', bq, bk)
            i = bt[:, :, None]
            j = btk[:, None, :]
            mask = (i < j) | (i > j + WINDOW) | (j == -1)
            sim = jnp.where(mask, -jnp.finfo(sim.dtype).max, sim)
            attn = jax.nn.softmax(sim, axis=-1)
            out = jnp.einsum('bhwij,bhwjd->bhwid', attn, bv)
            return out.reshape(b, h, n, d)

        def _layer(x, wqkv, qs, ksc, wo, lg, lb, w1, b1, w2, b2):
            b, n, _ = x.shape
            h = shift_token(x)
            qkv = h @ wqkv
            q, k, v = jnp.split(qkv, 3, axis=-1)
            to_heads = lambda t: t.reshape(b, n, HEADS, DIM_HEAD).transpose(0, 2, 1, 3)
            q, k, v = (to_heads(q), to_heads(k), to_heads(v))
            q = l2norm(q) * qs
            k = l2norm(k) * ksc
            q, k = rotary_xpos(q, k)
            o = local_attention(q, k, v)
            o = o.transpose(0, 2, 1, 3).reshape(b, n, INNER)
            x = x + o @ wo
            h = shift_token(x)
            mu = h.mean(-1, keepdims=True)
            var = h.var(-1, keepdims=True)
            h = (h - mu) / jnp.sqrt(var + 1e-05) * lg + lb
            h = h @ w1 + b1
            a, g = jnp.split(h, 2, axis=-1)
            h = a * jax.nn.gelu(g, approximate=False)
            x = x + h @ w2 + b2
            return x
        for l in range(DEPTH):
            x = _layer(x, wqkv[l], q_scale[l], k_scale[l], wo[l], ln_g[l], ln_b[l], w1[l], b1[l], w2[l], b2[l])
        return x
    x = L0_attn_x
    x = _layernorm(x + _L0_attn_ref(x, L0_attn_Wq, L0_attn_Wk, L0_attn_Wv, L0_attn_Wr, L0_attn_Wo), axis=-1)
    x = _layernorm(x + _L0_ffn_ref(x, L0_ffn_wqkv, L0_ffn_q_scale, L0_ffn_k_scale, L0_ffn_wo, L0_ffn_ln_g, L0_ffn_ln_b, L0_ffn_w1, L0_ffn_b1, L0_ffn_w2, L0_ffn_b2), axis=-1)
    return x

_drawn_inputs = setup_inputs


def setup_inputs(seed=0):
    import zlib

    import numpy as np

    out = dict(_drawn_inputs(seed))
    spreads = {'L0_ffn_q_scale': (1.0, 0.6),
     'L0_ffn_k_scale': (1.0, 0.6),
     'L0_ffn_ln_g': (1.0, 0.6),
     'L0_ffn_ln_b': (0.0, 0.8),
     'L0_ffn_b1': (0.0, 0.8),
     'L0_ffn_b2': (0.0, 0.449)}
    factors = {'L0_ffn_wqkv': 3.448, 'L0_ffn_wo': 3.433, 'L0_ffn_w1': 6.212, 'L0_ffn_w2': 6.117}
    for name, (base, spread) in spreads.items():
        noise = np.random.default_rng([zlib.crc32(name.encode()), seed]).standard_normal(out[name].shape)
        drawn = base * np.exp(spread * noise) if base else spread * noise
        out[name] = jnp.asarray(drawn.astype(out[name].dtype))
    for name, factor in factors.items():
        out[name] = (out[name] * factor).astype(out[name].dtype)
    return out
```

```python
from contextlib import ExitStack

import numpy as np

import concourse.bass as bass
from concourse import mybir

ALU = mybir.AluOpType
ACT = mybir.ActivationFunctionType
AX_X = mybir.AxisListType.X
F32 = mybir.dt.float32
BF16 = mybir.dt.bfloat16

P = 128
BATCH, SEQ, DIM = 8, 512, 128
TILES = SEQ // P

HEADS_A, HD_A, NODES = 16, 8, 4
FREQS = HD_A // 2
HN = HEADS_A * NODES
PAIRS = HEADS_A // 2
AUG = HD_A + 1
SCALE_A = HD_A ** -0.5
MAX_POS = 1023.0
ROUND = 12582912.0
SPLIT_PRODUCTS = ((0, 0), (0, 1), (1, 0), (0, 2), (2, 0), (1, 1))
SPLIT_ROWS = len(SPLIT_PRODUCTS) * HD_A
E_COLS = [SEQ - P * j for j in range(TILES)]
E_OFF = [sum(E_COLS[:j]) for j in range(TILES)]

DEPTH, HEADS_B, HD_B, WINDOW = 2, 8, 64, 64
INNER = HEADS_B * HD_B
CHUNKS = INNER // P
HID = int(DIM * 4 * 2 / 3)
HID_PARTS = [(0, P), (P, P), (2 * P, HID - 2 * P)]
QK_SCALE = 8.0
SPAN = P + WINDOW
PAD = SEQ + WINDOW
LN_EPS = 1e-5
NORM_MIN = 1e-12
MASKED = -1e30


def rope_freqs():
    return 1.0 / 10000.0 ** (np.arange(0, HD_A, 2) / HD_A)


def constants():

    bf = mybir.dt.np(BF16)
    c = {}
    c["ident"] = np.eye(P, dtype=np.float32)
    c["ident_b"] = np.eye(P).astype(bf)
    s, t = np.arange(P)[:, None], np.arange(SEQ)[None, :]
    c["before"] = (s < t).astype(np.float32)
    i, j = np.arange(P)[:, None], np.arange(P)[None, :]
    c["mask_a"] = np.stack([np.where(j > i, MASKED, 0), np.where(j < i, MASKED, 0)], 1).astype(bf)
    sel = np.zeros((P, 2, 2, FREQS, P))
    for f, fr in enumerate(rope_freqs()):
        co, si = np.cos(fr), np.sin(fr)
        for h in range(HEADS_A):
            for k in range(NODES):
                for d in (f, f + FREQS):
                    rc, rs, col = h * NODES + k, HN + h * NODES + k, h * HD_A + d
                    sign = -1.0 if d < FREQS else 1.0
                    sel[rc, 0, 0, f, col], sel[rc, 0, 1, f, col], sel[rs, 0, 1, f, col] = 1, co, -si
                    sel[rs, 1, 0, f, col], sel[rc, 1, 1, f, col], sel[rs, 1, 1, f, col] = sign, sign * si, sign * co
    c["sel_rope"] = sel.reshape(P, -1).astype(np.float32)
    half = (np.arange(P) < HN).astype(np.float64)
    c["cols"] = np.stack([0.25 * half, np.pi / 2 * half, np.full(P, LN_EPS)], 1).astype(np.float32)
    shift = np.zeros((4, PAIRS, 2, SEQ))
    shift[0:2, :, 0], shift[2:4, :, 1] = -1, -1
    c["shift_rows"] = shift.astype(bf)
    jj = np.arange(SPAN)[None, :]
    band = np.where((jj - WINDOW <= i) & (jj >= i), 0, MASKED)
    first = np.where(jj >= WINDOW, band, MASKED)
    ahead = np.where((jj - i >= 0) & (jj - i <= WINDOW), 0, MASKED)
    c["mask_b"] = np.stack([first, band, ahead], 1).astype(bf)
    neg = np.zeros((2 * HEADS_B, HEADS_B, P))
    for h in range(HEADS_B):
        neg[2 * h:2 * h + 2, h] = -1
    c["neg_sel"] = neg.astype(bf)
    half_idx = np.arange(0, HD_B, 2, dtype=np.float64)
    inv = (1.0 / 10000.0 ** (half_idx / HD_B)).astype(np.float32)
    pos = np.arange(SEQ, dtype=np.float32)
    fr = (pos[:, None] * inv[None, :]).astype(np.float64)
    base = (half_idx + 0.4 * HD_B) / (1.4 * HD_B)
    sc = base[None, :] ** ((pos.astype(np.float64) - SEQ // 2) / (WINDOW // 2))[:, None]
    two = lambda a: np.concatenate([a, a], 1)
    signed = np.concatenate([-np.sin(fr), np.sin(fr)], 1)
    tab = np.stack([np.stack([two(np.cos(fr) * sc), two(np.cos(fr) / sc)], 1),
                    np.stack([signed * two(sc), signed / two(sc)], 1)], 1)
    c["xpos"] = tab.reshape(TILES, P, 2, 2, HD_B).transpose(1, 2, 0, 3, 4).reshape(P, -1).astype(np.float32)
    return c


def chain(eng, sem):
    count = [0]

    def link(ins):
        count[0] += 1
        ins.then_inc(sem, 1)
        eng.wait_ge(sem, count[0])
    return link


def bcast(ap, n):
    return ap.unsqueeze(len(ap.shape)).broadcast_to(list(ap.shape) + [n])


def bcast_mid(ap, axis, n):
    shape = list(ap.shape)
    return ap.unsqueeze(axis).broadcast_to(shape[:axis] + [n] + shape[axis:])


class Sems:

    def __init__(self, nc, ctx, names, prefix):
        self.all = {n: ctx.enter_context(nc.semaphore(f"{prefix}_{n}")) for n in names.split()}

    def __getitem__(self, n):
        return self.all[n]


def soft_rope_attention(nc, io, xs, scratch, loops=BATCH):
    ctx = ExitStack()
    with ctx:
        def sb(name, shape, dt=F32):
            return ctx.enter_context(nc.sbuf_tensor("a_" + name, shape, dt))

        ident, ident_b = sb("ident", [P, P]), sb("ident_b", [P, P], BF16)
        before, mask = sb("before", [P, SEQ]), sb("mask", [P, 2, P], BF16)
        sel = sb("sel", [P, 2, 2, FREQS, P])
        cols = sb("cols", [P, 3])
        w_vr, w_qk, w_o = sb("w_vr", [P, DIM + HN]), sb("w_qk", [P, 4, DIM]), sb("w_o", [P, DIM])
        x, xT = sb("x", [P, TILES, DIM]), sb("xT", [P, SEQ])
        lg, ex = sb("lg", [P, TILES, HN]), sb("ex", [P, TILES, HN])
        v1 = sb("v1", [P, TILES, HEADS_A, AUG])
        mx, sm, rsm = (sb(n, [P, TILES, HEADS_A]) for n in ("mx", "sm", "rsm"))
        prob = sb("prob", [P, TILES, 2, HN])
        probe = sb("probe", [P, TILES, HN])
        v2 = sb("v2", [P, TILES, HEADS_A, 64])
        posc, pn, fr, pT, pnext, phere = (sb(n, [P, SEQ]) for n in ("posc", "pn", "fr", "pT", "pnext", "phere"))
        kk, zz = sb("kk", [P, 3, SEQ]), sb("zz", [P, 3, SEQ])
        G, U, V = (sb(n, [P, FREQS, SEQ]) for n in ("G", "U", "V"))
        cw = sb("cw", [P, 2, SEQ])
        tq, tk = kk[:, 0:2, :], zz[:, 0:2, :]
        qk, rem = sb("qk", [P, 2, SEQ]), sb("rem", [P, 2, SEQ])
        s3 = sb("s3", [P, 3, 2, SEQ], BF16)
        q6, k6 = sb("q6", [P, PAIRS, SEQ], BF16), sb("k6", [P, PAIRS, 2, SEQ], BF16)
        mN, mS, mT = sb("mN", [P, TILES, HEADS_A]), sb("mS", [P, TILES, HEADS_A, 2], BF16), sb("mT", [32, SEQ], BF16)
        E = [sb(f"E{i}", [P, 2, sum(E_COLS)]) for i in range(2)]
        Ot = [sb(f"Ot{i}", [P, SEQ]) for i in range(2)]
        Zn = sb("Zn", [P, TILES, HEADS_A, NODES * AUG])
        num, rden = sb("num", [P, TILES * HEADS_A, AUG]), sb("rden", [P, TILES * HEADS_A])
        att, aT = sb("att", [P, TILES, DIM]), sb("aT", [P, SEQ])
        y, y2, x1T = sb("y", [P, TILES, DIM]), sb("y2", [P, TILES, DIM]), sb("x1T", [P, SEQ])
        st, mv = sb("st", [P, TILES, 6]), sb("mv", [P, TILES, 2])
        lnv, rstd = sb("lnv", [P, TILES]), sb("rstd", [P, TILES])
        ps = ctx.enter_context(nc.psum_tensor("a_ps", [P, 8, SEQ], F32))

        ld = ctx.enter_context(nc.semaphore("a_consts_loaded"))
        zeroed = ctx.enter_context(nc.semaphore("a_zeroed"))
        S = Sems(nc, ctx, """x_loaded xT_ps xT_sb vr_ps lg_sb v1_sb lg_shifted ex_sb prob_sb pos_ps pT_ps pT_sb
            pn_sb parts_sb z_sb G_sb U_sb V_sb v2_sb qk_ps rope_ps cw_sb turned qk_sb split_sb split_out packed
            s_ps max_sb mS_sb mT_ps mT_sb m_rows sT_ps E_sb pv_ps Ot_sb tr_ps Z_sb att_sb aT_ps aT_sb o_ps var_sb
            rstd_sb x1_sb x1T_ps x1T_sb stored dve_order pool_order act_order""", "a")

        with nc.Block() as block:
            @block.sync
            def _(sp):
                sp.dma_start(ident[:], io["ident"]).then_inc(ld, 16)
                sp.dma_start(ident_b[:], io["ident_b"]).then_inc(ld, 16)
                sp.dma_start(before[:], io["before"]).then_inc(ld, 16)
                sp.dma_start(mask[:], io["mask_a"]).then_inc(ld, 16)
                sp.dma_start(sel[:].rearrange("p a b f m -> p (a b f m)"), io["sel_rope"]).then_inc(ld, 16)
                sp.dma_start(cols[:], io["cols"]).then_inc(ld, 16)
                sp.dma_start(w_vr[:], io["w_vr"]).then_inc(ld, 16)
                sp.dma_start(w_qk[:], io["w_qk"].rearrange("a p m -> p a m")).then_inc(ld, 16)
                sp.dma_start(w_o[:], io["w_o"]).then_inc(ld, 16)
                sp.wait_ge(zeroed, 1)
                sp.dma_start(k6[2 * SPLIT_ROWS:2 * SPLIT_ROWS + 4, :, :, :], io["shift_rows"]).then_inc(ld, 16)
                sp.wait_ge(ld, 160)

            @block.gpsimd
            def _(pool):
                nc.gpsimd.memset(k6[:], 0.0).then_inc(zeroed, 1)
                nc.gpsimd.memset(v2[:], 0.0).then_inc(zeroed, 1)
                nc.gpsimd.memset(v1[:], 1.0).then_inc(zeroed, 1)

        RING = [(0, 1), (2, 3), (4, 5)]

        with nc.Fori(0, loops) as b:
            with nc.Block() as block:
                @block.sync
                def _(sp):
                    sp.dma_start(x[:], io["L0_attn_x"][b].rearrange("(i p) e -> p i e", p=P)).then_inc(S["x_loaded"], 16)
                    sp.wait_ge(S["split_sb"], 1)
                    sp.dma_start(scratch.rearrange("s t h d n -> (h d) s t n"), s3[:]).then_inc(S["split_out"], 16)
                    sp.wait_ge(S["split_out"], 16)
                    for e in range(2):
                        for n, (qs, ks) in enumerate(SPLIT_PRODUCTS):
                            r = SPLIT_ROWS * e + HD_A * n
                            sp.dma_start(q6[r:r + HD_A, :, :],
                                         scratch[qs, 0].rearrange("(p e) d n -> e d p n", e=2)[e]).then_inc(S["packed"], 16)
                            sp.dma_start(k6[r:r + HD_A, :, e, :],
                                         scratch[ks, 1].rearrange("(p e) d n -> e d p n", e=2)[e]).then_inc(S["packed"], 16)
                    sp.wait_ge(S["mT_sb"], 1)
                    for p in range(PAIRS):
                        sp.dma_start(q6[2 * SPLIT_ROWS:2 * SPLIT_ROWS + 4, p, :], mT[4 * p:4 * p + 4, :]).then_inc(S["m_rows"], 16)
                    sp.wait_ge(S["x1T_sb"], 1)
                    sp.dma_start(xs[0, b], x1T[:]).then_inc(S["stored"], 16)
                    sp.wait_ge(S["stored"], 16)

                @block.tensor
                def _(pe):
                    pe.wait_ge(S["x_loaded"], 16)
                    for i in range(TILES):
                        last = pe.transpose(ps[:, 0, P * i:P * i + P], x[:, i, :], ident[:])
                    last.then_inc(S["xT_ps"], 1)
                    pe.wait_ge(S["xT_sb"], 1)
                    for i in range(TILES):
                        o = (i % 2) * (DIM + HN)
                        last = pe.matmul(ps[:, 1 + i // 2, o:o + DIM + HN], xT[:, P * i:P * i + P], w_vr[:], start=True, stop=True)
                    last.then_inc(S["vr_ps"], 1)
                    pe.wait_ge(S["prob_sb"], 2)
                    for i in range(TILES):
                        last = pe.matmul(ps[:, 3, P * i:SEQ], prob[:, i, :, :].rearrange("p r n -> p (r n)"), before[:, 0:SEQ - P * i],
                                         start=i == 0, stop=i == TILES - 1)
                    last.then_inc(S["pos_ps"], 1)
                    for i in range(TILES):
                        last = pe.transpose(ps[:, 4, P * i:P * i + P], prob[:, i, :, :].rearrange("p r n -> p (r n)"), ident[:])
                    last.then_inc(S["pT_ps"], 1)
                    pe.wait_ge(S["lg_sb"], 2)
                    pe.wait_ge(S["v1_sb"], 2)
                    pe.wait_ge(S["pn_sb"], 1)
                    for n in range(4):
                        pe.matmul(ps[:, n, :], w_qk[:, n, :], xT[:], start=True, stop=True).then_inc(S["qk_ps"], 1)
                    pe.wait_ge(S["U_sb"], 1)
                    pe.wait_ge(S["V_sb"], 1)
                    for t in range(2):
                        for n in range(2 * FREQS):
                            src = (U, V)[n % 2]
                            last = pe.matmul(ps[:, 5 + t, :], sel[:, t, n % 2, n // 2, :], src[:, n // 2, :],
                                             start=n == 0, stop=n == 2 * FREQS - 1)
                        last.then_inc(S["rope_ps"], 1)
                    pe.wait_ge(S["packed"], 16 * 4 * len(SPLIT_PRODUCTS))
                    pe.wait_ge(S["turned"], 2)
                    pe.wait_ge(S["cw_sb"], 2)
                    unit = 0
                    for p in range(PAIRS):
                        for i in range(TILES):
                            if unit >= 3:
                                pe.wait_ge(S["max_sb"], unit - 2)
                            for e in range(2):
                                o = ps[:, RING[unit % 3][e], 0:P * i + P]
                                pe.matmul(o, q6[0:2 * SPLIT_ROWS, p, P * i:P * i + P], k6[0:2 * SPLIT_ROWS, p, e, 0:P * i + P],
                                          start=True, stop=False)
                                last = pe.matmul(o[:, P * i:P * i + P], ident_b[:], mask[:, 0, :], start=False, stop=True)
                            last.then_inc(S["s_ps"], 1)
                            unit += 1
                    pe.wait_ge(S["mS_sb"], 2)
                    for i in range(TILES):
                        last = pe.transpose(ps[0:32, 6, :].bitcast(BF16)[:, P * i:P * i + P],
                                            mS[:, i, :, :].rearrange("p h l -> p (h l)"), ident_b[:])
                    last.then_inc(S["mT_ps"], 1)
                    pe.wait_ge(S["m_rows"], 16 * PAIRS)
                    pe.wait_ge(S["v2_sb"], 1)

                    def weights(p, e, i):
                        off = E_OFF[i]
                        return E[p % 2][:, e, off:off + E_COLS[i]]

                    for p in range(PAIRS + 2):
                        if p < PAIRS:
                            for j in range(TILES):
                                t = TILES * p + j
                                if t >= 3:
                                    pe.wait_ge(S["E_sb"], t - 2)
                                for e in range(2):
                                    o = ps[:, RING[(unit + t) % 3][e], 0:E_COLS[j]]
                                    pe.matmul(o, k6[0:2 * SPLIT_ROWS + 4, p, e, P * j:P * j + P], q6[0:2 * SPLIT_ROWS + 4, p, P * j:SEQ],
                                              start=True, stop=False)
                                    last = pe.matmul(o[:, 0:P], ident_b[:], mask[:, 1, :], start=False, stop=True)
                                last.then_inc(S["sT_ps"], 1)
                        if 1 <= p <= PAIRS:
                            c = p - 1
                            if c == 0:
                                pe.wait_ge(S["mT_sb"], 1)
                            else:
                                pe.wait_ge(S["Ot_sb"], c)
                            for j in range(TILES):
                                pe.wait_ge(S["E_sb"], TILES * c + j + 1)
                                for e in range(2):
                                    last = pe.matmul(ps[64 * e:64 * e + 64, 6, P * j:SEQ], v2[:, j, 2 * c + e, :], weights(c, e, j),
                                                     start=j == 0, stop=j == TILES - 1)
                            last.then_inc(S["pv_ps"], 1)
                        if p >= 2:
                            c = p - 2
                            pe.wait_ge(S["Ot_sb"], c + 1)
                            if c >= 1:
                                pe.wait_ge(S["Z_sb"], c)
                            for i in range(TILES):
                                last = pe.transpose(ps[:, 7, P * i:P * i + P], Ot[c % 2][:, P * i:P * i + P], ident[:])
                            last.then_inc(S["tr_ps"], 1)
                    pe.wait_ge(S["att_sb"], 1)
                    for i in range(TILES):
                        last = pe.transpose(ps[:, 0, P * i:P * i + P], att[:, i, :], ident[:])
                    last.then_inc(S["aT_ps"], 1)
                    pe.wait_ge(S["aT_sb"], 1)
                    for i in range(TILES):
                        last = pe.matmul(ps[:, 1, P * i:P * i + P], aT[:, P * i:P * i + P], w_o[:], start=True, stop=True)
                    last.then_inc(S["o_ps"], 1)
                    pe.wait_ge(S["x1_sb"], TILES)
                    for i in range(TILES):
                        last = pe.transpose(ps[:, 2, P * i:P * i + P], y2[:, i, :], ident[:])
                    last.then_inc(S["x1T_ps"], 1)

                @block.vector
                def _(dve):
                    link = chain(dve, S["dve_order"])
                    dve.wait_ge(S["lg_sb"], 2)
                    nodes = "p i (h n) -> p (i h) n"
                    flat = "p i h -> p (i h)"
                    link(dve.tensor_reduce(mx[:].rearrange(flat), lg[:].rearrange(nodes, n=NODES), AX_X, ALU.max))
                    dve.tensor_tensor(lg[:].rearrange(nodes, n=NODES), lg[:].rearrange(nodes, n=NODES),
                                      bcast(mx[:].rearrange(flat), NODES), ALU.subtract).then_inc(S["lg_shifted"], 1)
                    dve.wait_ge(S["ex_sb"], 1)
                    link(dve.tensor_reduce(sm[:].rearrange(flat), ex[:].rearrange(nodes, n=NODES), AX_X, ALU.add))
                    link(dve.reciprocal(rsm[:], sm[:]))
                    for r in range(2):
                        dve.tensor_tensor(prob[:, :, r, :].rearrange("p i (h n) -> p i h n", n=NODES),
                                          ex[:].rearrange("p i (h n) -> p i h n", n=NODES), bcast(rsm[:], NODES),
                                          ALU.mult).then_inc(S["prob_sb"], 1)
                    dve.wait_ge(S["pos_ps"], 1)
                    link(dve.tensor_scalar(posc[:], ps[:, 3, :], 0.0, MAX_POS, ALU.max, ALU.min))
                    link(dve.tensor_scalar(pn[:], posc[:], -0.5, ROUND, ALU.add, ALU.add))
                    dve.tensor_scalar(pn[:], pn[:], ROUND, None, ALU.subtract).then_inc(S["pn_sb"], 1)
                    dve.wait_ge(S["pn_sb"], 1)
                    fqs = rope_freqs()
                    for f in range(3):
                        ins = dve.tensor_scalar(kk[:, f, :], pn[:], float(fqs[f] / (2 * np.pi)), cols[:, 0:1], ALU.mult, ALU.add)
                        if f == 2:
                            link(ins)
                        else:
                            ins.then_inc(S["z_sb"], 1)
                    dve.wait_ge(S["z_sb"], 2)
                    link(dve.tensor_scalar(kk[:], kk[:], ROUND, ROUND, ALU.add, ALU.subtract))
                    for f, high in enumerate((6.28125, 62.8125, 628.3125)):
                        link(dve.scalar_tensor_tensor(zz[:, f, :], kk[:, f, :], -high, pn[:], ALU.mult, ALU.add))
                        dve.scalar_tensor_tensor(zz[:, f, :], kk[:, f, :], -float(2 * np.pi / fqs[f] - high), zz[:, f, :],
                                                 ALU.mult, ALU.add).then_inc(S["z_sb"], 1)
                    link(dve.tensor_tensor(fr[:], posc[:], pn[:], ALU.subtract))
                    dve.wait_ge(S["pT_sb"], 1)
                    dve.tensor_tensor(pnext[:], pT[:], fr[:], ALU.mult).then_inc(S["parts_sb"], 1)
                    dve.wait_ge(S["parts_sb"], 1)
                    dve.tensor_tensor(phere[:], pT[:], pnext[:], ALU.subtract).then_inc(S["parts_sb"], 1)
                    dve.wait_ge(S["parts_sb"], 2)
                    dve.wait_ge(S["G_sb"], FREQS)
                    dve.tensor_tensor(U[:], G[:], bcast_mid(phere[:], 1, FREQS), ALU.mult).then_inc(S["U_sb"], 1)
                    dve.wait_ge(S["qk_ps"], 4)
                    dve.wait_ge(S["cw_sb"], 2)
                    dve.tensor_tensor(tq, ps[:, 0:2, :], cw[:], ALU.mult).then_inc(S["turned"], 1)
                    dve.wait_ge(S["G_sb"], FREQS)
                    dve.tensor_tensor(tk, ps[:, 2:4, :], cw[:], ALU.mult).then_inc(S["turned"], 1)
                    dve.wait_ge(S["qk_sb"], 2)
                    link(dve.tensor_copy(s3[:, 0, :, :], qk[:]))
                    link(dve.tensor_tensor(rem[:], qk[:], s3[:, 0, :, :], ALU.subtract))
                    link(dve.tensor_copy(s3[:, 1, :, :], rem[:]))
                    dve.tensor_tensor(s3[:, 2, :, :], rem[:], s3[:, 1, :, :], ALU.subtract).then_inc(S["split_sb"], 1)
                    unit = 0
                    for p in range(PAIRS):
                        for i in range(TILES):
                            dve.wait_ge(S["s_ps"], unit + 1)
                            lo = RING[unit % 3][0]
                            dve.tensor_reduce(mN[:, i, 2 * p:2 * p + 2], ps[:, lo:lo + 2, 0:P * i + P], AX_X, ALU.max).then_inc(S["max_sb"], 1)
                            unit += 1
                    dve.wait_ge(S["max_sb"], unit)
                    mh, ml = mS[:, :, :, 0], mS[:, :, :, 1]
                    dve.tensor_copy(mh, mN[:]).then_inc(S["mS_sb"], 1)
                    dve.wait_ge(S["mS_sb"], 1)
                    dve.tensor_tensor(ml, mN[:], mh, ALU.subtract).then_inc(S["mS_sb"], 1)
                    for p in range(PAIRS):
                        dve.wait_ge(S["tr_ps"], p + 1)
                        for e in range(2):
                            h = 2 * p + e
                            src = ps[:, 7, :].rearrange("p (i m) -> p i m", i=TILES)[:, :, 64 * e:64 * e + NODES * AUG]
                            last = dve.tensor_tensor(Zn[:, :, h, :].rearrange("p i (n d) -> p i n d", n=NODES),
                                                     src.rearrange("p i (n d) -> p i n d", n=NODES),
                                                     bcast(prob[:, :, 0, NODES * h:NODES * h + NODES], AUG), ALU.mult)
                            last.then_inc(S["Z_sb"], 1) if e else last.then_inc(S["dve_order"], 1)
                    dve.wait_ge(S["Z_sb"], PAIRS)
                    return_sum(dve, S, Zn, num, rden, att)
                    dve.wait_ge(S["o_ps"], 1)
                    dve.tensor_tensor(y[:], ps[:, 1, :].rearrange("p (i e) -> p i e", i=TILES), x[:], ALU.add).then_inc(S["var_sb"], 1)
                    dve.wait_ge(S["var_sb"], 1)
                    for i in range(TILES):
                        dve.bn_stats(st[:, i, :], y[:, i, :]).then_inc(S["var_sb"], 1)
                    dve.wait_ge(S["var_sb"], 1 + TILES)
                    for i in range(TILES):
                        dve.bn_aggr(mv[:, i, :], st[:, i, :]).then_inc(S["var_sb"], 1)
                    dve.wait_ge(S["var_sb"], 1 + 2 * TILES)
                    dve.wait_ge(S["rstd_sb"], 1)
                    for i in range(TILES):
                        dve.tensor_scalar(y2[:, i, :], y[:, i, :], mv[:, i, 0:1], rstd[:, i:i + 1], ALU.subtract, ALU.mult).then_inc(S["x1_sb"], 1)

                @block.scalar
                def _(act):
                    act.wait_ge(S["xT_ps"], 1)
                    act.activation(xT[:], ps[:, 0, :], ACT.Copy).then_inc(S["xT_sb"], 1)
                    act.wait_ge(S["vr_ps"], 1)
                    for c in range(2):
                        vr = ps[:, 1 + c, 0:2 * (DIM + HN)].rearrange("p (i m) -> p i m", i=2)
                        act.activation(lg[:, 2 * c:2 * c + 2, :], vr[:, :, DIM:], ACT.Copy).then_inc(S["lg_sb"], 1)
                        act.activation(v1[:, 2 * c:2 * c + 2, :, 0:HD_A], vr[:, :, 0:DIM].rearrange("p i (h d) -> p i h d", d=HD_A),
                                       ACT.Copy).then_inc(S["v1_sb"], 1)
                    act.wait_ge(S["lg_shifted"], 1)
                    act.activation(ex[:], lg[:], ACT.Exp).then_inc(S["ex_sb"], 1)
                    act.wait_ge(S["pT_ps"], 1)
                    act.activation(pT[:], ps[:, 4, :], ACT.Copy).then_inc(S["pT_sb"], 1)
                    fqs = rope_freqs()
                    act.wait_ge(S["pn_sb"], 1)
                    act.activation(G[:, 3, :], pn[:], ACT.Sin, bias=cols[:, 1:2], scale=float(fqs[3])).then_inc(S["G_sb"], 1)
                    for f in range(3):
                        act.wait_ge(S["z_sb"], 3 + f)
                        act.activation(G[:, f, :], zz[:, f, :], ACT.Sin, bias=cols[:, 1:2], scale=float(fqs[f])).then_inc(S["G_sb"], 1)
                    for t in range(2):
                        act.wait_ge(S["rope_ps"], t + 1)
                        act.activation(cw[:, t, :], ps[:, 5 + t, :], ACT.Copy).then_inc(S["cw_sb"], 1)
                    act.wait_ge(S["mT_ps"], 1)
                    act.activation(mT[:], ps[0:32, 6, :].bitcast(BF16)[:, 0:SEQ], ACT.Copy).then_inc(S["mT_sb"], 1)
                    unit = PAIRS * TILES
                    for p in range(PAIRS + 1):
                        if p < PAIRS:
                            if p >= 2:
                                act.wait_ge(S["pv_ps"], p - 1)
                            for j in range(TILES):
                                t = TILES * p + j
                                act.wait_ge(S["sT_ps"], t + 1)
                                lo = RING[(unit + t) % 3][0]
                                act.activation(E[p % 2][:, :, E_OFF[j]:E_OFF[j] + E_COLS[j]], ps[:, lo:lo + 2, 0:E_COLS[j]],
                                               ACT.Exp, scale=SCALE_A).then_inc(S["E_sb"], 1)
                        if p >= 1:
                            c = p - 1
                            act.wait_ge(S["pv_ps"], c + 1)
                            if c >= 2:
                                act.wait_ge(S["tr_ps"], c - 1)
                            act.activation(Ot[c % 2][:], ps[:, 6, :], ACT.Copy).then_inc(S["Ot_sb"], 1)
                    act.wait_ge(S["aT_ps"], 1)
                    act.activation(aT[:], ps[:, 0, :], ACT.Copy).then_inc(S["aT_sb"], 1)
                    act.wait_ge(S["var_sb"], 1 + 2 * TILES)
                    act.activation(lnv[:], mv[:, :, 1], ACT.Ln, bias=cols[:, 2:3]).then_inc(S["act_order"], 1)
                    act.wait_ge(S["act_order"], 1)
                    act.activation(rstd[:], lnv[:], ACT.Exp, scale=-0.5).then_inc(S["rstd_sb"], 1)
                    act.wait_ge(S["x1T_ps"], 1)
                    act.activation(x1T[:], ps[:, 2, :], ACT.Copy).then_inc(S["x1T_sb"], 1)

                @block.gpsimd
                def _(pool):
                    pool.wait_ge(S["prob_sb"], 1)
                    pool.tensor_scalar(probe[:], prob[:, :, 0, :], 1e-8, None, ALU.add).then_inc(S["pool_order"], 1)
                    pool.wait_ge(S["pool_order"], 1)
                    pool.wait_ge(S["v1_sb"], 2)
                    pool.tensor_tensor(v2[:, :, :, 0:NODES * AUG].rearrange("p i h (n d) -> p (i h) n d", n=NODES),
                                       bcast(probe[:].rearrange("p i (h n) -> p (i h) n", n=NODES), AUG),
                                       bcast_mid(v1[:].rearrange("p i h d -> p (i h) d"), 2, NODES), ALU.mult).then_inc(S["v2_sb"], 1)
                    pool.wait_ge(S["parts_sb"], 1)
                    pool.wait_ge(S["G_sb"], FREQS)
                    pool.tensor_tensor(V[:], G[:], bcast_mid(pnext[:], 1, FREQS), ALU.mult).then_inc(S["V_sb"], 1)
                    for n, t in enumerate((tq, tk)):
                        pool.wait_ge(S["turned"], n + 1)
                        pool.tensor_tensor(qk[:, n, :], t[:, 0, :], t[:, 1, :], ALU.add).then_inc(S["qk_sb"], 1)

            nc.all_engine_barrier(sems_to_clear=sem_range(S))


def return_sum(dve, S, Zn, num, rden, att):
    flat = "p i h (n d) -> p (i h) d n"
    dve.tensor_reduce(num[:], Zn[:].rearrange(flat, n=NODES), AX_X, ALU.add).then_inc(S["Z_sb"], 1)
    dve.wait_ge(S["Z_sb"], PAIRS + 1)
    dve.reciprocal(rden[:], num[:, :, HD_A]).then_inc(S["Z_sb"], 1)
    dve.wait_ge(S["Z_sb"], PAIRS + 2)
    dve.tensor_tensor(att[:].rearrange("p i (h d) -> p (i h) d", d=HD_A), num[:, :, 0:HD_A], bcast(rden[:], HD_A),
                      ALU.mult).then_inc(S["att_sb"], 1)


def sem_range(S):
    nums = sorted(s.num for s in S.all.values())
    assert nums == list(range(nums[0], nums[-1] + 1))
    return range(nums[0], nums[-1] + 1)


def local_attention_layers(nc, io, xs, loops=BATCH, depth=DEPTH):
    ctx = ExitStack()
    with ctx:
        def sb(name, shape, dt=F32):
            return ctx.enter_context(nc.sbuf_tensor("b_" + name, shape, dt))

        ident, ident_b, ones = sb("ident", [P, P]), sb("ident_b", [P, P], BF16), sb("ones", [P, 64])
        mean_w = sb("mean_w", [P, P])
        mask, neg_sel = sb("mask", [P, 3, SPAN], BF16), sb("neg_sel", [2 * HEADS_B, HEADS_B, P], BF16)
        xpos, tab = sb("xpos", [P, 2, TILES, 2, HD_B]), sb("tab", [P, 2, TILES, 2, HD_B])
        scales = sb("scales", [P, 2, HD_B])
        cols = sb("cols", [P, 3])
        w_qkv, w_o = sb("w_qkv", [P, 3 * INNER]), sb("w_o", [P, CHUNKS, DIM])
        w1, w2 = sb("w1", [P, 2 * HID]), sb("w2", [P, 3, DIM])
        vec = sb("vec", [P, 3])
        b1 = sb("b1", [P, 2, 3])
        xT, hT = sb("xT", [P, SEQ]), sb("hT", [P, SEQ])
        v = sb("v", [P, TILES, INNER])
        sq = [sb(f"sq{i}", [P, 2 * INNER]) for i in range(2)]
        raw = [sb(f"raw{i}", [P, 2 * INNER]) for i in range(2)]
        Um = [sb(f"Um{i}", [P, 2 * INNER]) for i in range(2)]
        Vm = [sb(f"Vm{i}", [P, 2 * INNER]) for i in range(2)]
        W = sb("W", [P, TILES, 2 * INNER])
        ss, nrm, rn = (sb(n, [P, TILES, 2 * HEADS_B]) for n in ("ss", "nrm", "rn"))
        QT = sb("QT", [P, CHUNKS, PAD])
        KM = sb("KM", [P, CHUNKS, 2, PAD])
        mN, mS = sb("mN", [P, TILES, HEADS_B]), sb("mS", [P, TILES, HEADS_B, 2], BF16)
        mT = sb("mT", [2 * HEADS_B, PAD], BF16)
        E = [sb(f"E{i}", [P, 2, TILES, SPAN]) for i in range(2)]
        lnd, rd = sb("lnd", [P, SEQ]), sb("rd", [P, SEQ])
        oT = sb("oT", [P, CHUNKS, SEQ])
        x1, h2, hc, sq2, lnv, rs, hn, hn2 = (sb(n, [P, SEQ]) for n in ("x1", "h2", "hc", "sq2", "lnv", "rs", "hn", "hn2"))
        gl, u = sb("gl", [P, 3, SEQ]), sb("u", [P, 3, SEQ])
        xr, xo = sb("xr", [P, SEQ]), sb("xo", [P, SEQ])
        ps = ctx.enter_context(nc.psum_tensor("b_ps", [P, 8, SEQ], F32))

        ld, zeroed = ctx.enter_context(nc.semaphore("b_consts_loaded")), ctx.enter_context(nc.semaphore("b_zeroed"))
        wl, tabled = ctx.enter_context(nc.semaphore("b_weights_loaded")), ctx.enter_context(nc.semaphore("b_tables_scaled"))
        S = Sems(nc, ctx, """x_loaded qkv_ps raw_sb v_sb sq_sb ss_sb U_sb V_sb nrm_sb rn_sb W_sb Wn_sb qT_ps kT_ps QT_sb KM_sb
            s_ps max_sb mS_sb mT_ps mT_sb sT_ps E_sb num_ps lnd_sb rd_sb oT_sb wo_ps x1_sb h2_sb mean_ps hc_sb sq2_sb
            var_ps lnv_sb rs_sb hn_sb g_ps a_ps gl_sb u_sb w2_ps xr_sb xo_sb stored""", "b")

        with nc.Block() as block:
            @block.sync
            def _(sp):
                sp.dma_start(ident[:], io["ident"]).then_inc(ld, 16)
                sp.dma_start(ident_b[:], io["ident_b"]).then_inc(ld, 16)
                sp.dma_start(mask[:], io["mask_b"]).then_inc(ld, 16)
                sp.dma_start(neg_sel[:], io["neg_sel"]).then_inc(ld, 16)
                sp.dma_start(xpos[:].rearrange("p a i t d -> p (a i t d)"), io["xpos"]).then_inc(ld, 16)
                sp.dma_start(cols[:], io["cols"]).then_inc(ld, 16)
                sp.wait_ge(ld, 96)

            @block.gpsimd
            def _(pool):
                nc.gpsimd.memset(KM[:], 0.0).then_inc(zeroed, 1)
                nc.gpsimd.memset(QT[:], 0.0).then_inc(zeroed, 1)
                nc.gpsimd.memset(mT[:], 0.0).then_inc(zeroed, 1)
                nc.gpsimd.memset(hT[:], 0.0).then_inc(zeroed, 1)
                nc.gpsimd.memset(h2[:], 0.0).then_inc(zeroed, 1)
                nc.gpsimd.memset(ones[:], 1.0).then_inc(zeroed, 1)
                nc.gpsimd.memset(mean_w[:], 1.0 / DIM).then_inc(zeroed, 1)

        RING = [(2, 3), (4, 5), (6, 7)]
        QKV = [(0, 2), (3, 5)]

        with nc.Fori(0, depth) as l:
            with nc.Block() as block:
                @block.sync
                def _(sp):
                    sp.dma_start(w_qkv[:], io["L0_ffn_wqkv"][l]).then_inc(wl, 16)
                    sp.dma_start(w_o[:], io["L0_ffn_wo"][l].rearrange("(c p) m -> p c m", p=P)).then_inc(wl, 16)
                    sp.dma_start(w1[:], io["L0_ffn_w1"][l]).then_inc(wl, 16)
                    for c, (o, n) in enumerate(HID_PARTS):
                        sp.dma_start(w2[0:n, c, :], io["L0_ffn_w2"][l][o:o + n, :]).then_inc(wl, 16)
                        for g in range(2):
                            sp.dma_start(b1[0:n, g, c:c + 1], io["L0_ffn_b1"][l][g * HID + o:g * HID + o + n].unsqueeze(1)).then_inc(wl, 16)
                    for n, name in enumerate(("ln_g", "ln_b", "b2")):
                        sp.dma_start(vec[:, n:n + 1], io["L0_ffn_" + name][l].unsqueeze(1)).then_inc(wl, 16)
                    for n, name in enumerate(("q_scale", "k_scale")):
                        sp.dma_start(scales[:, n, :], io["L0_ffn_" + name][l].partition_broadcast(P)).then_inc(wl, 16)
                    sp.wait_ge(wl, 16 * 17)

                @block.vector
                def _(dve):
                    dve.wait_ge(wl, 16 * 17)
                    for i in range(TILES):
                        dve.tensor_tensor(tab[:, 0, i, :, :], xpos[:, 0, i, :, :], scales[:], ALU.mult).then_inc(tabled, 1)
                        for half in range(2):
                            a, o = half * HD_B // 2, (1 - half) * HD_B // 2
                            dve.tensor_tensor(tab[:, 1, i, :, a:a + HD_B // 2], xpos[:, 1, i, :, a:a + HD_B // 2],
                                              scales[:, :, o:o + HD_B // 2], ALU.mult).then_inc(tabled, 1)

            with nc.Fori(0, loops) as b:
                with nc.Block() as block:
                    @block.sync
                    def _(sp):
                        sp.dma_start(xT[:], xs[l, b]).then_inc(S["x_loaded"], 16)
                        sp.dma_start(hT[0:64, :], xs[l, b][0:64, :]).then_inc(S["x_loaded"], 16)
                        sp.dma_start(hT[64:P, 1:SEQ], xs[l, b][64:P, 0:SEQ - 1]).then_inc(S["x_loaded"], 16)
                        sp.wait_ge(S["xo_sb"], 1)
                        sp.dma_start(xs[l + 1, b], xo[:]).then_inc(S["stored"], 16)
                        sp.wait_ge(S["stored"], 16)

                    @block.tensor
                    def _(pe):
                        pe.wait_ge(S["x_loaded"], 48)
                        for i in range(TILES):
                            qkb, vb = QKV[i % 2]
                            if i >= 2:
                                pe.wait_ge(S["raw_sb"], i - 1)
                                pe.wait_ge(S["v_sb"], i - 1)
                            for n, bank in enumerate((qkb, qkb + 1, vb)):
                                last = pe.matmul(ps[:, bank, :], hT[:, P * i:P * i + P], w_qkv[:, INNER * n:INNER * n + INNER], start=True, stop=True)
                            last.then_inc(S["qkv_ps"], 1)
                        for i in range(TILES):
                            qb = 6 if i % 2 == 0 else 0
                            pe.wait_ge(S["Wn_sb"], i + 1)
                            if i == 1:
                                pe.wait_ge(S["raw_sb"], 3)
                            if i >= 2:
                                pe.wait_ge(S["QT_sb"], i - 1)
                                pe.wait_ge(S["KM_sb"], 2 * (i - 1))
                            for c in range(CHUNKS):
                                last = pe.transpose(ps[:, qb, P * c:P * c + P], W[:, i, P * c:P * c + P], ident[:])
                            last.then_inc(S["qT_ps"], 1)
                            for c in range(CHUNKS):
                                last = pe.transpose(ps[:, qb + 1, P * c:P * c + P], W[:, i, INNER + P * c:INNER + P * c + P], ident[:])
                            last.then_inc(S["kT_ps"], 1)
                        pe.wait_ge(S["QT_sb"], TILES)
                        pe.wait_ge(S["KM_sb"], 2 * TILES)
                        pe.wait_ge(S["raw_sb"], TILES)
                        pe.wait_ge(S["v_sb"], TILES)
                        unit = 0
                        for c in range(CHUNKS):
                            for half in range(2):
                                if unit >= 3:
                                    pe.wait_ge(S["max_sb"], unit - 2)
                                for e in range(2):
                                    for n in range(2):
                                        i = 2 * half + n
                                        o = ps[:, RING[unit % 3][e], SPAN * n:SPAN * n + SPAN]
                                        pe.matmul(o, QT[:, c, P * i:P * i + P], KM[:, c, e, P * i:P * i + SPAN], start=True, stop=False)
                                        last = pe.matmul(o, ident_b[:], mask[:, min(i, 1), :], start=False, stop=True)
                                last.then_inc(S["s_ps"], 1)
                                unit += 1
                        pe.wait_ge(S["mS_sb"], 2)
                        for i in range(TILES):
                            last = pe.transpose(ps[0:2 * HEADS_B, 0, :].bitcast(BF16)[:, P * i:P * i + P],
                                                mS[:, i, :, :].rearrange("p h l -> p (h l)"), ident_b[:])
                        last.then_inc(S["mT_ps"], 1)
                        pe.wait_ge(S["mT_sb"], 1)
                        for c in range(CHUNKS + 1):
                            if c < CHUNKS:
                                for half in range(2):
                                    t = 2 * c + half
                                    if t < 3:
                                        pe.wait_ge(S["max_sb"], unit + t - 2)
                                    else:
                                        pe.wait_ge(S["E_sb"], t - 2)
                                    for e in range(2):
                                        for n in range(2):
                                            j = 2 * half + n
                                            o = ps[:, RING[(unit + t) % 3][e], SPAN * n:SPAN * n + SPAN]
                                            pe.matmul(o, KM[:, c, e, WINDOW + P * j:WINDOW + P * j + P], QT[:, c, P * j:P * j + SPAN],
                                                      start=True, stop=False)
                                            pe.matmul(o, neg_sel[:, 2 * c + e, :], mT[:, P * j:P * j + SPAN], start=False, stop=False)
                                            last = pe.matmul(o, ident_b[:], mask[:, 2, :], start=False, stop=True)
                                    last.then_inc(S["sT_ps"], 1)
                            if c >= 1:
                                d = c - 1
                                if d >= 1:
                                    pe.wait_ge(S["oT_sb"], d)
                                for j in range(TILES):
                                    pe.wait_ge(S["E_sb"], 2 * d + j // 2 + 1)
                                    n = min(SPAN, SEQ - P * j)
                                    for e in range(2):
                                        h = 2 * d + e
                                        rows = slice(64 * e, 64 * e + 64)
                                        pe.matmul(ps[rows, 0, P * j:P * j + n], v[:, j, HD_B * h:HD_B * h + HD_B], E[d % 2][:, e, j, 0:n],
                                                  start=j == 0, stop=j == TILES - 1, skip_group_check=True)
                                        last = pe.matmul(ps[rows, 1, P * j:P * j + n], ones[:], E[d % 2][:, e, j, 0:n],
                                                         start=j == 0, stop=j == TILES - 1, skip_group_check=True)
                                last.then_inc(S["num_ps"], 1)
                        pe.wait_ge(S["oT_sb"], CHUNKS)
                        for c in range(CHUNKS):
                            last = pe.matmul(ps[:, 0, :], w_o[:, c, :], oT[:, c, :], start=c == 0, stop=c == CHUNKS - 1)
                        last.then_inc(S["wo_ps"], 1)
                        pe.wait_ge(S["h2_sb"], 2)
                        pe.matmul(ps[:, 1, :], mean_w[:], h2[:], start=True, stop=True).then_inc(S["mean_ps"], 1)
                        pe.wait_ge(S["sq2_sb"], 1)
                        pe.matmul(ps[:, 2, :], mean_w[:], sq2[:], start=True, stop=True).then_inc(S["var_ps"], 1)
                        pe.wait_ge(S["hn_sb"], 2)
                        for c, (o, n) in enumerate(HID_PARTS):
                            pe.matmul(ps[0:n, 3 + c, :], w1[:, HID + o:HID + o + n], hn2[:], start=True, stop=True).then_inc(S["g_ps"], 1)
                        for c, (o, n) in enumerate(HID_PARTS):
                            bank = (6, 7, 0)[c]
                            pe.matmul(ps[0:n, bank, :], w1[:, o:o + n], hn2[:], start=True, stop=True).then_inc(S["a_ps"], 1)
                        for c, (o, n) in enumerate(HID_PARTS):
                            pe.wait_ge(S["u_sb"], c + 1)
                            last = pe.matmul(ps[:, 1, :], w2[0:n, c, :], u[0:n, c, :], start=c == 0, stop=c == 2)
                        last.then_inc(S["w2_ps"], 1)

                    @block.vector
                    def _(dve):
                        for i in range(TILES):
                            src = raw[i % 2][:].rearrange("p (t h d) -> p t h d", t=2, d=HD_B)
                            dve.wait_ge(S["raw_sb"], i + 1)
                            if i >= 2:
                                dve.wait_ge(S["W_sb"], i - 1)
                            heads = "p (t h d) -> p t h d"
                            dve.tensor_tensor(Um[i % 2][:].rearrange(heads, t=2, d=HD_B), src, bcast_mid(tab[:, 0, i, :, :], 2, HEADS_B),
                                              ALU.mult).then_inc(S["U_sb"], 1)
                            for half in range(2):
                                a, o = half * HD_B // 2, (1 - half) * HD_B // 2
                                dve.tensor_tensor(Vm[i % 2][:].rearrange(heads, t=2, d=HD_B)[:, :, :, a:a + HD_B // 2],
                                                  src[:, :, :, o:o + HD_B // 2],
                                                  bcast_mid(tab[:, 1, i, :, a:a + HD_B // 2], 2, HEADS_B), ALU.mult).then_inc(S["V_sb"], 1)
                            dve.wait_ge(S["sq_sb"], i + 1)
                            dve.tensor_reduce(ss[:, i, :], sq[i % 2][:].rearrange("p (h d) -> p h d", d=HD_B), AX_X, ALU.add).then_inc(S["ss_sb"], 1)
                        dve.wait_ge(S["nrm_sb"], 1)
                        dve.tensor_scalar(nrm[:], nrm[:], NORM_MIN, None, ALU.max).then_inc(S["rn_sb"], 1)
                        dve.wait_ge(S["rn_sb"], 1)
                        dve.reciprocal(rn[:], nrm[:]).then_inc(S["rn_sb"], 1)
                        dve.wait_ge(S["rn_sb"], 2)
                        for i in range(TILES):
                            dve.wait_ge(S["W_sb"], i + 1)
                            w = W[:, i, :].rearrange("p (h d) -> p h d", d=HD_B)
                            dve.tensor_tensor(w, w, bcast(rn[:, i, :], HD_B), ALU.mult).then_inc(S["Wn_sb"], 1)
                        for i in range(TILES):
                            qb = 6 if i % 2 == 0 else 0
                            dve.wait_ge(S["kT_ps"], i + 1)
                            src = ps[:, qb + 1, :].rearrange("p (c n) -> p c n", c=CHUNKS)
                            for e in range(2):
                                rows = slice(64 * e, 64 * e + 64)
                                dve.tensor_copy(KM[rows, :, e, WINDOW + P * i:WINDOW + P * i + P], src[rows]).then_inc(S["KM_sb"], 1)
                        for unit in range(2 * CHUNKS):
                            c, half = unit // 2, unit % 2
                            dve.wait_ge(S["s_ps"], unit + 1)
                            lo = RING[unit % 3][0]
                            src = ps[:, lo:lo + 2, 0:2 * SPAN].rearrange("p e (n s) -> p n e s", n=2)
                            dve.tensor_reduce(mN[:, 2 * half:2 * half + 2, 2 * c:2 * c + 2], src, AX_X, ALU.max).then_inc(S["max_sb"], 1)
                        dve.wait_ge(S["max_sb"], 2 * CHUNKS)
                        mh, ml = mS[:, :, :, 0], mS[:, :, :, 1]
                        dve.tensor_copy(mh, mN[:]).then_inc(S["mS_sb"], 1)
                        dve.wait_ge(S["mS_sb"], 1)
                        dve.tensor_tensor(ml, mN[:], mh, ALU.subtract).then_inc(S["mS_sb"], 1)
                        for c in range(CHUNKS):
                            dve.wait_ge(S["num_ps"], c + 1)
                            dve.wait_ge(S["rd_sb"], c + 1)
                            dve.tensor_tensor(oT[:, c, :], ps[:, 0, :], rd[:], ALU.mult).then_inc(S["oT_sb"], 1)
                        dve.wait_ge(S["wo_ps"], 1)
                        dve.tensor_tensor(x1[:], ps[:, 0, :], xT[:], ALU.add).then_inc(S["x1_sb"], 1)
                        dve.wait_ge(S["x1_sb"], 1)
                        dve.tensor_copy(h2[0:64, :], x1[0:64, :]).then_inc(S["h2_sb"], 1)
                        dve.tensor_copy(h2[64:P, 1:SEQ], x1[64:P, 0:SEQ - 1]).then_inc(S["h2_sb"], 1)
                        dve.wait_ge(S["h2_sb"], 2)
                        dve.wait_ge(S["mean_ps"], 1)
                        dve.tensor_tensor(hc[:], h2[:], ps[:, 1, :], ALU.subtract).then_inc(S["hc_sb"], 1)
                        dve.wait_ge(S["hc_sb"], 1)
                        dve.wait_ge(S["rs_sb"], 1)
                        dve.tensor_tensor(hn[:], hc[:], rs[:], ALU.mult).then_inc(S["hn_sb"], 1)
                        dve.wait_ge(S["hn_sb"], 1)
                        dve.tensor_scalar(hn2[:], hn[:], vec[:, 0:1], vec[:, 1:2], ALU.mult, ALU.add).then_inc(S["hn_sb"], 1)
                        for c, (o, n) in enumerate(HID_PARTS):
                            bank = (6, 7, 0)[c]
                            dve.wait_ge(S["a_ps"], c + 1)
                            dve.wait_ge(S["gl_sb"], c + 1)
                            dve.scalar_tensor_tensor(u[0:n, c, :], ps[0:n, bank, :], b1[0:n, 0, c:c + 1], gl[0:n, c, :],
                                                     ALU.add, ALU.mult).then_inc(S["u_sb"], 1)
                        dve.wait_ge(S["w2_ps"], 1)
                        dve.scalar_tensor_tensor(xo[:], ps[:, 1, :], vec[:, 2:3], x1[:], ALU.add, ALU.add).then_inc(S["xo_sb"], 1)

                    @block.scalar
                    def _(act):
                        for i in range(TILES):
                            qkb, vb = QKV[i % 2]
                            act.wait_ge(S["qkv_ps"], i + 1)
                            if i >= 2:
                                act.wait_ge(S["ss_sb"], i - 1)
                                act.wait_ge(S["U_sb"], i - 1)
                                act.wait_ge(S["V_sb"], 2 * (i - 1))
                            act.activation(raw[i % 2][:].rearrange("p (t n) -> p t n", t=2), ps[:, qkb:qkb + 2, :], ACT.Copy).then_inc(S["raw_sb"], 1)
                            act.activation(v[:, i, :], ps[:, vb, :], ACT.Copy).then_inc(S["v_sb"], 1)
                            act.wait_ge(S["raw_sb"], i + 1)
                            act.activation(sq[i % 2][:], raw[i % 2][:], ACT.Square).then_inc(S["sq_sb"], 1)
                        act.wait_ge(S["ss_sb"], TILES)
                        act.activation(nrm[:], ss[:], ACT.Sqrt).then_inc(S["nrm_sb"], 1)
                        for i in range(TILES):
                            qb = 6 if i % 2 == 0 else 0
                            act.wait_ge(S["qT_ps"], i + 1)
                            act.activation(QT[:, :, P * i:P * i + P], ps[:, qb, :].rearrange("p (c n) -> p c n", c=CHUNKS), ACT.Copy).then_inc(S["QT_sb"], 1)
                        act.wait_ge(S["mT_ps"], 1)
                        act.activation(mT[:, 0:SEQ], ps[0:2 * HEADS_B, 0, :].bitcast(BF16)[:, 0:SEQ], ACT.Copy).then_inc(S["mT_sb"], 1)
                        for c in range(CHUNKS + 1):
                            if c < CHUNKS:
                                if c >= 2:
                                    act.wait_ge(S["num_ps"], c - 1)
                                for half in range(2):
                                    t = 2 * c + half
                                    act.wait_ge(S["sT_ps"], t + 1)
                                    lo = RING[(2 * CHUNKS + t) % 3][0]
                                    act.activation(E[c % 2][:, :, 2 * half:2 * half + 2, :],
                                                   ps[:, lo:lo + 2, 0:2 * SPAN].rearrange("p e (n s) -> p e n s", n=2),
                                                   ACT.Exp, scale=QK_SCALE).then_inc(S["E_sb"], 1)
                            if c >= 1:
                                d = c - 1
                                act.wait_ge(S["num_ps"], d + 1)
                                act.activation(lnd[:], ps[:, 1, :], ACT.Ln).then_inc(S["lnd_sb"], 1)
                                act.wait_ge(S["lnd_sb"], d + 1)
                                if d >= 1:
                                    act.wait_ge(S["oT_sb"], d)
                                act.activation(rd[:], lnd[:], ACT.Exp, scale=-1.0).then_inc(S["rd_sb"], 1)
                        act.wait_ge(S["hc_sb"], 1)
                        act.activation(sq2[:], hc[:], ACT.Square).then_inc(S["sq2_sb"], 1)
                        act.wait_ge(S["var_ps"], 1)
                        act.activation(lnv[:], ps[:, 2, :], ACT.Ln, bias=cols[:, 2:3]).then_inc(S["lnv_sb"], 1)
                        act.wait_ge(S["lnv_sb"], 1)
                        act.activation(rs[:], lnv[:], ACT.Exp, scale=-0.5).then_inc(S["rs_sb"], 1)
                        for c, (o, n) in enumerate(HID_PARTS):
                            act.wait_ge(S["g_ps"], c + 1)
                            act.activation(gl[0:n, c, :], ps[0:n, 3 + c, :], ACT.Gelu, bias=b1[0:n, 1, c:c + 1]).then_inc(S["gl_sb"], 1)

                    @block.gpsimd
                    def _(pool):
                        for i in range(TILES):
                            pool.wait_ge(S["U_sb"], i + 1)
                            pool.wait_ge(S["V_sb"], 2 * (i + 1))
                            pool.tensor_tensor(W[:, i, :], Um[i % 2][:], Vm[i % 2][:], ALU.add).then_inc(S["W_sb"], 1)

                nc.all_engine_barrier(sems_to_clear=sem_range(S))
            nc.all_engine_barrier(sems_to_clear=range(wl.num, tabled.num + 1))


def final_layernorm(nc, io, xs, out, loops=BATCH):
    with ExitStack() as ctx:
        def sb(name, shape, dt=F32):
            return ctx.enter_context(nc.sbuf_tensor("c_" + name, shape, dt))

        ident, cols = sb("ident", [P, P]), sb("cols", [P, 3])
        xa, xb = ([sb(f"{n}{i}", [P, SEQ]) for i in range(2)] for n in ("xa", "xb"))
        xsum = [sb(f"xsum{i}", [P, SEQ]) for i in range(2)]
        st, mv = sb("st", [P, 2, TILES, 6]), sb("mv", [P, 2, TILES, 2])
        nrm, rstd = sb("nrm", [P, 2, TILES]), sb("rstd", [P, 2, TILES])
        y = [sb(f"y{i}", [P, TILES, DIM]) for i in range(2)]
        ps = ctx.enter_context(nc.psum_tensor("c_ps", [P, 2, SEQ], F32))
        ld = ctx.enter_context(nc.semaphore("c_consts_loaded"))
        S = Sems(nc, ctx, "a_loaded b_loaded sum_sb y_ps st_sb mv_sb nrm_sb rstd_sb y_sb stored", "c")

        with nc.Block() as block:
            @block.sync
            def _(sp):
                sp.dma_start(ident[:], io["ident"]).then_inc(ld, 16)
                sp.dma_start(cols[:], io["cols"]).then_inc(ld, 16)
                sp.wait_ge(ld, 32)

        xs2 = xs.rearrange("l (b u) p n -> l b u p n", u=2)
        out2 = out.rearrange("(b u) (i p) e -> b u p i e", u=2, p=P)
        with nc.Fori(0, loops // 2) as b:
            with nc.Block() as block:
                @block.sync
                def _(sp):
                    for u in range(2):
                        sp.dma_start(xa[u][:], xs2[0, b, u]).then_inc(S["a_loaded"], 16)
                        sp.dma_start(xb[u][:], xs2[DEPTH, b, u]).then_inc(S["b_loaded"], 16)
                    for u in range(2):
                        sp.wait_ge(S["y_sb"], TILES * (u + 1))
                        sp.dma_start(out2[b, u], y[u][:]).then_inc(S["stored"], 16)
                    sp.wait_ge(S["stored"], 32)

                @block.tensor
                def _(pe):
                    for u in range(2):
                        pe.wait_ge(S["sum_sb"], u + 1)
                        for i in range(TILES):
                            last = pe.transpose(ps[:, u, P * i:P * i + P], xsum[u][:, P * i:P * i + P], ident[:])
                        last.then_inc(S["y_ps"], 1)

                @block.vector
                def _(dve):
                    dve.wait_ge(S["a_loaded"], 32)
                    dve.wait_ge(S["b_loaded"], 32)
                    for u in range(2):
                        dve.tensor_tensor(xsum[u][:], xa[u][:], xb[u][:], ALU.add).then_inc(S["sum_sb"], 1)
                    for u in range(2):
                        dve.wait_ge(S["y_ps"], u + 1)
                        for i in range(TILES):
                            dve.bn_stats(st[:, u, i, :], ps[:, u, P * i:P * i + P]).then_inc(S["st_sb"], 1)
                    dve.wait_ge(S["st_sb"], 2 * TILES)
                    for u in range(2):
                        for i in range(TILES):
                            dve.bn_aggr(mv[:, u, i, :], st[:, u, i, :]).then_inc(S["mv_sb"], 1)
                    dve.wait_ge(S["mv_sb"], 2 * TILES)
                    dve.wait_ge(S["nrm_sb"], 1)
                    dve.reciprocal(rstd[:], nrm[:]).then_inc(S["rstd_sb"], 1)
                    dve.wait_ge(S["rstd_sb"], 1)
                    for u in range(2):
                        for i in range(TILES):
                            dve.tensor_scalar(y[u][:, i, :], ps[:, u, P * i:P * i + P], mv[:, u, i, 0:1], rstd[:, u, i:i + 1],
                                              ALU.subtract, ALU.mult).then_inc(S["y_sb"], 1)

                @block.scalar
                def _(act):
                    act.wait_ge(S["mv_sb"], 2 * TILES)
                    act.activation(nrm[:], mv[:, :, :, 1], ACT.Sqrt, bias=cols[:, 2:3]).then_inc(S["nrm_sb"], 1)

            nc.all_engine_barrier(sems_to_clear=sem_range(S))


DIRECT = ["L0_attn_x"] + ["L0_ffn_" + n for n in ("wqkv", "q_scale", "k_scale", "wo", "ln_g", "ln_b", "w1", "b1", "w2", "b2")]


def lay_out(inputs):
    arrays = {n: np.ascontiguousarray(inputs[n]) for n in DIRECT}
    wq, wk, wv, wr, wo = (np.asarray(inputs["L0_attn_W" + n]) for n in "qkvro")
    other_half = np.arange(DIM).reshape(HEADS_A, 2, FREQS)[:, ::-1].reshape(DIM)
    arrays["w_vr"] = np.concatenate([wv, wr], 1)
    arrays["w_qk"] = np.stack([wq, wq[:, other_half], wk, wk[:, other_half]])
    arrays["w_o"] = np.ascontiguousarray(wo)
    arrays.update(constants())
    return arrays


def build(nc, io, out):
    xs = nc.dram_tensor("xs", [DEPTH + 1, BATCH, DIM, SEQ], F32).ap()
    scratch = nc.dram_tensor("split_qk", [3, 2, HEADS_A, HD_A, SEQ], BF16).ap()
    soft_rope_attention(nc, io, xs, scratch)
    local_attention_layers(nc, io, xs)
    final_layernorm(nc, io, xs, out)


def kernel(**inputs):
    import concourse.bacc as bacc
    from concourse.bass_utils import run_bass_kernel_spmd

    nc = bacc.Bacc("TRN2", target_bir_lowering=False, num_devices=1)
    arrays = lay_out(inputs)
    io = {n: nc.dram_tensor(f"in_{n}_dram", a.shape, mybir.dt.from_np(a.dtype), kind="ExternalInput").ap() for n, a in arrays.items()}
    out = nc.dram_tensor("out_0_dram", (BATCH, SEQ, DIM), F32, kind="ExternalOutput").ap()
    build(nc, io, out)
    r = run_bass_kernel_spmd(nc, [{f"in_{n}_dram": a for n, a in arrays.items()}], core_ids=[0])
    return r.results[0]["out_0_dram"]
```

```python
from contextlib import ExitStack

import numpy as np

import concourse.bass as bass
from concourse import mybir

ALU = mybir.AluOpType
ACT = mybir.ActivationFunctionType
AX_X = mybir.AxisListType.X
F32 = mybir.dt.float32
BF16 = mybir.dt.bfloat16

P = 128
BATCH, SEQ, DIM = 8, 512, 128
TILES = SEQ // P

HEADS_A, HD_A, NODES = 16, 8, 4
FREQS = HD_A // 2
HN = HEADS_A * NODES
PAIRS = HEADS_A // 2
AUG = HD_A + 1
SCALE_A = HD_A ** -0.5
MAX_POS = 1023.0
ROUND = 12582912.0
SPLIT_PRODUCTS = ((0, 0), (0, 1), (1, 0), (0, 2), (2, 0), (1, 1))
SPLIT_ROWS = len(SPLIT_PRODUCTS) * HD_A
E_COLS = [SEQ - P * j for j in range(TILES)]
E_OFF = [sum(E_COLS[:j]) for j in range(TILES)]

DEPTH, HEADS_B, HD_B, WINDOW = 2, 8, 64, 64
INNER = HEADS_B * HD_B
CHUNKS = INNER // P
HID = int(DIM * 4 * 2 / 3)
HID_PARTS = [(0, P), (P, P), (2 * P, HID - 2 * P)]
QK_SCALE = 8.0
SPAN = P + WINDOW
PAD = SEQ + WINDOW
LN_EPS = 1e-5
NORM_MIN = 1e-12
MASKED = -1e30
LAYER_LOADS = 6 + 3 * len(HID_PARTS) + 3
TWO = range(2)


def rope_freqs():
    return 1.0 / 10000.0 ** (np.arange(0, HD_A, 2) / HD_A)


def constants():

    bf = mybir.dt.np(BF16)
    c = {}
    c["ident"] = np.eye(P, dtype=np.float32)
    c["ident_b"] = np.eye(P).astype(bf)
    s, t = np.arange(P)[:, None], np.arange(SEQ)[None, :]
    c["before"] = (s < t).astype(np.float32)
    i, j = np.arange(P)[:, None], np.arange(P)[None, :]
    c["mask_a"] = np.stack([np.where(j > i, MASKED, 0), np.where(j < i, MASKED, 0)], 1).astype(bf)
    sums = np.zeros((P, 2, FREQS, 2 * HEADS_A))
    spread = np.zeros((P, 2, P))
    for f, fr in enumerate(rope_freqs()):
        co, si = np.cos(fr), np.sin(fr)
        for h in range(HEADS_A):
            rc, rs = slice(h * NODES, h * NODES + NODES), slice(HN + h * NODES, HN + h * NODES + NODES)
            sums[rc, 0, f, h], sums[rs, 0, f, HEADS_A + h] = 1, 1
            sums[rc, 1, f, h], sums[rs, 1, f, h] = co, -si
            sums[rc, 1, f, HEADS_A + h], sums[rs, 1, f, HEADS_A + h] = si, co
            for d in (f, f + FREQS):
                spread[2 * HEADS_A * f + h, 0, h * HD_A + d] = 1
                spread[2 * HEADS_A * f + HEADS_A + h, 1, h * HD_A + d] = -1 if d < FREQS else 1
    c["node_sums"] = sums.reshape(P, -1).astype(np.float32)
    c["spread"] = spread.reshape(P, -1).astype(np.float32)
    half = (np.arange(P) < HN).astype(np.float64)
    c["cols"] = np.stack([0.25 * half, np.pi / 2 * half, np.full(P, LN_EPS)], 1).astype(np.float32)
    shift = np.zeros((4, PAIRS, 2, SEQ))
    shift[0:2, :, 0], shift[2:4, :, 1] = -1, -1
    c["shift_rows"] = shift.astype(bf)
    jj = np.arange(SPAN)[None, :]
    band = np.where((jj - WINDOW <= i) & (jj >= i), 0, MASKED)
    first = np.where(jj >= WINDOW, band, MASKED)
    ahead = np.where((jj - i >= 0) & (jj - i <= WINDOW), 0, MASKED)
    c["mask_b"] = np.stack([first, band, ahead], 1).astype(bf)
    neg = np.zeros((P, HEADS_B, P))
    for h in range(HEADS_B):
        neg[2 * h:2 * h + 2, h] = -1
    c["neg_sel"] = neg.astype(bf)
    half_idx = np.arange(0, HD_B, 2, dtype=np.float64)
    inv = (1.0 / 10000.0 ** (half_idx / HD_B)).astype(np.float32)
    pos = np.arange(SEQ, dtype=np.float32)
    fr = (pos[:, None] * inv[None, :]).astype(np.float64)
    base = (half_idx + 0.4 * HD_B) / (1.4 * HD_B)
    sc = base[None, :] ** ((pos.astype(np.float64) - SEQ // 2) / (WINDOW // 2))[:, None]
    two = lambda a: np.concatenate([a, a], 1)
    signed = np.concatenate([-np.sin(fr), np.sin(fr)], 1)
    tab = np.stack([np.stack([two(np.cos(fr) * sc), two(np.cos(fr) / sc)], 1),
                    np.stack([signed * two(sc), signed / two(sc)], 1)], 1)
    c["xpos"] = tab.reshape(TILES, P, 2, 2, HD_B).transpose(1, 2, 0, 3, 4).reshape(P, -1).astype(np.float32)
    return c


def chain(eng, sem):
    count = [0]

    def link(ins):
        count[0] += 1
        ins.then_inc(sem, 1)
        eng.wait_ge(sem, count[0])
    return link


def bcast(ap, n):
    return ap.unsqueeze(len(ap.shape)).broadcast_to(list(ap.shape) + [n])


def bcast_mid(ap, axis, n):
    shape = list(ap.shape)
    return ap.unsqueeze(axis).broadcast_to(shape[:axis] + [n] + shape[axis:])


class Sems:

    def __init__(self, nc, ctx, names, prefix):
        self.all = {n: ctx.enter_context(nc.semaphore(f"{prefix}_{n}")) for n in names.split()}

    def __getitem__(self, n):
        return self.all[n]


PARTS, LAG = 6, 2
STEPS = PAIRS + LAG + 2
MAX_PARTS = ((0, (0, 1)), (1, (0, 1)), (2, (0,)), (2, (1,)), (3, (0,)), (3, (1,)))
T_PARTS = ((0, (0,)), (0, (1,)), (1, (0,)), (1, (1,)), (2, (0, 1)), (3, (0, 1)))
T_DONE = (2, 4, 5, 6)
MAXIMA_AT = 2
WHEN = {"turn x": (0, 1), "values": (0, 3), "node max": (0, 5), "node sums": (1, 1), "positions": (1, 3), "turn probs": (1, 4),
        "whole positions": (2, 3), "turns": (2, 4), "angle 0": (2, 5), "angle 1": (3, 0), "angle 2": (3, 1), "sines": (3, 2),
        "weighted sines": (3, 5), "node cosines": (4, 2), "cosines": (4, 4), "q": (5, 1), "k": (5, 5), "split": (6, 3),
        "attended": (1, 5), "turn attended": (2, 2), "project": (2, 4), "variance": (3, 0),
        "normalise": (3, 3), "turn output": (4, 5)}


def soft_rope_attention(nc, io, xs, scratch, loops=BATCH):
    ctx = ExitStack()
    with ctx:
        def sb(name, shape, dt=F32):
            return ctx.enter_context(nc.sbuf_tensor("a_" + name, shape, dt))

        ident, ident_b = sb("ident", [P, P]), sb("ident_b", [P, P], BF16)
        before, mask = sb("before", [P, SEQ]), sb("mask", [P, 2, P], BF16)
        node_sums, spread = sb("node_sums", [P, 2, FREQS, 2 * HEADS_A]), sb("spread", [P, 2, P])
        cols = sb("cols", [P, 3])
        w_vr, w_qk, w_o = sb("w_vr", [P, DIM + HN]), sb("w_qk", [P, 4, DIM]), sb("w_o", [P, DIM])
        x, xT = sb("x", [P, TILES, DIM]), sb("xT", [P, SEQ])
        lg, ex = sb("lg", [P, TILES, HN]), sb("ex", [P, TILES, HN])
        v1 = sb("v1", [P, TILES, HEADS_A, AUG])
        mx, sm, rsm = (sb(n, [P, TILES, HEADS_A]) for n in ("mx", "sm", "rsm"))
        prob = sb("prob", [P, TILES, 2, HN])
        probe = sb("probe", [P, TILES, HN])
        posc, pn, fr, pT, pnext, phere = (sb(n, [P, SEQ]) for n in ("posc", "pn", "fr", "pT", "pnext", "phere"))
        kk, zz = sb("kk", [P, 3, SEQ]), sb("zz", [P, 3, SEQ])
        G, U, V = (sb(n, [P, FREQS, SEQ]) for n in ("G", "U", "V"))
        cs, cw = sb("cs", [P, SEQ]), sb("cw", [P, 2, SEQ])
        tq, tk = kk[:, 0:2, :], zz[:, 0:2, :]
        qk, rem = sb("qk", [P, 2, SEQ]), sb("rem", [P, 2, SEQ])
        s3 = sb("s3", [P, 3, 2, SEQ], BF16)
        q6, k6 = ([sb(f"{n}{i}", [P, PAIRS, *e, SEQ], BF16) for i in TWO] for n, e in (("q6_", []), ("k6_", [2])))
        v2 = sb("v2", [P, TILES, HEADS_A * NODES * AUG + 64 - NODES * AUG])
        prob_q = sb("prob_q", [P, TILES, HN])
        mN, mS = sb("mN", [P, TILES, HEADS_A]), sb("mS", [P, TILES, HEADS_A, 2], BF16)
        E = [sb(f"E{i}", [P, 2, sum(E_COLS)]) for i in TWO]
        Ot = [sb(f"Ot{i}", [P, SEQ]) for i in TWO]
        Zn = sb("Zn", [P, TILES, HEADS_A, NODES * AUG])
        xr = sb("xr", [P, TILES, DIM])
        num, rden = sb("num", [P, TILES * HEADS_A, AUG]), sb("rden", [P, TILES * HEADS_A])
        att, aT = sb("att", [P, TILES, DIM]), sb("aT", [P, SEQ])
        y, y2, x1T = sb("y", [P, TILES, DIM]), sb("y2", [P, TILES, DIM]), sb("x1T", [P, SEQ])
        st, mv = sb("st", [P, TILES, 6]), sb("mv", [P, TILES, 2])
        lnv, rstd = sb("lnv", [P, TILES]), sb("rstd", [P, TILES])
        ps = ctx.enter_context(nc.psum_tensor("a_ps", [P, 8, SEQ], F32))
        RING_T, RING_M = (0, 1), (2, 3)
        PV, TURN = 4, 5
        F1, F2 = 6, 7

        ld = ctx.enter_context(nc.semaphore("a_consts_loaded"))
        zeroed = [ctx.enter_context(nc.semaphore(f"a_zeroed{i}")) for i in TWO]
        S = Sems(nc, ctx, """x_loaded x_ahead xT_ps xT_sb vr_ps lg_sb v1_sb lg_shifted ex_sb prob_sb pos_ps pT_ps pT_sb
            pn_sb parts_sb z_sb G_sb U_sb V_sb v2_sb qk_ps cs_ps cs_sb rope_ps cw_sb turned qk_sb split_sb split_out packed
            s_ps max_sb mS_sb mT_ps mT_sb sT_ps E_sb pv_ps Ot_sb tr_ps Z_sb prob_q_sb xr_loaded num_sb att_sb aT_ps aT_sb
            o_ps var_sb rstd_sb x1_sb x1T_ps x1T_sb stored dve_order pool_order act_order""", "a")

        with nc.Block() as block:
            @block.sync
            def _(sp):
                sp.dma_start(ident[:], io["ident"]).then_inc(ld, 16)
                sp.dma_start(ident_b[:], io["ident_b"]).then_inc(ld, 16)
                sp.dma_start(before[:], io["before"]).then_inc(ld, 16)
                sp.dma_start(mask[:], io["mask_a"]).then_inc(ld, 16)
                sp.dma_start(node_sums[:].rearrange("p a f m -> p (a f m)"), io["node_sums"]).then_inc(ld, 16)
                sp.dma_start(spread[:].rearrange("p a m -> p (a m)"), io["spread"]).then_inc(ld, 16)
                sp.dma_start(cols[:], io["cols"]).then_inc(ld, 16)
                sp.dma_start(w_vr[:], io["w_vr"]).then_inc(ld, 16)
                sp.dma_start(w_qk[:], io["w_qk"].rearrange("a p m -> p a m")).then_inc(ld, 16)
                sp.dma_start(w_o[:], io["w_o"]).then_inc(ld, 16)
                for i in TWO:
                    sp.wait_ge(zeroed[i], 1)
                    sp.dma_start(k6[i][2 * SPLIT_ROWS:2 * SPLIT_ROWS + 4, :, :, :], io["shift_rows"]).then_inc(ld, 16)
                sp.wait_ge(ld, 16 * 12)

            @block.gpsimd
            def _(pool):
                pool.memset(k6[0][:], 0.0).then_inc(zeroed[0], 1)
                pool.memset(v2[:], 0.0).then_inc(zeroed[0], 1)
                pool.memset(v1[:], 1.0).then_inc(zeroed[0], 1)

            @block.vector
            def _(dve):
                dve.memset(k6[1][:], 0.0).then_inc(zeroed[1], 1)

        M_ROWS = slice(2 * SPLIT_ROWS, 2 * SPLIT_ROWS + 4)

        def max_bank(parts, maxima):
            return RING_M[(parts + maxima) % 2]

        def turn(front, main, tail, now, ahead=None):
            q_now, k_now, q_next, k_next = q6[now], k6[now], q6[1 - now], k6[1 - now]

            def due(step, place, part):
                return part is not None and WHEN[step] == place

            with nc.Block() as block:
                @block.sync
                def _(sp):
                    if front is not None and not main:
                        sp.dma_start(x[:], io["L0_attn_x"][front].rearrange("(i p) e -> p i e", p=P)).then_inc(S["x_loaded"], 16)
                    if tail is not None:
                        sp.dma_start(xr[:], io["L0_attn_x"][tail].rearrange("(i p) e -> p i e", p=P)).then_inc(S["xr_loaded"], 16)
                    if tail is not None:
                        sp.wait_ge(S["x1T_sb"], 1)
                        sp.dma_start(xs[0, tail], x1T[:]).then_inc(S["stored"], 16)
                    if ahead is not None:
                        sp.wait_ge(S["xT_ps"], 1)
                        sp.dma_start(x[:], io["L0_attn_x"][ahead].rearrange("(i p) e -> p i e", p=P)).then_inc(S["x_ahead"], 16)
                    if front is not None:
                        sp.wait_ge(S["split_sb"], 1)
                        sp.dma_start(scratch.rearrange("s t h d n -> (h d) s t n"), s3[:]).then_inc(S["split_out"], 16)
                        sp.wait_ge(S["split_out"], 16)
                        for e in TWO:
                            for n, (qs, ks) in enumerate(SPLIT_PRODUCTS):
                                r = SPLIT_ROWS * e + HD_A * n
                                sp.dma_start(q_next[r:r + HD_A, :, :],
                                             scratch[qs, 0].rearrange("(p e) d n -> e d p n", e=2)[e]).then_inc(S["packed"], 16)
                                sp.dma_start(k_next[r:r + HD_A, :, e, :],
                                             scratch[ks, 1].rearrange("(p e) d n -> e d p n", e=2)[e]).then_inc(S["packed"], 16)
                        sp.wait_ge(S["packed"], 16 * 4 * len(SPLIT_PRODUCTS))
                    if ahead is not None:
                        sp.wait_ge(S["x_ahead"], 16)
                    if tail is not None:
                        sp.wait_ge(S["stored"], 16)

                @block.tensor
                def _(pe):
                    turned_pairs = [0]

                    def transposes(bank, src, done):
                        for i in range(TILES):
                            last = pe.transpose(ps[:, bank, P * i:P * i + P], src(i), ident[:])
                        last.then_inc(S[done], 1)

                    def front_and_tail(place):
                        if due("turn x", place, front):
                            if not main:
                                pe.wait_ge(S["x_loaded"], 16)
                            transposes(F1, lambda i: x[:, i, :], "xT_ps")
                        if due("values", place, front):
                            pe.wait_ge(S["xT_sb"], 1)
                            for bank, half in ((F2, 0), (F1, 1)):
                                for n in TWO:
                                    i, o = 2 * half + n, n * (DIM + HN)
                                    last = pe.matmul(ps[:, bank, o:o + DIM + HN], xT[:, P * i:P * i + P], w_vr[:], start=True, stop=True)
                                last.then_inc(S["vr_ps"], 1)
                        if due("positions", place, front):
                            pe.wait_ge(S["lg_sb"], 1)
                            pe.wait_ge(S["v1_sb"], 1)
                            pe.wait_ge(S["prob_sb"], 2)
                            for i in range(TILES):
                                last = pe.matmul(ps[:, F2, P * i:SEQ], prob[:, i, :, :].rearrange("p r n -> p (r n)"), before[:, 0:SEQ - P * i],
                                                 start=i == 0, stop=i == TILES - 1)
                            last.then_inc(S["pos_ps"], 1)
                        if due("turn probs", place, front):
                            pe.wait_ge(S["lg_sb"], 2)
                            pe.wait_ge(S["v1_sb"], 2)
                            transposes(F1, lambda i: prob[:, i, :, :].rearrange("p r n -> p (r n)"), "pT_ps")
                        if due("node cosines", place, front):
                            pe.wait_ge(S["U_sb"], 1)
                            pe.wait_ge(S["V_sb"], FREQS)
                            pe.wait_ge(S["pT_sb"], 1)
                            for n, src in enumerate((U, V)):
                                for f in range(FREQS):
                                    rows = slice(2 * HEADS_A * f, 2 * HEADS_A * (f + 1))
                                    last = pe.matmul(ps[rows, F1, :], node_sums[:, n, f, :], src[:, f, :], start=n == 0, stop=n == 1)
                            last.then_inc(S["cs_ps"], 1)
                        if due("cosines", place, front):
                            pe.wait_ge(S["cs_sb"], 1)
                            pe.wait_ge(S["pn_sb"], 1)
                            for t in TWO:
                                pe.matmul(ps[:, (F1, F2)[t], :], spread[:, t, :], cs[:], start=True, stop=True).then_inc(S["rope_ps"], 1)
                        for t, step in enumerate(("q", "k")):
                            if due(step, place, front):
                                if t == 0:
                                    pe.wait_ge(S["cw_sb"], 2)
                                else:
                                    pe.wait_ge(S["turned"], 1)
                                for n in TWO:
                                    last = pe.matmul(ps[:, (F1, F2)[n], :], w_qk[:, 2 * t + n, :], xT[:], start=True, stop=True)
                                last.then_inc(S["qk_ps"], 1)
                        if due("turn attended", place, tail):
                            pe.wait_ge(S["att_sb"], 1)
                            transposes(TURN, lambda i: att[:, i, :], "aT_ps")
                        if due("project", place, tail):
                            pe.wait_ge(S["aT_sb"], 1)
                            for i in range(TILES):
                                last = pe.matmul(ps[:, TURN, P * i:P * i + P], aT[:, P * i:P * i + P], w_o[:], start=True, stop=True)
                            last.then_inc(S["o_ps"], 1)
                        if due("turn output", place, tail):
                            if main:
                                pe.wait_ge(S["Z_sb"], 2 * turned_pairs[0])
                            pe.wait_ge(S["x1_sb"], TILES)
                            transposes(TURN, lambda i: y2[:, i, :], "x1T_ps")

                    used, read = [0], {}

                    def next_bank(signal, count):
                        bank = RING_M[used[0] % 2]
                        used[0] += 1
                        if bank in read:
                            pe.wait_ge(S[read[bank][0]], read[bank][1])
                        read[bank] = (signal, count)
                        return bank

                    def max_scores(p, part):
                        i, heads = MAX_PARTS[part]
                        bank, n = next_bank("max_sb", PARTS * p + part + 1), P * i + P
                        for at, e in enumerate(heads):
                            o = ps[:, bank, n * at:n * at + n]
                            pe.matmul(o, q_now[0:2 * SPLIT_ROWS, p, P * i:P * i + P], k_now[0:2 * SPLIT_ROWS, p, e, 0:n], start=True, stop=False)
                            last = pe.matmul(o[:, P * i:n], ident_b[:], mask[:, 0, :], start=False, stop=True)
                        last.then_inc(S["s_ps"], 1)

                    def turn_maxima(p):
                        bank = next_bank("mT_sb", p + 1)
                        pe.wait_ge(S["mS_sb"], 2 * (p + 1))
                        for i in range(TILES):
                            last = pe.transpose(ps[M_ROWS, bank, :].bitcast(BF16)[:, P * i:P * i + P],
                                                mS[:, i, 2 * p:2 * p + 2, :].rearrange("p h l -> p (h l)"), ident_b[:])
                        last.then_inc(S["mT_ps"], 1)

                    def scores(p, part):
                        j, heads = T_PARTS[part]
                        t, n = PARTS * p + part, E_COLS[j]
                        if part == 0:
                            pe.wait_ge(S["mT_sb"], p + 1)
                        if t >= 2:
                            pe.wait_ge(S["E_sb"], t - 1)
                        for at, e in enumerate(heads):
                            o = ps[:, RING_T[t % 2], n * at:n * at + n]
                            pe.matmul(o, k_now[0:2 * SPLIT_ROWS + 4, p, e, P * j:P * j + P], q_now[0:2 * SPLIT_ROWS + 4, p, P * j:SEQ],
                                      start=True, stop=False)
                            last = pe.matmul(o[:, 0:P], ident_b[:], mask[:, 1, :], start=False, stop=True)
                        last.then_inc(S["sT_ps"], 1)

                    def weighted(c, j):
                        if j == 0 and c >= 1:
                            pe.wait_ge(S["Ot_sb"], c)
                        pe.wait_ge(S["E_sb"], PARTS * c + T_DONE[j])
                        for e in TWO:
                            at = (2 * c + e) * NODES * AUG
                            last = pe.matmul(ps[64 * e:64 * e + 64, PV, P * j:SEQ], v2[:, j, at:at + 64],
                                             E[c % 2][:, e, E_OFF[j]:E_OFF[j] + E_COLS[j]], start=j == 0, stop=j == TILES - 1)
                        if j == TILES - 1:
                            last.then_inc(S["pv_ps"], 1)

                    def turn_weighted(c, place):
                        pe.wait_ge(S["Ot_sb"], c + 1)
                        if c >= 1:
                            pe.wait_ge(S["Z_sb"], 2 * c)
                        elif tail is not None:
                            pe.wait_ge(S["var_sb"], 1)
                        if tail is not None and WHEN["turn output"] < place:
                            pe.wait_ge(S["x1T_sb"], 1)
                        transposes(TURN, lambda i: Ot[c % 2][:, P * i:P * i + P], "tr_ps")
                        turned_pairs[0] += 1

                    for r in range(STEPS):
                        for part in range(PARTS):
                            if main and r < PAIRS:
                                max_scores(r, part)
                            if main and part == MAXIMA_AT and 1 <= r <= PAIRS:
                                turn_maxima(r - 1)
                            if main and LAG <= r < PAIRS + LAG:
                                scores(r - LAG, part)
                            if main and part == 1 and r >= LAG + 2:
                                turn_weighted(r - LAG - 2, (r, part))
                            if main and part >= 2 and LAG < r <= PAIRS + LAG:
                                weighted(r - LAG - 1, part - 2)
                            front_and_tail((r, part))

                @block.vector
                def _(dve):
                    link = chain(dve, S["dve_order"])
                    nodes = "p i (h n) -> p (i h) n"
                    flat = "p i h -> p (i h)"
                    fqs = rope_freqs()

                    def front_and_tail(place):
                        if due("node max", place, front):
                            dve.wait_ge(S["lg_sb"], 2)
                            link(dve.tensor_reduce(mx[:].rearrange(flat), lg[:].rearrange(nodes, n=NODES), AX_X, ALU.max))
                            dve.tensor_tensor(lg[:].rearrange(nodes, n=NODES), lg[:].rearrange(nodes, n=NODES),
                                              bcast(mx[:].rearrange(flat), NODES), ALU.subtract).then_inc(S["lg_shifted"], 1)
                        if due("node sums", place, front):
                            dve.wait_ge(S["ex_sb"], 1)
                            link(dve.tensor_reduce(sm[:].rearrange(flat), ex[:].rearrange(nodes, n=NODES), AX_X, ALU.add))
                            link(dve.reciprocal(rsm[:], sm[:]))
                            for r in TWO:
                                dve.tensor_tensor(prob[:, :, r, :].rearrange("p i (h n) -> p i h n", n=NODES),
                                                  ex[:].rearrange("p i (h n) -> p i h n", n=NODES), bcast(rsm[:], NODES),
                                                  ALU.mult).then_inc(S["prob_sb"], 1)
                        if due("whole positions", place, front):
                            dve.wait_ge(S["pos_ps"], 1)
                            link(dve.tensor_scalar(posc[:], ps[:, F2, :], 0.0, MAX_POS, ALU.max, ALU.min))
                            link(dve.tensor_scalar(pn[:], posc[:], -0.5, ROUND, ALU.add, ALU.add))
                            dve.tensor_scalar(pn[:], pn[:], ROUND, None, ALU.subtract).then_inc(S["pn_sb"], 1)
                        if due("turns", place, front):
                            dve.wait_ge(S["pn_sb"], 1)
                            for f in range(3):
                                ins = dve.tensor_scalar(kk[:, f, :], pn[:], float(fqs[f] / (2 * np.pi)), cols[:, 0:1], ALU.mult, ALU.add)
                                if f == 2:
                                    link(ins)
                                else:
                                    ins.then_inc(S["z_sb"], 1)
                            dve.wait_ge(S["z_sb"], 2)
                            link(dve.tensor_scalar(kk[:], kk[:], ROUND, ROUND, ALU.add, ALU.subtract))
                        for f, high in enumerate((6.28125, 62.8125, 628.3125)):
                            if due(f"angle {f}", place, front):
                                link(dve.scalar_tensor_tensor(zz[:, f, :], kk[:, f, :], -high, pn[:], ALU.mult, ALU.add))
                                dve.scalar_tensor_tensor(zz[:, f, :], kk[:, f, :], -float(2 * np.pi / fqs[f] - high), zz[:, f, :],
                                                         ALU.mult, ALU.add).then_inc(S["z_sb"], 1)
                        if due("weighted sines", place, front):
                            dve.wait_ge(S["parts_sb"], 3)
                            dve.wait_ge(S["G_sb"], FREQS)
                            dve.tensor_tensor(U[:], G[:], bcast_mid(phere[:], 1, FREQS), ALU.mult).then_inc(S["U_sb"], 1)
                        if due("q", place, front):
                            dve.wait_ge(S["qk_ps"], 1)
                            dve.wait_ge(S["cw_sb"], 2)
                            dve.tensor_tensor(tq, ps[:, F1:F2 + 1, :], cw[:], ALU.mult).then_inc(S["turned"], 1)
                        if due("k", place, front):
                            dve.wait_ge(S["qk_ps"], 2)
                            dve.wait_ge(S["G_sb"], FREQS)
                            dve.tensor_tensor(tk, ps[:, F1:F2 + 1, :], cw[:], ALU.mult).then_inc(S["turned"], 1)
                        if due("split", place, front):
                            dve.wait_ge(S["qk_sb"], 2)
                            link(dve.tensor_copy(s3[:, 0, :, :], qk[:]))
                            link(dve.tensor_tensor(rem[:], qk[:], s3[:, 0, :, :], ALU.subtract))
                            link(dve.tensor_copy(s3[:, 1, :, :], rem[:]))
                            dve.tensor_tensor(s3[:, 2, :, :], rem[:], s3[:, 1, :, :], ALU.subtract).then_inc(S["split_sb"], 1)
                        if due("attended", place, tail):
                            dve.tensor_reduce(num[:], Zn[:].rearrange("p i h (n d) -> p (i h) d n", n=NODES), AX_X, ALU.add).then_inc(S["num_sb"], 1)
                            dve.wait_ge(S["num_sb"], 1)
                            dve.reciprocal(rden[:], num[:, :, HD_A]).then_inc(S["num_sb"], 1)
                            dve.wait_ge(S["num_sb"], 2)
                            dve.tensor_tensor(att[:].rearrange("p i (h d) -> p (i h) d", d=HD_A), num[:, :, 0:HD_A], bcast(rden[:], HD_A),
                                              ALU.mult).then_inc(S["att_sb"], 1)
                        if due("variance", place, tail):
                            dve.wait_ge(S["o_ps"], 1)
                            dve.wait_ge(S["xr_loaded"], 16)
                            dve.tensor_tensor(y[:], ps[:, TURN, :].rearrange("p (i e) -> p i e", i=TILES), xr[:], ALU.add).then_inc(S["var_sb"], 1)
                            dve.wait_ge(S["var_sb"], 1)
                            for i in range(TILES):
                                dve.bn_stats(st[:, i, :], y[:, i, :]).then_inc(S["var_sb"], 1)
                            dve.wait_ge(S["var_sb"], 1 + TILES)
                            for i in range(TILES):
                                dve.bn_aggr(mv[:, i, :], st[:, i, :]).then_inc(S["var_sb"], 1)
                        if due("normalise", place, tail):
                            dve.wait_ge(S["var_sb"], 1 + 2 * TILES)
                            dve.wait_ge(S["rstd_sb"], 1)
                            for i in range(TILES):
                                dve.tensor_scalar(y2[:, i, :], y[:, i, :], mv[:, i, 0:1], rstd[:, i:i + 1], ALU.subtract, ALU.mult).then_inc(S["x1_sb"], 1)

                    for r in range(STEPS):
                        for part in range(PARTS):
                            if main and r < PAIRS:
                                i, heads = MAX_PARTS[part]
                                unit = PARTS * r + part
                                bank, n = max_bank(unit, max(0, r - (part <= MAXIMA_AT))), P * i + P
                                dve.wait_ge(S["s_ps"], unit + 1)
                                dve.tensor_reduce(mN[:, i, 2 * r + heads[0]:2 * r + heads[-1] + 1],
                                                  ps[:, bank, 0:len(heads) * n].rearrange("p (e n) -> p e n", n=n), AX_X, ALU.max).then_inc(S["max_sb"], 1)
                            if main and part == 0 and 1 <= r <= PAIRS:
                                heads = slice(2 * (r - 1), 2 * r)
                                dve.wait_ge(S["max_sb"], PARTS * r)
                                mh, ml = mS[:, :, heads, 0], mS[:, :, heads, 1]
                                dve.tensor_copy(mh, mN[:, :, heads]).then_inc(S["mS_sb"], 1)
                                dve.wait_ge(S["mS_sb"], 2 * r - 1)
                                dve.tensor_tensor(ml, mN[:, :, heads], mh, ALU.subtract).then_inc(S["mS_sb"], 1)
                            if main and part == 2 and r >= LAG + 2:
                                c = r - LAG - 2
                                if c == 0 and tail is not None:
                                    dve.wait_ge(S["num_sb"], 1)
                                dve.wait_ge(S["tr_ps"], c + 1)
                                for e in TWO:
                                    h = 2 * c + e
                                    src = ps[:, TURN, :].rearrange("p (i m) -> p i m", i=TILES)[:, :, 64 * e:64 * e + NODES * AUG]
                                    dve.tensor_tensor(Zn[:, :, h, :].rearrange("p i (n d) -> p i n d", n=NODES),
                                                      src.rearrange("p i (n d) -> p i n d", n=NODES),
                                                      bcast(prob_q[:, :, NODES * h:NODES * h + NODES], AUG), ALU.mult).then_inc(S["Z_sb"], 1)
                            front_and_tail((r, part))
                    if front is not None:
                        dve.wait_ge(S["prob_sb"], 1)
                        if main:
                            dve.wait_ge(S["Z_sb"], 2 * PAIRS)
                        dve.tensor_copy(prob_q[:], prob[:, :, 0, :]).then_inc(S["prob_q_sb"], 1)

                @block.scalar
                def _(act):
                    fqs = rope_freqs()

                    def front_and_tail(place):
                        if due("turn x", place, front):
                            act.wait_ge(S["xT_ps"], 1)
                            act.activation(xT[:], ps[:, F1, :], ACT.Copy).then_inc(S["xT_sb"], 1)
                        if due("values", place, front):
                            for half, bank in enumerate((F2, F1)):
                                act.wait_ge(S["vr_ps"], half + 1)
                                vr = ps[:, bank, 0:2 * (DIM + HN)].rearrange("p (i m) -> p i m", i=2)
                                act.activation(lg[:, 2 * half:2 * half + 2, :], vr[:, :, DIM:], ACT.Copy).then_inc(S["lg_sb"], 1)
                                act.activation(v1[:, 2 * half:2 * half + 2, :, 0:HD_A], vr[:, :, 0:DIM].rearrange("p i (h d) -> p i h d", d=HD_A),
                                               ACT.Copy).then_inc(S["v1_sb"], 1)
                        if due("node max", place, front):
                            act.wait_ge(S["lg_shifted"], 1)
                            act.activation(ex[:], lg[:], ACT.Exp).then_inc(S["ex_sb"], 1)
                        if due("turn probs", place, front):
                            act.wait_ge(S["pT_ps"], 1)
                            act.activation(pT[:], ps[:, F1, :], ACT.Copy).then_inc(S["pT_sb"], 1)
                        if due("sines", place, front):
                            act.wait_ge(S["pn_sb"], 1)
                            act.activation(G[:, 3, :], pn[:], ACT.Sin, bias=cols[:, 1:2], scale=float(fqs[3])).then_inc(S["G_sb"], 1)
                            for f in range(3):
                                act.wait_ge(S["z_sb"], 3 + f)
                                act.activation(G[:, f, :], zz[:, f, :], ACT.Sin, bias=cols[:, 1:2], scale=float(fqs[f])).then_inc(S["G_sb"], 1)
                            nc.scalar.preload_act_table_set("natural_log_exp_and_others")
                        if due("node cosines", place, front):
                            act.wait_ge(S["cs_ps"], 1)
                            act.activation(cs[:], ps[:, F1, :], ACT.Copy).then_inc(S["cs_sb"], 1)
                        if due("cosines", place, front):
                            for t in TWO:
                                act.wait_ge(S["rope_ps"], t + 1)
                                act.activation(cw[:, t, :], ps[:, (F1, F2)[t], :], ACT.Copy).then_inc(S["cw_sb"], 1)
                        if due("turn attended", place, tail):
                            act.wait_ge(S["aT_ps"], 1)
                            act.activation(aT[:], ps[:, TURN, :], ACT.Copy).then_inc(S["aT_sb"], 1)
                        if due("variance", place, tail):
                            act.wait_ge(S["var_sb"], 1 + 2 * TILES)
                            act.activation(lnv[:], mv[:, :, 1], ACT.Ln, bias=cols[:, 2:3]).then_inc(S["act_order"], 1)
                            act.wait_ge(S["act_order"], 1)
                            act.activation(rstd[:], lnv[:], ACT.Exp, scale=-0.5).then_inc(S["rstd_sb"], 1)
                        if due("turn output", place, tail):
                            act.wait_ge(S["x1T_ps"], 1)
                            act.activation(x1T[:], ps[:, TURN, :], ACT.Copy).then_inc(S["x1T_sb"], 1)

                    nc.scalar.preload_act_table_set("natural_log_exp_and_others")
                    for r in range(STEPS):
                        for part in range(PARTS):
                            if main and part == MAXIMA_AT and 1 <= r <= PAIRS:
                                p = r - 1
                                act.wait_ge(S["mT_ps"], p + 1)
                                bank = max_bank(PARTS * min(p + 1, PAIRS) + (MAXIMA_AT + 1 if p + 1 < PAIRS else 0), p)
                                act.activation(q_now[M_ROWS, p, :], ps[M_ROWS, bank, :].bitcast(BF16)[:, 0:SEQ], ACT.Copy).then_inc(S["mT_sb"], 1)
                            if main and LAG <= r < PAIRS + LAG:
                                p = r - LAG
                                t = PARTS * p + part
                                j, heads = T_PARTS[part]
                                if part == 0 and p >= 2:
                                    act.wait_ge(S["pv_ps"], p - 1)
                                act.wait_ge(S["sT_ps"], t + 1)
                                n = E_COLS[j]
                                act.activation(E[p % 2][:, heads[0]:heads[-1] + 1, E_OFF[j]:E_OFF[j] + n],
                                               ps[:, RING_T[t % 2], 0:len(heads) * n].rearrange("p (e n) -> p e n", n=n),
                                               ACT.Exp, scale=SCALE_A).then_inc(S["E_sb"], 1)
                            if main and part == PARTS - 1 and LAG < r <= PAIRS + LAG:
                                c = r - LAG - 1
                                act.wait_ge(S["pv_ps"], c + 1)
                                if c >= 2:
                                    act.wait_ge(S["tr_ps"], c - 1)
                                act.activation(Ot[c % 2][:], ps[:, PV, :], ACT.Copy).then_inc(S["Ot_sb"], 1)
                            front_and_tail((r, part))

                @block.gpsimd
                def _(pool):
                    if front is None:
                        return
                    pool.wait_ge(S["prob_sb"], 1)
                    pool.tensor_scalar(probe[:], prob[:, :, 0, :], 1e-8, None, ALU.add).then_inc(S["pool_order"], 1)
                    pool.wait_ge(S["pn_sb"], 1)
                    pool.tensor_tensor(fr[:], posc[:], pn[:], ALU.subtract).then_inc(S["parts_sb"], 1)
                    pool.wait_ge(S["parts_sb"], 1)
                    pool.wait_ge(S["pT_sb"], 1)
                    pool.tensor_tensor(pnext[:], pT[:], fr[:], ALU.mult).then_inc(S["parts_sb"], 1)
                    pool.wait_ge(S["parts_sb"], 2)
                    pool.tensor_tensor(phere[:], pT[:], pnext[:], ALU.subtract).then_inc(S["parts_sb"], 1)
                    for n, f in enumerate((3, 0, 1, 2)):
                        pool.wait_ge(S["G_sb"], n + 1)
                        pool.tensor_tensor(V[:, f, :], G[:, f, :], pnext[:], ALU.mult).then_inc(S["V_sb"], 1)
                    for n, t in enumerate((tq, tk)):
                        pool.wait_ge(S["turned"], n + 1)
                        pool.tensor_tensor(qk[:, n, :], t[:, 0, :], t[:, 1, :], ALU.add).then_inc(S["qk_sb"], 1)
                    pool.wait_ge(S["pool_order"], 1)
                    pool.wait_ge(S["v1_sb"], 2)
                    for c in range(PAIRS):
                        if main:
                            pool.wait_ge(S["pv_ps"], c + 1)
                        for e in TWO:
                            h = 2 * c + e
                            dst = v2[:, :, h * NODES * AUG:(h + 1) * NODES * AUG].rearrange("p i (n d) -> p i n d", n=NODES)
                            pool.tensor_tensor(dst, bcast(probe[:, :, NODES * h:NODES * h + NODES], AUG),
                                               bcast_mid(v1[:, :, h, :], 2, NODES), ALU.mult).then_inc(S["v2_sb"], 1)

            end_turn(nc, S)

        turn(front=0, main=False, tail=None, now=1, ahead=1)
        turn(front=1, main=True, tail=None, now=0, ahead=2 if loops > 2 else None)
        with nc.Fori(0, (loops - 4) // 2) as n:
            for k in TWO:
                turn(front=2 * n + k + 2, main=True, tail=2 * n + k, now=1 - k, ahead=2 * n + k + 3)
        turn(front=loops - 2, main=True, tail=loops - 4, now=1, ahead=loops - 1)
        turn(front=loops - 1, main=True, tail=loops - 3, now=0)
        turn(front=None, main=True, tail=loops - 2, now=1)
        turn(front=None, main=False, tail=loops - 1, now=0)


def end_turn(nc, *stages):
    nums = sorted(s.num for stage in stages for s in stage.all.values())
    starts = [n for n in nums if n - 1 not in nums]
    ends = [n + 1 for n in nums if n + 1 not in nums]
    for a, z in zip(starts, ends):
        nc.all_engine_barrier(sems_to_clear=range(a, z))


def local_attention_layers(nc, io, xs, loops=BATCH, depth=DEPTH):
    ctx = ExitStack()
    with ctx:
        def sb(name, shape, dt=F32):
            return ctx.enter_context(nc.sbuf_tensor("b_" + name, shape, dt))

        def two(name, shape, dt=F32):
            return [sb(f"{name}{u}", shape, dt) for u in TWO]

        ident, ident_b, ones = sb("ident", [P, P]), sb("ident_b", [P, P], BF16), sb("ones", [P, 64])
        mean_w = sb("mean_w", [P, P])
        mask, neg_sel = sb("mask", [P, 3, SPAN], BF16), sb("neg_sel", [P, HEADS_B, P], BF16)
        tab = sb("tab", [P, 2, TILES, 2, HD_B])
        scales = sb("scales", [P, 2, HD_B])
        cols = sb("cols", [P, 3])
        w_qkv, w_o = sb("w_qkv", [P, 3 * INNER]), sb("w_o", [P, CHUNKS, DIM])
        w1, w2 = sb("w1", [P, 2 * HID]), sb("w2", [P, 3, DIM])
        vec = sb("vec", [P, 3])
        b1 = sb("b1", [P, 2, 3])
        xT, hT, x1 = two("xT", [P, SEQ]), two("hT", [P, SEQ]), two("x1", [P, SEQ])
        v = two("v", [P, TILES, INNER])
        raw, rot, sq = (two(n, [P, 2 * INNER]) for n in ("raw", "rot", "sq"))
        W = two("W", [P, TILES * 2 * INNER])
        ss, nrm, rn = (two(n, [P, TILES, 2 * HEADS_B]) for n in ("ss", "nrm", "rn"))
        QT = two("QT", [P, CHUNKS, PAD])
        KM = two("KM", [P, CHUNKS, 2, PAD])
        QTb, KMb = two("QTb", [P, CHUNKS, SEQ], BF16), two("KMb", [P, CHUNKS, 2, PAD], BF16)
        mN, mS = two("mN", [P, TILES, HEADS_B]), two("mS", [P, TILES, HEADS_B, 2], BF16)
        mT = two("mT", [P, PAD], BF16)
        ps = ctx.enter_context(nc.psum_tensor("b_ps", [P, 8, SEQ], F32))
        def room(u, at, *shape):
            n = int(np.prod(shape))
            names = " ".join(f"d{i}" for i in range(len(shape)))
            sizes = {f"d{i}": x for i, x in enumerate(shape)}
            return W[u][:, at:at + n].rearrange(f"p ({names}) -> p {names}", **sizes)

        oT = [room(u, 0, CHUNKS, SEQ) for u in TWO]
        E = [room(u, CHUNKS * SEQ, 2, TILES, SPAN) for u in TWO]
        rd = [room(u, CHUNKS * SEQ + 2 * TILES * SPAN, SEQ) for u in TWO]
        h2 = two("h2", [P, SEQ])
        hc, sq2, rs = ([room(u, n * SEQ, SEQ) for u in TWO] for n in range(3))
        gl = [v[u][:].rearrange("p i n -> p (i n)")[:, 0:3 * SEQ].rearrange("p (c n) -> p c n", c=3) for u in TWO]

        ld, zeroed = ctx.enter_context(nc.semaphore("b_consts_loaded")), ctx.enter_context(nc.semaphore("b_zeroed"))
        wl, tabled = ctx.enter_context(nc.semaphore("b_weights_loaded")), ctx.enter_context(nc.semaphore("b_tables_scaled"))
        S = [Sems(nc, ctx, """x_loaded qkv_ps raw_sb v_sb sq_sb ss_sb U_sb V_sb nrm_sb rn_sb W_sb Wn_sb Wk_sb qT_ps kT_ps QT_sb KM_sb QTb_sb KMb_sb
            s_ps max_sb mS_sb mT_ps mT_sb sT_ps E_sb num_ps lnd_sb rd_sb oT_sb wo_ps x1_sb h2_sb mean_ps hc_sb sq2_sb
            var_ps lnv_sb rs_sb hn_sb g_ps a_ps gl_sb u_sb w2_ps xo_sb stored""", f"b{u}") for u in TWO]

        with nc.Block() as block:
            @block.sync
            def _(sp):
                sp.dma_start(ident[:], io["ident"]).then_inc(ld, 16)
                sp.dma_start(ident_b[:], io["ident_b"]).then_inc(ld, 16)
                sp.dma_start(mask[:], io["mask_b"]).then_inc(ld, 16)
                sp.dma_start(neg_sel[:], io["neg_sel"]).then_inc(ld, 16)
                sp.dma_start(cols[:], io["cols"]).then_inc(ld, 16)
                sp.wait_ge(ld, 80)

            @block.gpsimd
            def _(pool):
                for u in TWO:
                    for buf in (KM, QT, KMb, mT, hT, h2):
                        nc.gpsimd.memset(buf[u][:], 0.0).then_inc(zeroed, 1)
                nc.gpsimd.memset(ones[:], 1.0).then_inc(zeroed, 1)
                nc.gpsimd.memset(mean_w[:], 1.0 / DIM).then_inc(zeroed, 1)

        xs2 = xs.rearrange("l (b u) p n -> l b u p n", u=2)
        with nc.Fori(0, depth) as l:
            with nc.Block() as block:
                @block.sync
                def _(sp):
                    sp.dma_start(tab[:].rearrange("p a i t d -> p (a i t d)"), io["xpos"]).then_inc(wl, 16)
                    sp.dma_start(w_qkv[:], io["L0_ffn_wqkv"][l]).then_inc(wl, 16)
                    sp.dma_start(w_o[:], io["L0_ffn_wo"][l].rearrange("(c p) m -> p c m", p=P)).then_inc(wl, 16)
                    sp.dma_start(w1[:], io["L0_ffn_w1"][l]).then_inc(wl, 16)
                    for n, name in enumerate(("q_scale", "k_scale")):
                        sp.dma_start(scales[:, n, :], io["L0_ffn_" + name][l].partition_broadcast(P)).then_inc(wl, 16)
                    sp.wait_ge(wl, 16 * LAYER_LOADS)

                @block.scalar
                def _(act):
                    for c, (o, n) in enumerate(HID_PARTS):
                        act.dma_start(w2[0:n, c, :], io["L0_ffn_w2"][l][o:o + n, :]).then_inc(wl, 16)
                        for g in range(2):
                            act.dma_start(b1[0:n, g, c:c + 1], io["L0_ffn_b1"][l][g * HID + o:g * HID + o + n].unsqueeze(1)).then_inc(wl, 16)
                    for n, name in enumerate(("ln_g", "ln_b", "b2")):
                        act.dma_start(vec[:, n:n + 1], io["L0_ffn_" + name][l].unsqueeze(1)).then_inc(wl, 16)

                @block.vector
                def _(dve):
                    dve.wait_ge(wl, 16 * LAYER_LOADS)
                    for i in range(TILES):
                        dve.tensor_tensor(tab[:, 0, i, :, :], tab[:, 0, i, :, :], scales[:], ALU.mult).then_inc(tabled, 1)
                        for half in range(2):
                            a, o = half * HD_B // 2, (1 - half) * HD_B // 2
                            dve.tensor_tensor(tab[:, 1, i, :, a:a + HD_B // 2], tab[:, 1, i, :, a:a + HD_B // 2],
                                              scales[:, :, o:o + HD_B // 2], ALU.mult).then_inc(tabled, 1)

            with nc.Fori(0, loops // 2) as b:
                with nc.Block() as block:
                    @block.sync
                    def _(sp):
                        for u in TWO:
                            src = xs2[l, b, u]
                            sp.dma_start(hT[u][0:64, :], src[0:64, :]).then_inc(S[u]["x_loaded"], 16)
                            sp.dma_start(hT[u][64:P, 1:SEQ], src[64:P, 0:SEQ - 1]).then_inc(S[u]["x_loaded"], 16)
                            sp.dma_start(xT[u][:], src).then_inc(S[u]["x_loaded"], 16)
                        for u in TWO:
                            sp.wait_ge(S[u]["xo_sb"], 1)
                            sp.dma_start(xs2[l + 1, b, u], xT[u][:]).then_inc(S[u]["stored"], 16)
                        for u in TWO:
                            sp.wait_ge(S[u]["stored"], 16)

                    @block.tensor
                    def _(pe):
                        for i in range(TILES):
                            for u in TWO:
                                if i == 0:
                                    pe.wait_ge(S[u]["x_loaded"], 48)
                                else:
                                    pe.wait_ge(S[u]["raw_sb"], i)
                                for n in range(2):
                                    pe.matmul(ps[:, 4 * u + n, :], hT[u][:, P * i:P * i + P], w_qkv[:, INNER * n:INNER * n + INNER],
                                              start=True, stop=True).then_inc(S[u]["qkv_ps"], 1)
                                if i >= 1:
                                    pe.wait_ge(S[u]["v_sb"], i)
                                pe.matmul(ps[:, 4 * u + 2, :], hT[u][:, P * i:P * i + P], w_qkv[:, 2 * INNER:3 * INNER],
                                          start=True, stop=True).then_inc(S[u]["qkv_ps"], 1)
                        for i in range(TILES):
                            for u in TWO:
                                qb = 4 * u + 2 * (i % 2)
                                pe.wait_ge(S[u]["Wn_sb"], i + 1)
                                if i == 0:
                                    pe.wait_ge(S[u]["raw_sb"], TILES)
                                if i == 1:
                                    pe.wait_ge(S[u]["v_sb"], TILES)
                                if i >= 2:
                                    pe.wait_ge(S[u]["QTb_sb"], i - 1)
                                    pe.wait_ge(S[u]["KM_sb"], 2 * (i - 1))
                                for n, done in enumerate(("qT_ps", "kT_ps")):
                                    if n == 1:
                                        pe.wait_ge(S[u]["Wk_sb"], i + 1)
                                    for c in range(CHUNKS):
                                        at = 2 * INNER * i + INNER * n + P * c
                                        last = pe.transpose(ps[:, qb + n, P * c:P * c + P], W[u][:, at:at + P], ident[:])
                                    last.then_inc(S[u][done], 1)
                        for unit in range(2 * CHUNKS):
                            c, half = unit // 2, unit % 2
                            for u in TWO:
                                if unit == 0:
                                    pe.wait_ge(S[u]["QTb_sb"], TILES)
                                    pe.wait_ge(S[u]["KMb_sb"], 2 * TILES)
                                if unit >= 2:
                                    pe.wait_ge(S[u]["max_sb"], unit - 1)
                                for e in range(2):
                                    for n in range(2):
                                        i = 2 * half + n
                                        o = ps[:, 4 * u + 2 * (unit % 2) + e, SPAN * n:SPAN * n + SPAN]
                                        pe.matmul(o, QTb[u][:, c, P * i:P * i + P], KMb[u][:, c, e, P * i:P * i + SPAN], start=True, stop=False)
                                        last = pe.matmul(o, ident_b[:], mask[:, min(i, 1), :], start=False, stop=True)
                                last.then_inc(S[u]["s_ps"], 1)
                        for u in TWO:
                            pe.wait_ge(S[u]["mS_sb"], 2)
                            for i in range(TILES):
                                last = pe.transpose(ps[0:2 * HEADS_B, 4 * u, :].bitcast(BF16)[:, P * i:P * i + P],
                                                    mS[u][:, i, :, :].rearrange("p h l -> p (h l)"), ident_b[:])
                            last.then_inc(S[u]["mT_ps"], 1)
                        for c in range(CHUNKS):
                            for half in range(2):
                                for u in TWO:
                                    if c == half == 0:
                                        pe.wait_ge(S[u]["mT_sb"], 1)
                                    else:
                                        pe.wait_ge(S[u]["E_sb"], 2 * c + half)
                                    for e in range(2):
                                        for n in range(2):
                                            j = 2 * half + n
                                            o = ps[:, 4 * u + e, SPAN * n:SPAN * n + SPAN]
                                            pe.matmul(o, KM[u][:, c, e, WINDOW + P * j:WINDOW + P * j + P], QT[u][:, c, P * j:P * j + SPAN],
                                                      start=True, stop=False)
                                            pe.matmul(o, neg_sel[:, 2 * c + e, :], mT[u][:, P * j:P * j + SPAN], start=False, stop=False)
                                            last = pe.matmul(o, ident_b[:], mask[:, 2, :], start=False, stop=True)
                                    last.then_inc(S[u]["sT_ps"], 1)
                            for u in TWO:
                                if c >= 1:
                                    pe.wait_ge(S[u]["oT_sb"], c)
                                for j in range(TILES):
                                    pe.wait_ge(S[u]["E_sb"], 2 * c + j // 2 + 1)
                                    n = min(SPAN, SEQ - P * j)
                                    for bank in (2, 3):
                                        for e in range(2):
                                            h = 2 * c + e
                                            lhs = v[u][:, j, HD_B * h:HD_B * h + HD_B] if bank == 2 else ones[:]
                                            last = pe.matmul(ps[64 * e:64 * e + 64, 4 * u + bank, P * j:P * j + n], lhs, E[u][:, e, j, 0:n],
                                                             start=j == 0, stop=j == TILES - 1, skip_group_check=True)
                                last.then_inc(S[u]["num_ps"], 1)
                        for u in TWO:
                            pe.wait_ge(S[u]["oT_sb"], CHUNKS)
                            for c in range(CHUNKS):
                                last = pe.matmul(ps[:, 4 * u, :], w_o[:, c, :], oT[u][:, c, :], start=c == 0, stop=c == CHUNKS - 1)
                            last.then_inc(S[u]["wo_ps"], 1)
                        for u in TWO:
                            pe.wait_ge(S[u]["h2_sb"], 2)
                            pe.matmul(ps[:, 4 * u + 1, :], mean_w[:], h2[u][:], start=True, stop=True).then_inc(S[u]["mean_ps"], 1)
                        for u in TWO:
                            pe.wait_ge(S[u]["sq2_sb"], 1)
                            pe.matmul(ps[:, 4 * u + 2, :], mean_w[:], sq2[u], start=True, stop=True).then_inc(S[u]["var_ps"], 1)
                        for c, (o, n) in enumerate(HID_PARTS):
                            for u in TWO:
                                if c == 0:
                                    pe.wait_ge(S[u]["hn_sb"], 2)
                                if c == 2:
                                    pe.wait_ge(S[u]["u_sb"], 1)
                                gb, ab = ((3, 0), (1, 2), (3, 0))[c]
                                pe.matmul(ps[0:n, 4 * u + gb, :], w1[:, HID + o:HID + o + n], h2[u][:], start=True, stop=True).then_inc(S[u]["g_ps"], 1)
                                pe.matmul(ps[0:n, 4 * u + ab, :], w1[:, o:o + n], h2[u][:], start=True, stop=True).then_inc(S[u]["a_ps"], 1)
                        for u in TWO:
                            for c, (o, n) in enumerate(HID_PARTS):
                                pe.wait_ge(S[u]["u_sb"], max(c + 1, 2))
                                last = pe.matmul(ps[:, 4 * u + 1, :], w2[0:n, c, :], gl[u][0:n, c, :], start=c == 0, stop=c == 2)
                            last.then_inc(S[u]["w2_ps"], 1)

                    @block.vector
                    def _(dve):
                        heads = "p (t h d) -> p t h d"
                        for i in range(TILES):
                            for u in TWO:
                                at = 2 * INNER * i
                                src = raw[u][:].rearrange(heads, t=2, d=HD_B)
                                dve.wait_ge(S[u]["raw_sb"], i + 1)
                                dve.tensor_tensor(W[u][:, at:at + 2 * INNER].rearrange(heads, t=2, d=HD_B), src,
                                                  bcast_mid(tab[:, 0, i, :, :], 2, HEADS_B), ALU.mult).then_inc(S[u]["U_sb"], 1)
                                if i >= 1:
                                    dve.wait_ge(S[u]["W_sb"], i)
                                for half in range(2):
                                    a, o = half * HD_B // 2, (1 - half) * HD_B // 2
                                    dve.tensor_tensor(rot[u][:].rearrange(heads, t=2, d=HD_B)[:, :, :, a:a + HD_B // 2],
                                                      src[:, :, :, o:o + HD_B // 2],
                                                      bcast_mid(tab[:, 1, i, :, a:a + HD_B // 2], 2, HEADS_B), ALU.mult).then_inc(S[u]["V_sb"], 1)
                                dve.wait_ge(S[u]["sq_sb"], i + 1)
                                dve.tensor_reduce(ss[u][:, i, :], sq[u][:].rearrange("p (h d) -> p h d", d=HD_B), AX_X, ALU.add).then_inc(S[u]["ss_sb"], 1)
                        for u in TWO:
                            dve.wait_ge(S[u]["nrm_sb"], 1)
                            dve.tensor_scalar(nrm[u][:], nrm[u][:], NORM_MIN, None, ALU.max).then_inc(S[u]["rn_sb"], 1)
                        for u in TWO:
                            dve.wait_ge(S[u]["rn_sb"], 1)
                            dve.reciprocal(rn[u][:], nrm[u][:]).then_inc(S[u]["rn_sb"], 1)

                        def normalise(i, u):
                            dve.wait_ge(S[u]["rn_sb"], 2)
                            dve.wait_ge(S[u]["W_sb"], i + 1)
                            w = W[u][:, 2 * INNER * i:2 * INNER * i + INNER].rearrange("p (h d) -> p h d", d=HD_B)
                            dve.tensor_tensor(w, w, bcast(rn[u][:, i, 0:HEADS_B], HD_B), ALU.mult).then_inc(S[u]["Wn_sb"], 1)

                        def keep_k(i, u):
                            dve.wait_ge(S[u]["kT_ps"], i + 1)
                            src = ps[:, 4 * u + 2 * (i % 2) + 1, :].rearrange("p (c n) -> p c n", c=CHUNKS)
                            for e in range(2):
                                rows = slice(64 * e, 64 * e + 64)
                                dve.tensor_copy(KM[u][rows, :, e, WINDOW + P * i:WINDOW + P * i + P], src[rows]).then_inc(S[u]["KM_sb"], 1)

                        for i in range(TILES + 1):
                            for u in TWO:
                                if i < TILES:
                                    normalise(i, u)
                                if i >= 1:
                                    keep_k(i - 1, u)
                        for unit in range(2 * CHUNKS):
                            c, half = unit // 2, unit % 2
                            for u in TWO:
                                dve.wait_ge(S[u]["s_ps"], unit + 1)
                                lo = 4 * u + 2 * (unit % 2)
                                src = ps[:, lo:lo + 2, 0:2 * SPAN].rearrange("p e (n s) -> p n e s", n=2)
                                dve.tensor_reduce(mN[u][:, 2 * half:2 * half + 2, 2 * c:2 * c + 2], src, AX_X, ALU.max).then_inc(S[u]["max_sb"], 1)
                        for u in TWO:
                            dve.wait_ge(S[u]["max_sb"], 2 * CHUNKS)
                            dve.tensor_copy(mS[u][:, :, :, 0], mN[u][:]).then_inc(S[u]["mS_sb"], 1)
                            dve.wait_ge(S[u]["mS_sb"], 1)
                            dve.tensor_tensor(mS[u][:, :, :, 1], mN[u][:], mS[u][:, :, :, 0], ALU.subtract).then_inc(S[u]["mS_sb"], 1)
                        for c in range(CHUNKS):
                            for u in TWO:
                                dve.wait_ge(S[u]["num_ps"], c + 1)
                                dve.wait_ge(S[u]["rd_sb"], c + 1)
                                dve.tensor_tensor(oT[u][:, c, :], ps[:, 4 * u + 2, :], rd[u], ALU.mult).then_inc(S[u]["oT_sb"], 1)
                        for u in TWO:
                            dve.wait_ge(S[u]["wo_ps"], 1)
                            dve.tensor_tensor(x1[u][:], ps[:, 4 * u, :], xT[u][:], ALU.add).then_inc(S[u]["x1_sb"], 1)
                            dve.wait_ge(S[u]["x1_sb"], 1)
                            dve.tensor_copy(h2[u][0:64, :], x1[u][0:64, :]).then_inc(S[u]["h2_sb"], 1)
                            dve.tensor_copy(h2[u][64:P, 1:SEQ], x1[u][64:P, 0:SEQ - 1]).then_inc(S[u]["h2_sb"], 1)
                        for u in TWO:
                            dve.wait_ge(S[u]["h2_sb"], 2)
                            dve.wait_ge(S[u]["mean_ps"], 1)
                            dve.tensor_tensor(hc[u], h2[u][:], ps[:, 4 * u + 1, :], ALU.subtract).then_inc(S[u]["hc_sb"], 1)
                        for u in TWO:
                            dve.wait_ge(S[u]["hc_sb"], 1)
                            dve.wait_ge(S[u]["rs_sb"], 1)
                            dve.tensor_tensor(hc[u], hc[u], rs[u], ALU.mult).then_inc(S[u]["hn_sb"], 1)
                            dve.wait_ge(S[u]["hn_sb"], 1)
                            dve.tensor_scalar(h2[u][:], hc[u], vec[:, 0:1], vec[:, 1:2], ALU.mult, ALU.add).then_inc(S[u]["hn_sb"], 1)
                        for c, (o, n) in enumerate(HID_PARTS):
                            for u in TWO:
                                ab = (0, 2, 0)[c]
                                dve.wait_ge(S[u]["a_ps"], c + 1)
                                dve.wait_ge(S[u]["gl_sb"], c + 1)
                                dve.scalar_tensor_tensor(gl[u][0:n, c, :], ps[0:n, 4 * u + ab, :], b1[0:n, 0, c:c + 1], gl[u][0:n, c, :],
                                                         ALU.add, ALU.mult).then_inc(S[u]["u_sb"], 1)
                        for u in TWO:
                            dve.wait_ge(S[u]["w2_ps"], 1)
                            dve.scalar_tensor_tensor(xT[u][:], ps[:, 4 * u + 1, :], vec[:, 2:3], x1[u][:], ALU.add, ALU.add).then_inc(S[u]["xo_sb"], 1)
                            dve.memset(h2[u][64:P, 0:1], 0.0).then_inc(S[u]["xo_sb"], 1)

                    @block.scalar
                    def _(act):
                        for i in range(TILES):
                            for u in TWO:
                                if i >= 1:
                                    act.wait_ge(S[u]["U_sb"], i)
                                    act.wait_ge(S[u]["V_sb"], 2 * i)
                                    act.wait_ge(S[u]["ss_sb"], i)
                                act.wait_ge(S[u]["qkv_ps"], 3 * i + 2)
                                act.activation(raw[u][:].rearrange("p (t n) -> p t n", t=2), ps[:, 4 * u:4 * u + 2, :], ACT.Copy).then_inc(S[u]["raw_sb"], 1)
                                act.wait_ge(S[u]["qkv_ps"], 3 * i + 3)
                                act.activation(v[u][:, i, :], ps[:, 4 * u + 2, :], ACT.Copy).then_inc(S[u]["v_sb"], 1)
                                act.wait_ge(S[u]["raw_sb"], i + 1)
                                act.activation(sq[u][:], raw[u][:], ACT.Square).then_inc(S[u]["sq_sb"], 1)
                        for u in TWO:
                            act.wait_ge(S[u]["ss_sb"], TILES)
                            act.activation(nrm[u][:], ss[u][:], ACT.Sqrt).then_inc(S[u]["nrm_sb"], 1)
                        nc.scalar.preload_act_table_set("natural_log_exp_and_others")
                        for i in range(TILES):
                            for u in TWO:
                                act.wait_ge(S[u]["qT_ps"], i + 1)
                                act.activation(QT[u][:, :, P * i:P * i + P], ps[:, 4 * u + 2 * (i % 2), :].rearrange("p (c n) -> p c n", c=CHUNKS),
                                               ACT.Copy).then_inc(S[u]["QT_sb"], 1)
                                act.activation(QTb[u][:, :, P * i:P * i + P], ps[:, 4 * u + 2 * (i % 2), :].rearrange("p (c n) -> p c n", c=CHUNKS),
                                               ACT.Copy).then_inc(S[u]["QTb_sb"], 1)
                                act.wait_ge(S[u]["KM_sb"], 2 * (i + 1))
                                for e in range(2):
                                    rows, cs = slice(64 * e, 64 * e + 64), slice(WINDOW + P * i, WINDOW + P * i + P)
                                    act.activation(KMb[u][rows, :, e, cs], KM[u][rows, :, e, cs], ACT.Copy).then_inc(S[u]["KMb_sb"], 1)
                        for u in TWO:
                            act.wait_ge(S[u]["mT_ps"], 1)
                            act.activation(mT[u][0:2 * HEADS_B, 0:SEQ], ps[0:2 * HEADS_B, 4 * u, :].bitcast(BF16)[:, 0:SEQ], ACT.Copy).then_inc(S[u]["mT_sb"], 1)
                        for c in range(CHUNKS):
                            for half in range(2):
                                for u in TWO:
                                    if c >= 1:
                                        act.wait_ge(S[u]["num_ps"], c)
                                    act.wait_ge(S[u]["sT_ps"], 2 * c + half + 1)
                                    act.activation(E[u][:, :, 2 * half:2 * half + 2, :],
                                                   ps[:, 4 * u:4 * u + 2, 0:2 * SPAN].rearrange("p e (n s) -> p e n s", n=2),
                                                   ACT.Exp, scale=QK_SCALE).then_inc(S[u]["E_sb"], 1)
                            for u in TWO:
                                act.wait_ge(S[u]["num_ps"], c + 1)
                                if c >= 1:
                                    act.wait_ge(S[u]["oT_sb"], c)
                                act.activation(rd[u], ps[:, 4 * u + 3, :], ACT.Ln).then_inc(S[u]["lnd_sb"], 1)
                                act.wait_ge(S[u]["lnd_sb"], c + 1)
                                act.activation(rd[u], rd[u], ACT.Exp, scale=-1.0).then_inc(S[u]["rd_sb"], 1)
                        for u in TWO:
                            act.wait_ge(S[u]["hc_sb"], 1)
                            act.activation(sq2[u], hc[u], ACT.Square).then_inc(S[u]["sq2_sb"], 1)
                        for u in TWO:
                            act.wait_ge(S[u]["var_ps"], 1)
                            act.activation(rs[u], ps[:, 4 * u + 2, :], ACT.Ln, bias=cols[:, 2:3]).then_inc(S[u]["lnv_sb"], 1)
                            act.wait_ge(S[u]["lnv_sb"], 1)
                            act.activation(rs[u], rs[u], ACT.Exp, scale=-0.5).then_inc(S[u]["rs_sb"], 1)
                        for c, (o, n) in enumerate(HID_PARTS):
                            for u in TWO:
                                gb = (3, 1, 3)[c]
                                act.wait_ge(S[u]["g_ps"], c + 1)
                                act.activation(gl[u][0:n, c, :], ps[0:n, 4 * u + gb, :], ACT.Gelu, bias=b1[0:n, 1, c:c + 1]).then_inc(S[u]["gl_sb"], 1)

                    @block.gpsimd
                    def _(pool):
                        for i in range(TILES):
                            for u in TWO:
                                w = W[u][:, 2 * INNER * i:2 * INNER * (i + 1)]
                                pool.wait_ge(S[u]["U_sb"], i + 1)
                                pool.wait_ge(S[u]["V_sb"], 2 * (i + 1))
                                pool.tensor_tensor(w, w, rot[u][:], ALU.add).then_inc(S[u]["W_sb"], 1)
                        for i in range(TILES):
                            for u in TWO:
                                w = W[u][:, 2 * INNER * i + INNER:2 * INNER * (i + 1)].rearrange("p (h d) -> p h d", d=HD_B)
                                pool.wait_ge(S[u]["rn_sb"], 2)
                                pool.wait_ge(S[u]["W_sb"], i + 1)
                                pool.tensor_tensor(w, w, bcast(rn[u][:, i, HEADS_B:], HD_B), ALU.mult).then_inc(S[u]["Wk_sb"], 1)

                end_turn(nc, *S)
            nc.all_engine_barrier(sems_to_clear=range(wl.num, tabled.num + 1))


def final_layernorm(nc, io, xs, out, loops=BATCH):
    with ExitStack() as ctx:
        def sb(name, shape, dt=F32):
            return ctx.enter_context(nc.sbuf_tensor("c_" + name, shape, dt))

        ident, cols = sb("ident", [P, P]), sb("cols", [P, 3])
        xa, xb = ([sb(f"{n}{i}", [P, SEQ]) for i in range(2)] for n in ("xa", "xb"))
        xsum = [sb(f"xsum{i}", [P, SEQ]) for i in range(2)]
        st, mv = sb("st", [P, 2, TILES, 6]), sb("mv", [P, 2, TILES, 2])
        nrm, rstd = sb("nrm", [P, 2, TILES]), sb("rstd", [P, 2, TILES])
        y = [sb(f"y{i}", [P, TILES, DIM]) for i in range(2)]
        ps = ctx.enter_context(nc.psum_tensor("c_ps", [P, 2, SEQ], F32))
        ld = ctx.enter_context(nc.semaphore("c_consts_loaded"))
        S = Sems(nc, ctx, "a_loaded b_loaded sum_sb y_ps st_sb mv_sb nrm_sb rstd_sb y_sb stored", "c")

        with nc.Block() as block:
            @block.sync
            def _(sp):
                sp.dma_start(ident[:], io["ident"]).then_inc(ld, 16)
                sp.dma_start(cols[:], io["cols"]).then_inc(ld, 16)
                sp.wait_ge(ld, 32)

        xs2 = xs.rearrange("l (b u) p n -> l b u p n", u=2)
        out2 = out.rearrange("(b u) (i p) e -> b u p i e", u=2, p=P)
        with nc.Fori(0, loops // 2) as b:
            with nc.Block() as block:
                @block.sync
                def _(sp):
                    for u in range(2):
                        sp.dma_start(xa[u][:], xs2[0, b, u]).then_inc(S["a_loaded"], 16)
                        sp.dma_start(xb[u][:], xs2[DEPTH, b, u]).then_inc(S["b_loaded"], 16)
                    for u in range(2):
                        sp.wait_ge(S["y_sb"], TILES * (u + 1))
                        sp.dma_start(out2[b, u], y[u][:]).then_inc(S["stored"], 16)
                    sp.wait_ge(S["stored"], 32)

                @block.tensor
                def _(pe):
                    for u in range(2):
                        pe.wait_ge(S["sum_sb"], u + 1)
                        for i in range(TILES):
                            last = pe.transpose(ps[:, u, P * i:P * i + P], xsum[u][:, P * i:P * i + P], ident[:])
                        last.then_inc(S["y_ps"], 1)

                @block.vector
                def _(dve):
                    dve.wait_ge(S["a_loaded"], 32)
                    dve.wait_ge(S["b_loaded"], 32)
                    for u in range(2):
                        dve.tensor_tensor(xsum[u][:], xa[u][:], xb[u][:], ALU.add).then_inc(S["sum_sb"], 1)
                    for u in range(2):
                        dve.wait_ge(S["y_ps"], u + 1)
                        for i in range(TILES):
                            dve.bn_stats(st[:, u, i, :], ps[:, u, P * i:P * i + P]).then_inc(S["st_sb"], 1)
                    dve.wait_ge(S["st_sb"], 2 * TILES)
                    for u in range(2):
                        for i in range(TILES):
                            dve.bn_aggr(mv[:, u, i, :], st[:, u, i, :]).then_inc(S["mv_sb"], 1)
                    dve.wait_ge(S["mv_sb"], 2 * TILES)
                    dve.wait_ge(S["nrm_sb"], 1)
                    dve.reciprocal(rstd[:], nrm[:]).then_inc(S["rstd_sb"], 1)
                    dve.wait_ge(S["rstd_sb"], 1)
                    for u in range(2):
                        for i in range(TILES):
                            dve.tensor_scalar(y[u][:, i, :], ps[:, u, P * i:P * i + P], mv[:, u, i, 0:1], rstd[:, u, i:i + 1],
                                              ALU.subtract, ALU.mult).then_inc(S["y_sb"], 1)

                @block.scalar
                def _(act):
                    act.wait_ge(S["mv_sb"], 2 * TILES)
                    act.activation(nrm[:], mv[:, :, :, 1], ACT.Sqrt, bias=cols[:, 2:3]).then_inc(S["nrm_sb"], 1)

            end_turn(nc, S)


DIRECT = ["L0_attn_x"] + ["L0_ffn_" + n for n in ("wqkv", "q_scale", "k_scale", "wo", "ln_g", "ln_b", "w1", "b1", "w2", "b2")]


def lay_out(inputs):
    arrays = {n: np.ascontiguousarray(inputs[n]) for n in DIRECT}
    wq, wk, wv, wr, wo = (np.asarray(inputs["L0_attn_W" + n]) for n in "qkvro")
    other_half = np.arange(DIM).reshape(HEADS_A, 2, FREQS)[:, ::-1].reshape(DIM)
    arrays["w_vr"] = np.concatenate([wv, wr], 1)
    arrays["w_qk"] = np.stack([wq, wq[:, other_half], wk, wk[:, other_half]])
    arrays["w_o"] = np.ascontiguousarray(wo)
    arrays.update(constants())
    return arrays


def build(nc, io, out):
    xs = nc.dram_tensor("xs", [DEPTH + 1, BATCH, DIM, SEQ], F32).ap()
    scratch = nc.dram_tensor("split_qk", [3, 2, HEADS_A, HD_A, SEQ], BF16).ap()
    soft_rope_attention(nc, io, xs, scratch)
    local_attention_layers(nc, io, xs)
    final_layernorm(nc, io, xs, out)


def kernel(**inputs):
    import concourse.bacc as bacc
    from concourse.bass_utils import run_bass_kernel_spmd

    nc = bacc.Bacc("TRN2", target_bir_lowering=False, num_devices=1)
    arrays = lay_out(inputs)
    io = {n: nc.dram_tensor(f"in_{n}_dram", a.shape, mybir.dt.from_np(a.dtype), kind="ExternalInput").ap() for n, a in arrays.items()}
    out = nc.dram_tensor("out_0_dram", (BATCH, SEQ, DIM), F32, kind="ExternalOutput").ap()
    build(nc, io, out)
    r = run_bass_kernel_spmd(nc, [{f"in_{n}_dram": a for n, a in arrays.items()}], core_ids=[0])
    return r.results[0]["out_0_dram"]
```

```python
from contextlib import ExitStack

import numpy as np

import concourse.bass as bass
from concourse import mybir

ALU = mybir.AluOpType
ACT = mybir.ActivationFunctionType
AX_X = mybir.AxisListType.X
F32 = mybir.dt.float32
BF16 = mybir.dt.bfloat16

P = 128
BATCH, SEQ, DIM = 8, 512, 128
TILES = SEQ // P

HEADS_A, HD_A, NODES = 16, 8, 4
FREQS = HD_A // 2
HN = HEADS_A * NODES
PAIRS = HEADS_A // 2
AUG = HD_A + 1
SCALE_A = HD_A ** -0.5
MAX_POS = 1023.0
ROUND = 12582912.0
SPLIT_PRODUCTS = ((0, 0), (0, 1), (1, 0), (0, 2), (2, 0), (1, 1))
SPLIT_ROWS = len(SPLIT_PRODUCTS) * HD_A
E_COLS = [SEQ - P * j for j in range(TILES)]
E_OFF = [sum(E_COLS[:j]) for j in range(TILES)]

DEPTH, HEADS_B, HD_B, WINDOW = 2, 8, 64, 64
INNER = HEADS_B * HD_B
CHUNKS = INNER // P
HID = int(DIM * 4 * 2 / 3)
HID_PARTS = [(0, P), (P, P), (2 * P, HID - 2 * P)]
QK_SCALE = 8.0
SPAN = P + WINDOW
PAD = SEQ + WINDOW
LN_EPS = 1e-5
NORM_MIN = 1e-12
MASKED = -1e30
FRONT_LOADS, TAIL_LOADS = 4, 2 + 3 * len(HID_PARTS) + 3
TWO = range(2)


def rope_freqs():
    return 1.0 / 10000.0 ** (np.arange(0, HD_A, 2) / HD_A)


def constants():

    bf = mybir.dt.np(BF16)
    c = {}
    c["ident"] = np.eye(P, dtype=np.float32)
    c["ident_b"] = np.eye(P).astype(bf)
    s, t = np.arange(P)[:, None], np.arange(SEQ)[None, :]
    c["before"] = (s < t).astype(np.float32)
    i, j = np.arange(P)[:, None], np.arange(P)[None, :]
    c["mask_a"] = np.stack([np.where(j > i, MASKED, 0), np.where(j < i, MASKED, 0)], 1).astype(bf)
    sums = np.zeros((P, 2, FREQS, 2 * HEADS_A))
    spread = np.zeros((P, 2, P))
    for f, fr in enumerate(rope_freqs()):
        co, si = np.cos(fr), np.sin(fr)
        for h in range(HEADS_A):
            rc, rs = slice(h * NODES, h * NODES + NODES), slice(HN + h * NODES, HN + h * NODES + NODES)
            sums[rc, 0, f, h], sums[rs, 0, f, HEADS_A + h] = 1, 1
            sums[rc, 1, f, h], sums[rs, 1, f, h] = co, -si
            sums[rc, 1, f, HEADS_A + h], sums[rs, 1, f, HEADS_A + h] = si, co
            for d in (f, f + FREQS):
                spread[2 * HEADS_A * f + h, 0, h * HD_A + d] = 1
                spread[2 * HEADS_A * f + HEADS_A + h, 1, h * HD_A + d] = -1 if d < FREQS else 1
    c["node_sums"] = sums.reshape(P, -1).astype(np.float32)
    c["spread"] = spread.reshape(P, -1).astype(np.float32)
    half = (np.arange(P) < HN).astype(np.float64)
    c["cols"] = np.stack([0.25 * half, np.pi / 2 * half, np.full(P, LN_EPS)], 1).astype(np.float32)
    shift = np.zeros((4, PAIRS, 2, SEQ))
    shift[0:2, :, 0], shift[2:4, :, 1] = -1, -1
    c["shift_rows"] = shift.astype(bf)
    jj = np.arange(SPAN)[None, :]
    band = np.where((jj - WINDOW <= i) & (jj >= i), 0, MASKED)
    first = np.where(jj >= WINDOW, band, MASKED)
    ahead = np.where((jj - i >= 0) & (jj - i <= WINDOW), 0, MASKED)
    c["mask_b"] = np.stack([first, band, ahead], 1).astype(bf)
    neg = np.zeros((P, HEADS_B, P))
    for h in range(HEADS_B):
        neg[2 * h:2 * h + 2, h] = -1
    c["neg_sel"] = neg.astype(bf)
    half_idx = np.arange(0, HD_B, 2, dtype=np.float64)
    inv = (1.0 / 10000.0 ** (half_idx / HD_B)).astype(np.float32)
    pos = np.arange(SEQ, dtype=np.float32)
    fr = (pos[:, None] * inv[None, :]).astype(np.float64)
    base = (half_idx + 0.4 * HD_B) / (1.4 * HD_B)
    sc = base[None, :] ** ((pos.astype(np.float64) - SEQ // 2) / (WINDOW // 2))[:, None]
    two = lambda a: np.concatenate([a, a], 1)
    signed = np.concatenate([-np.sin(fr), np.sin(fr)], 1)
    tab = np.stack([np.stack([two(np.cos(fr) * sc), two(np.cos(fr) / sc)], 1),
                    np.stack([signed * two(sc), signed / two(sc)], 1)], 1)
    c["xpos"] = tab.reshape(TILES, P, 2, 2, HD_B).transpose(1, 2, 0, 3, 4).reshape(P, -1).astype(np.float32)
    return c


def chain(eng, sem):
    count = [0]

    def link(ins):
        count[0] += 1
        ins.then_inc(sem, 1)
        eng.wait_ge(sem, count[0])
    return link


def bcast(ap, n):
    return ap.unsqueeze(len(ap.shape)).broadcast_to(list(ap.shape) + [n])


def bcast_mid(ap, axis, n):
    shape = list(ap.shape)
    return ap.unsqueeze(axis).broadcast_to(shape[:axis] + [n] + shape[axis:])


class Sems:

    def __init__(self, nc, ctx, names, prefix):
        self.all = {n: ctx.enter_context(nc.semaphore(f"{prefix}_{n}")) for n in names.split()}

    def __getitem__(self, n):
        return self.all[n]


PARTS, LAG = 6, 2
STEPS = PAIRS + LAG + 2
MAX_PARTS = ((0, (0, 1)), (1, (0, 1)), (2, (0,)), (2, (1,)), (3, (0,)), (3, (1,)))
T_PARTS = ((0, (0,)), (0, (1,)), (1, (0,)), (1, (1,)), (2, (0, 1)), (3, (0, 1)))
T_DONE = (2, 4, 5, 6)
MAXIMA_AT = 2
WHEN = {"turn x": (0, 1), "values": (1, 1), "node max": (1, 2), "node sums": (1, 4), "positions": (2, 0),
        "turn probs": (3, 0), "whole positions": (2, 3), "turns": (2, 4), "angle 0": (2, 5), "angle 1": (2, 5),
        "angle 2": (3, 1), "sines": (3, 1), "weighted sines": (3, 3), "node cosines": (4, 2), "cosines": (5, 0),
        "q": (5, 2), "k": (5, 5), "split": (6, 2), "attended": (1, 5), "turn attended": (2, 3), "project": (2, 4),
        "variance": (2, 4), "normalise": (3, 2), "turn output": (4, 5)}


def soft_rope_attention(nc, io, xs, scratch, loops=BATCH):
    ctx = ExitStack()
    with ctx:
        def sb(name, shape, dt=F32):
            return ctx.enter_context(nc.sbuf_tensor("a_" + name, shape, dt))

        ident, ident_b = sb("ident", [P, P]), sb("ident_b", [P, P], BF16)
        before, mask = sb("before", [P, SEQ]), sb("mask", [P, 2, P], BF16)
        node_sums, spread = sb("node_sums", [P, 2, FREQS, 2 * HEADS_A]), sb("spread", [P, 2, P])
        cols = sb("cols", [P, 3])
        w_vr, w_qk, w_o = sb("w_vr", [P, DIM + HN]), sb("w_qk", [P, 4, DIM]), sb("w_o", [P, DIM])
        x, xT = sb("x", [P, TILES, DIM]), sb("xT", [P, SEQ])
        lg, ex = sb("lg", [P, TILES, HN]), sb("ex", [P, TILES, HN])
        v1 = sb("v1", [P, TILES, HEADS_A, AUG])
        mx, sm, rsm = (sb(n, [P, TILES, HEADS_A]) for n in ("mx", "sm", "rsm"))
        prob = sb("prob", [P, TILES, 2, HN])
        probe = sb("probe", [P, TILES, HN])
        posc, pn, fr, pT, pnext, phere = (sb(n, [P, SEQ]) for n in ("posc", "pn", "fr", "pT", "pnext", "phere"))
        kk, zz = sb("kk", [P, 3, SEQ]), sb("zz", [P, 3, SEQ])
        G, U, V = (sb(n, [P, FREQS, SEQ]) for n in ("G", "U", "V"))
        cs, cw = sb("cs", [P, SEQ]), sb("cw", [P, 2, SEQ])
        tq, tk = kk[:, 0:2, :], zz[:, 0:2, :]
        qk, rem = sb("qk", [P, 2, SEQ]), sb("rem", [P, 2, SEQ])
        s3 = sb("s3", [P, 3, 2, SEQ], BF16)
        q6, k6 = ([sb(f"{n}{i}", [P, PAIRS, *e, SEQ], BF16) for i in TWO] for n, e in (("q6_", []), ("k6_", [2])))
        v2 = sb("v2", [P, TILES, HEADS_A * NODES * AUG + 64 - NODES * AUG])
        prob_q = sb("prob_q", [P, TILES, HN])
        mN, mS = sb("mN", [P, TILES, HEADS_A]), sb("mS", [P, TILES, HEADS_A, 2], BF16)
        E = [sb(f"E{i}", [P, 2, sum(E_COLS)]) for i in TWO]
        Ot = [sb(f"Ot{i}", [P, SEQ]) for i in TWO]
        Zn = sb("Zn", [P, TILES, HEADS_A, NODES * AUG])
        xr = sb("xr", [P, TILES, DIM])
        num, rden = sb("num", [P, TILES * HEADS_A, AUG]), sb("rden", [P, TILES * HEADS_A])
        att, aT = sb("att", [P, TILES, DIM]), sb("aT", [P, SEQ])
        y, y2, x1T = sb("y", [P, TILES, DIM]), sb("y2", [P, TILES, DIM]), sb("x1T", [P, SEQ])
        st, mv = sb("st", [P, TILES, 6]), sb("mv", [P, TILES, 2])
        lnv, rstd = sb("lnv", [P, TILES]), sb("rstd", [P, TILES])
        ps = ctx.enter_context(nc.psum_tensor("a_ps", [P, 8, SEQ], F32))
        RING_T, RING_M = (0, 1), (2, 3)
        PV, TURN = 4, 5
        F1, F2 = 6, 7

        ld = ctx.enter_context(nc.semaphore("a_consts_loaded"))
        zeroed = [ctx.enter_context(nc.semaphore(f"a_zeroed{i}")) for i in TWO]
        S = Sems(nc, ctx, """x_loaded x_ahead xT_ps xT_sb vr_ps lg_sb v1_sb lg_shifted ex_sb prob_sb pos_ps pT_ps pT_sb
            pn_sb parts_sb z_sb G_sb U_sb V_sb v2_sb qk_ps cs_ps cs_sb rope_ps cw_sb turned qk_sb split_sb split_out packed
            s_ps max_sb mS_sb mT_ps mT_sb sT_ps E_sb pv_ps Ot_sb tr_ps Z_sb prob_q_sb xr_loaded num_sb att_sb aT_ps aT_sb
            o_ps var_sb rstd_sb x1_sb x1T_ps x1T_sb stored dve_order pool_order act_order""", "a")

        with nc.Block() as block:
            @block.sync
            def _(sp):
                sp.dma_start(ident[:], io["ident"]).then_inc(ld, 16)
                sp.dma_start(ident_b[:], io["ident_b"]).then_inc(ld, 16)
                sp.dma_start(before[:], io["before"]).then_inc(ld, 16)
                sp.dma_start(mask[:], io["mask_a"]).then_inc(ld, 16)
                sp.dma_start(node_sums[:].rearrange("p a f m -> p (a f m)"), io["node_sums"]).then_inc(ld, 16)
                sp.dma_start(spread[:].rearrange("p a m -> p (a m)"), io["spread"]).then_inc(ld, 16)
                sp.dma_start(cols[:], io["cols"]).then_inc(ld, 16)
                sp.dma_start(w_vr[:], io["w_vr"]).then_inc(ld, 16)
                sp.dma_start(w_qk[:], io["w_qk"].rearrange("a p m -> p a m")).then_inc(ld, 16)
                sp.dma_start(w_o[:], io["w_o"]).then_inc(ld, 16)
                for i in TWO:
                    sp.wait_ge(zeroed[i], 1)
                    sp.dma_start(k6[i][2 * SPLIT_ROWS:2 * SPLIT_ROWS + 4, :, :, :], io["shift_rows"]).then_inc(ld, 16)
                sp.wait_ge(ld, 16 * 12)

            @block.gpsimd
            def _(pool):
                pool.memset(k6[0][:], 0.0).then_inc(zeroed[0], 1)
                pool.memset(v2[:], 0.0).then_inc(zeroed[0], 1)
                pool.memset(v1[:], 1.0).then_inc(zeroed[0], 1)

            @block.vector
            def _(dve):
                dve.memset(k6[1][:], 0.0).then_inc(zeroed[1], 1)

        M_ROWS = slice(2 * SPLIT_ROWS, 2 * SPLIT_ROWS + 4)

        def max_bank(parts, maxima):
            return RING_M[(parts + maxima) % 2]

        def turn(front, main, tail, now, ahead=None):
            q_now, k_now, q_next, k_next = q6[now], k6[now], q6[1 - now], k6[1 - now]

            def due(step, place, part):
                return part is not None and WHEN[step] == place

            with nc.Block() as block:
                @block.sync
                def _(sp):
                    if front is not None and not main:
                        sp.dma_start(x[:], io["L0_attn_x"][front].rearrange("(i p) e -> p i e", p=P)).then_inc(S["x_loaded"], 16)
                    if tail is not None:
                        sp.dma_start(xr[:], io["L0_attn_x"][tail].rearrange("(i p) e -> p i e", p=P)).then_inc(S["xr_loaded"], 16)
                    if tail is not None:
                        sp.wait_ge(S["x1T_sb"], 1)
                        sp.dma_start(xs[0, tail], x1T[:]).then_inc(S["stored"], 16)
                    if ahead is not None:
                        sp.wait_ge(S["xT_ps"], 1)
                        sp.dma_start(x[:], io["L0_attn_x"][ahead].rearrange("(i p) e -> p i e", p=P)).then_inc(S["x_ahead"], 16)
                    if front is not None:
                        sp.wait_ge(S["split_sb"], 1)
                        sp.dma_start(scratch.rearrange("s t h d n -> (h d) s t n"), s3[:]).then_inc(S["split_out"], 16)
                        sp.wait_ge(S["split_out"], 16)
                        for e in TWO:
                            for n, (qs, ks) in enumerate(SPLIT_PRODUCTS):
                                r = SPLIT_ROWS * e + HD_A * n
                                sp.dma_start(q_next[r:r + HD_A, :, :],
                                             scratch[qs, 0].rearrange("(p e) d n -> e d p n", e=2)[e]).then_inc(S["packed"], 16)
                                sp.dma_start(k_next[r:r + HD_A, :, e, :],
                                             scratch[ks, 1].rearrange("(p e) d n -> e d p n", e=2)[e]).then_inc(S["packed"], 16)
                        sp.wait_ge(S["packed"], 16 * 4 * len(SPLIT_PRODUCTS))
                    if ahead is not None:
                        sp.wait_ge(S["x_ahead"], 16)
                    if tail is not None:
                        sp.wait_ge(S["stored"], 16)

                @block.tensor
                def _(pe):
                    turned_pairs = [0]

                    def transposes(bank, src, done):
                        for i in range(TILES):
                            last = pe.transpose(ps[:, bank, P * i:P * i + P], src(i), ident[:])
                        last.then_inc(S[done], 1)

                    def front_and_tail(place):
                        if due("turn x", place, front):
                            if not main:
                                pe.wait_ge(S["x_loaded"], 16)
                            transposes(F1, lambda i: x[:, i, :], "xT_ps")
                        if due("values", place, front):
                            pe.wait_ge(S["xT_sb"], 1)
                            for bank, half in ((F2, 0), (F1, 1)):
                                for n in TWO:
                                    i, o = 2 * half + n, n * (DIM + HN)
                                    last = pe.matmul(ps[:, bank, o:o + DIM + HN], xT[:, P * i:P * i + P], w_vr[:], start=True, stop=True)
                                last.then_inc(S["vr_ps"], 1)
                        if due("positions", place, front):
                            pe.wait_ge(S["lg_sb"], 1)
                            pe.wait_ge(S["v1_sb"], 1)
                            pe.wait_ge(S["prob_sb"], 2)
                            for i in range(TILES):
                                last = pe.matmul(ps[:, F2, P * i:SEQ], prob[:, i, :, :].rearrange("p r n -> p (r n)"), before[:, 0:SEQ - P * i],
                                                 start=i == 0, stop=i == TILES - 1)
                            last.then_inc(S["pos_ps"], 1)
                        if due("turn probs", place, front):
                            pe.wait_ge(S["lg_sb"], 2)
                            pe.wait_ge(S["v1_sb"], 2)
                            transposes(F1, lambda i: prob[:, i, :, :].rearrange("p r n -> p (r n)"), "pT_ps")
                        if due("node cosines", place, front):
                            pe.wait_ge(S["U_sb"], 1)
                            pe.wait_ge(S["V_sb"], FREQS)
                            pe.wait_ge(S["pT_sb"], 1)
                            for n, src in enumerate((U, V)):
                                for f in range(FREQS):
                                    rows = slice(2 * HEADS_A * f, 2 * HEADS_A * (f + 1))
                                    last = pe.matmul(ps[rows, F1, :], node_sums[:, n, f, :], src[:, f, :], start=n == 0, stop=n == 1)
                            last.then_inc(S["cs_ps"], 1)
                        if due("cosines", place, front):
                            pe.wait_ge(S["cs_sb"], 1)
                            pe.wait_ge(S["pn_sb"], 1)
                            for t in TWO:
                                pe.matmul(ps[:, (F1, F2)[t], :], spread[:, t, :], cs[:], start=True, stop=True).then_inc(S["rope_ps"], 1)
                        for t, step in enumerate(("q", "k")):
                            if due(step, place, front):
                                if t == 0:
                                    pe.wait_ge(S["cw_sb"], 2)
                                else:
                                    pe.wait_ge(S["turned"], 1)
                                for n in TWO:
                                    last = pe.matmul(ps[:, (F1, F2)[n], :], w_qk[:, 2 * t + n, :], xT[:], start=True, stop=True)
                                last.then_inc(S["qk_ps"], 1)
                        if due("turn attended", place, tail):
                            pe.wait_ge(S["att_sb"], 1)
                            transposes(TURN, lambda i: att[:, i, :], "aT_ps")
                        if due("project", place, tail):
                            pe.wait_ge(S["aT_sb"], 1)
                            for i in range(TILES):
                                last = pe.matmul(ps[:, TURN, P * i:P * i + P], aT[:, P * i:P * i + P], w_o[:], start=True, stop=True)
                            last.then_inc(S["o_ps"], 1)
                        if due("turn output", place, tail):
                            if main:
                                pe.wait_ge(S["Z_sb"], 2 * turned_pairs[0])
                            pe.wait_ge(S["x1_sb"], TILES)
                            transposes(TURN, lambda i: y2[:, i, :], "x1T_ps")

                    used, read = [0], {}

                    def next_bank(signal, count):
                        bank = RING_M[used[0] % 2]
                        used[0] += 1
                        if bank in read:
                            pe.wait_ge(S[read[bank][0]], read[bank][1])
                        read[bank] = (signal, count)
                        return bank

                    def max_scores(p, part):
                        i, heads = MAX_PARTS[part]
                        bank, n = next_bank("max_sb", PARTS * p + part + 1), P * i + P
                        for at, e in enumerate(heads):
                            o = ps[:, bank, n * at:n * at + n]
                            pe.matmul(o, q_now[0:2 * SPLIT_ROWS, p, P * i:P * i + P], k_now[0:2 * SPLIT_ROWS, p, e, 0:n], start=True, stop=False)
                            last = pe.matmul(o[:, P * i:n], ident_b[:], mask[:, 0, :], start=False, stop=True)
                        last.then_inc(S["s_ps"], 1)

                    def turn_maxima(p):
                        bank = next_bank("mT_sb", p + 1)
                        pe.wait_ge(S["mS_sb"], 2 * (p + 1))
                        for i in range(TILES):
                            last = pe.transpose(ps[M_ROWS, bank, :].bitcast(BF16)[:, P * i:P * i + P],
                                                mS[:, i, 2 * p:2 * p + 2, :].rearrange("p h l -> p (h l)"), ident_b[:])
                        last.then_inc(S["mT_ps"], 1)

                    def scores(p, part):
                        j, heads = T_PARTS[part]
                        t, n = PARTS * p + part, E_COLS[j]
                        if part == 0:
                            pe.wait_ge(S["mT_sb"], p + 1)
                        if t >= 2:
                            pe.wait_ge(S["E_sb"], t - 1)
                        for at, e in enumerate(heads):
                            o = ps[:, RING_T[t % 2], n * at:n * at + n]
                            pe.matmul(o, k_now[0:2 * SPLIT_ROWS + 4, p, e, P * j:P * j + P], q_now[0:2 * SPLIT_ROWS + 4, p, P * j:SEQ],
                                      start=True, stop=False)
                            last = pe.matmul(o[:, 0:P], ident_b[:], mask[:, 1, :], start=False, stop=True)
                        last.then_inc(S["sT_ps"], 1)

                    def weighted(c, j):
                        if j == 0 and c >= 1:
                            pe.wait_ge(S["Ot_sb"], c)
                        pe.wait_ge(S["E_sb"], PARTS * c + T_DONE[j])
                        for e in TWO:
                            at = (2 * c + e) * NODES * AUG
                            last = pe.matmul(ps[64 * e:64 * e + 64, PV, P * j:SEQ], v2[:, j, at:at + 64],
                                             E[c % 2][:, e, E_OFF[j]:E_OFF[j] + E_COLS[j]], start=j == 0, stop=j == TILES - 1)
                        if j == TILES - 1:
                            last.then_inc(S["pv_ps"], 1)

                    def turn_weighted(c, place):
                        pe.wait_ge(S["Ot_sb"], c + 1)
                        if c >= 1:
                            pe.wait_ge(S["Z_sb"], 2 * c)
                        elif tail is not None:
                            pe.wait_ge(S["var_sb"], 1)
                        if tail is not None and WHEN["turn output"] < place:
                            pe.wait_ge(S["x1T_sb"], 1)
                        transposes(TURN, lambda i: Ot[c % 2][:, P * i:P * i + P], "tr_ps")
                        turned_pairs[0] += 1

                    for r in range(STEPS):
                        for part in range(PARTS):
                            if main and r < PAIRS:
                                max_scores(r, part)
                            if main and part == MAXIMA_AT and 1 <= r <= PAIRS:
                                turn_maxima(r - 1)
                            if main and LAG <= r < PAIRS + LAG:
                                scores(r - LAG, part)
                            if main and part == 1 and r >= LAG + 2:
                                turn_weighted(r - LAG - 2, (r, part))
                            if main and part >= 2 and LAG < r <= PAIRS + LAG:
                                weighted(r - LAG - 1, part - 2)
                            front_and_tail((r, part))

                @block.vector
                def _(dve):
                    link = chain(dve, S["dve_order"])
                    nodes = "p i (h n) -> p (i h) n"
                    flat = "p i h -> p (i h)"
                    fqs = rope_freqs()

                    def front_and_tail(place):
                        if due("node max", place, front):
                            dve.wait_ge(S["lg_sb"], 2)
                            link(dve.tensor_reduce(mx[:].rearrange(flat), lg[:].rearrange(nodes, n=NODES), AX_X, ALU.max))
                            dve.tensor_tensor(lg[:].rearrange(nodes, n=NODES), lg[:].rearrange(nodes, n=NODES),
                                              bcast(mx[:].rearrange(flat), NODES), ALU.subtract).then_inc(S["lg_shifted"], 1)
                        if due("node sums", place, front):
                            dve.wait_ge(S["ex_sb"], 1)
                            link(dve.tensor_reduce(sm[:].rearrange(flat), ex[:].rearrange(nodes, n=NODES), AX_X, ALU.add))
                            link(dve.reciprocal(rsm[:], sm[:]))
                            for r in TWO:
                                dve.tensor_tensor(prob[:, :, r, :].rearrange("p i (h n) -> p i h n", n=NODES),
                                                  ex[:].rearrange("p i (h n) -> p i h n", n=NODES), bcast(rsm[:], NODES),
                                                  ALU.mult).then_inc(S["prob_sb"], 1)
                        if due("whole positions", place, front):
                            dve.wait_ge(S["pos_ps"], 1)
                            link(dve.tensor_scalar(posc[:], ps[:, F2, :], 0.0, MAX_POS, ALU.max, ALU.min))
                            link(dve.tensor_scalar(pn[:], posc[:], -0.5, ROUND, ALU.add, ALU.add))
                            dve.tensor_scalar(pn[:], pn[:], ROUND, None, ALU.subtract).then_inc(S["pn_sb"], 1)
                        if due("turns", place, front):
                            dve.wait_ge(S["pn_sb"], 1)
                            for f in range(3):
                                ins = dve.tensor_scalar(kk[:, f, :], pn[:], float(fqs[f] / (2 * np.pi)), cols[:, 0:1], ALU.mult, ALU.add)
                                if f == 2:
                                    link(ins)
                                else:
                                    ins.then_inc(S["z_sb"], 1)
                            dve.wait_ge(S["z_sb"], 2)
                            link(dve.tensor_scalar(kk[:], kk[:], ROUND, ROUND, ALU.add, ALU.subtract))
                        for f, high in enumerate((6.28125, 62.8125, 628.3125)):
                            if due(f"angle {f}", place, front):
                                link(dve.scalar_tensor_tensor(zz[:, f, :], kk[:, f, :], -high, pn[:], ALU.mult, ALU.add))
                                dve.scalar_tensor_tensor(zz[:, f, :], kk[:, f, :], -float(2 * np.pi / fqs[f] - high), zz[:, f, :],
                                                         ALU.mult, ALU.add).then_inc(S["z_sb"], 1)
                        if due("weighted sines", place, front):
                            dve.wait_ge(S["parts_sb"], 3)
                            dve.wait_ge(S["G_sb"], FREQS)
                            dve.tensor_tensor(U[:], G[:], bcast_mid(phere[:], 1, FREQS), ALU.mult).then_inc(S["U_sb"], 1)
                        if due("q", place, front):
                            dve.wait_ge(S["qk_ps"], 1)
                            dve.wait_ge(S["cw_sb"], 2)
                            dve.tensor_tensor(tq, ps[:, F1:F2 + 1, :], cw[:], ALU.mult).then_inc(S["turned"], 1)
                        if due("k", place, front):
                            dve.wait_ge(S["qk_ps"], 2)
                            dve.wait_ge(S["G_sb"], FREQS)
                            dve.tensor_tensor(tk, ps[:, F1:F2 + 1, :], cw[:], ALU.mult).then_inc(S["turned"], 1)
                        if due("split", place, front):
                            dve.wait_ge(S["qk_sb"], 2)
                            link(dve.tensor_copy(s3[:, 0, :, :], qk[:]))
                            link(dve.tensor_tensor(rem[:], qk[:], s3[:, 0, :, :], ALU.subtract))
                            link(dve.tensor_copy(s3[:, 1, :, :], rem[:]))
                            dve.tensor_tensor(s3[:, 2, :, :], rem[:], s3[:, 1, :, :], ALU.subtract).then_inc(S["split_sb"], 1)
                        if due("attended", place, tail):
                            dve.tensor_reduce(num[:], Zn[:].rearrange("p i h (n d) -> p (i h) d n", n=NODES), AX_X, ALU.add).then_inc(S["num_sb"], 1)
                            dve.wait_ge(S["num_sb"], 1)
                            dve.reciprocal(rden[:], num[:, :, HD_A]).then_inc(S["num_sb"], 1)
                            dve.wait_ge(S["num_sb"], 2)
                            dve.tensor_tensor(att[:].rearrange("p i (h d) -> p (i h) d", d=HD_A), num[:, :, 0:HD_A], bcast(rden[:], HD_A),
                                              ALU.mult).then_inc(S["att_sb"], 1)
                        if due("variance", place, tail):
                            dve.wait_ge(S["o_ps"], 1)
                            dve.wait_ge(S["xr_loaded"], 16)
                            dve.tensor_tensor(y[:], ps[:, TURN, :].rearrange("p (i e) -> p i e", i=TILES), xr[:], ALU.add).then_inc(S["var_sb"], 1)
                            dve.wait_ge(S["var_sb"], 1)
                            for i in range(TILES):
                                dve.bn_stats(st[:, i, :], y[:, i, :]).then_inc(S["var_sb"], 1)
                            dve.wait_ge(S["var_sb"], 1 + TILES)
                            for i in range(TILES):
                                dve.bn_aggr(mv[:, i, :], st[:, i, :]).then_inc(S["var_sb"], 1)
                        if due("normalise", place, tail):
                            dve.wait_ge(S["var_sb"], 1 + 2 * TILES)
                            dve.wait_ge(S["rstd_sb"], 1)
                            for i in range(TILES):
                                dve.tensor_scalar(y2[:, i, :], y[:, i, :], mv[:, i, 0:1], rstd[:, i:i + 1], ALU.subtract, ALU.mult).then_inc(S["x1_sb"], 1)

                    for r in range(STEPS):
                        for part in range(PARTS):
                            if main and r < PAIRS:
                                i, heads = MAX_PARTS[part]
                                unit = PARTS * r + part
                                bank, n = max_bank(unit, max(0, r - (part <= MAXIMA_AT))), P * i + P
                                dve.wait_ge(S["s_ps"], unit + 1)
                                dve.tensor_reduce(mN[:, i, 2 * r + heads[0]:2 * r + heads[-1] + 1],
                                                  ps[:, bank, 0:len(heads) * n].rearrange("p (e n) -> p e n", n=n), AX_X, ALU.max).then_inc(S["max_sb"], 1)
                            if main and part == 0 and 1 <= r <= PAIRS:
                                heads = slice(2 * (r - 1), 2 * r)
                                dve.wait_ge(S["max_sb"], PARTS * r)
                                mh, ml = mS[:, :, heads, 0], mS[:, :, heads, 1]
                                dve.tensor_copy(mh, mN[:, :, heads]).then_inc(S["mS_sb"], 1)
                                dve.wait_ge(S["mS_sb"], 2 * r - 1)
                                dve.tensor_tensor(ml, mN[:, :, heads], mh, ALU.subtract).then_inc(S["mS_sb"], 1)
                            if main and part == 2 and r >= LAG + 2:
                                c = r - LAG - 2
                                if c == 0 and tail is not None:
                                    dve.wait_ge(S["num_sb"], 1)
                                dve.wait_ge(S["tr_ps"], c + 1)
                                for e in TWO:
                                    h = 2 * c + e
                                    src = ps[:, TURN, :].rearrange("p (i m) -> p i m", i=TILES)[:, :, 64 * e:64 * e + NODES * AUG]
                                    dve.tensor_tensor(Zn[:, :, h, :].rearrange("p i (n d) -> p i n d", n=NODES),
                                                      src.rearrange("p i (n d) -> p i n d", n=NODES),
                                                      bcast(prob_q[:, :, NODES * h:NODES * h + NODES], AUG), ALU.mult).then_inc(S["Z_sb"], 1)
                            front_and_tail((r, part))
                    if front is not None:
                        dve.wait_ge(S["prob_sb"], 1)
                        if main:
                            dve.wait_ge(S["Z_sb"], 2 * PAIRS)
                        dve.tensor_copy(prob_q[:], prob[:, :, 0, :]).then_inc(S["prob_q_sb"], 1)

                @block.scalar
                def _(act):
                    fqs = rope_freqs()

                    def front_and_tail(place):
                        if due("turn x", place, front):
                            act.wait_ge(S["xT_ps"], 1)
                            act.activation(xT[:], ps[:, F1, :], ACT.Copy).then_inc(S["xT_sb"], 1)
                        if due("values", place, front):
                            for half, bank in enumerate((F2, F1)):
                                act.wait_ge(S["vr_ps"], half + 1)
                                vr = ps[:, bank, 0:2 * (DIM + HN)].rearrange("p (i m) -> p i m", i=2)
                                act.activation(lg[:, 2 * half:2 * half + 2, :], vr[:, :, DIM:], ACT.Copy).then_inc(S["lg_sb"], 1)
                                act.activation(v1[:, 2 * half:2 * half + 2, :, 0:HD_A], vr[:, :, 0:DIM].rearrange("p i (h d) -> p i h d", d=HD_A),
                                               ACT.Copy).then_inc(S["v1_sb"], 1)
                        if due("node max", place, front):
                            act.wait_ge(S["lg_shifted"], 1)
                            act.activation(ex[:], lg[:], ACT.Exp).then_inc(S["ex_sb"], 1)
                        if due("turn probs", place, front):
                            act.wait_ge(S["pT_ps"], 1)
                            act.activation(pT[:], ps[:, F1, :], ACT.Copy).then_inc(S["pT_sb"], 1)
                        if due("sines", place, front):
                            act.wait_ge(S["pn_sb"], 1)
                            act.activation(G[:, 3, :], pn[:], ACT.Sin, bias=cols[:, 1:2], scale=float(fqs[3])).then_inc(S["G_sb"], 1)
                            for f in range(3):
                                act.wait_ge(S["z_sb"], 3 + f)
                                act.activation(G[:, f, :], zz[:, f, :], ACT.Sin, bias=cols[:, 1:2], scale=float(fqs[f])).then_inc(S["G_sb"], 1)
                            nc.scalar.preload_act_table_set("natural_log_exp_and_others")
                        if due("node cosines", place, front):
                            act.wait_ge(S["cs_ps"], 1)
                            act.activation(cs[:], ps[:, F1, :], ACT.Copy).then_inc(S["cs_sb"], 1)
                        if due("cosines", place, front):
                            for t in TWO:
                                act.wait_ge(S["rope_ps"], t + 1)
                                act.activation(cw[:, t, :], ps[:, (F1, F2)[t], :], ACT.Copy).then_inc(S["cw_sb"], 1)
                        if due("turn attended", place, tail):
                            act.wait_ge(S["aT_ps"], 1)
                            act.activation(aT[:], ps[:, TURN, :], ACT.Copy).then_inc(S["aT_sb"], 1)
                        if due("variance", place, tail):
                            act.wait_ge(S["var_sb"], 1 + 2 * TILES)
                            act.activation(lnv[:], mv[:, :, 1], ACT.Ln, bias=cols[:, 2:3]).then_inc(S["act_order"], 1)
                            act.wait_ge(S["act_order"], 1)
                            act.activation(rstd[:], lnv[:], ACT.Exp, scale=-0.5).then_inc(S["rstd_sb"], 1)
                        if due("turn output", place, tail):
                            act.wait_ge(S["x1T_ps"], 1)
                            act.activation(x1T[:], ps[:, TURN, :], ACT.Copy).then_inc(S["x1T_sb"], 1)

                    nc.scalar.preload_act_table_set("natural_log_exp_and_others")
                    for r in range(STEPS):
                        for part in range(PARTS):
                            if main and part == MAXIMA_AT and 1 <= r <= PAIRS:
                                p = r - 1
                                act.wait_ge(S["mT_ps"], p + 1)
                                bank = max_bank(PARTS * min(p + 1, PAIRS) + (MAXIMA_AT + 1 if p + 1 < PAIRS else 0), p)
                                act.activation(q_now[M_ROWS, p, :], ps[M_ROWS, bank, :].bitcast(BF16)[:, 0:SEQ], ACT.Copy).then_inc(S["mT_sb"], 1)
                            if main and LAG <= r < PAIRS + LAG:
                                p = r - LAG
                                t = PARTS * p + part
                                j, heads = T_PARTS[part]
                                if part == 0 and p >= 2:
                                    act.wait_ge(S["pv_ps"], p - 1)
                                act.wait_ge(S["sT_ps"], t + 1)
                                n = E_COLS[j]
                                act.activation(E[p % 2][:, heads[0]:heads[-1] + 1, E_OFF[j]:E_OFF[j] + n],
                                               ps[:, RING_T[t % 2], 0:len(heads) * n].rearrange("p (e n) -> p e n", n=n),
                                               ACT.Exp, scale=SCALE_A).then_inc(S["E_sb"], 1)
                            if main and part == PARTS - 1 and LAG < r <= PAIRS + LAG:
                                c = r - LAG - 1
                                act.wait_ge(S["pv_ps"], c + 1)
                                if c >= 2:
                                    act.wait_ge(S["tr_ps"], c - 1)
                                act.activation(Ot[c % 2][:], ps[:, PV, :], ACT.Copy).then_inc(S["Ot_sb"], 1)
                            front_and_tail((r, part))

                @block.gpsimd
                def _(pool):
                    if front is None:
                        return
                    pool.wait_ge(S["prob_sb"], 1)
                    pool.tensor_scalar(probe[:], prob[:, :, 0, :], 1e-8, None, ALU.add).then_inc(S["pool_order"], 1)
                    pool.wait_ge(S["pn_sb"], 1)
                    pool.tensor_tensor(fr[:], posc[:], pn[:], ALU.subtract).then_inc(S["parts_sb"], 1)
                    pool.wait_ge(S["parts_sb"], 1)
                    pool.wait_ge(S["pT_sb"], 1)
                    pool.tensor_tensor(pnext[:], pT[:], fr[:], ALU.mult).then_inc(S["parts_sb"], 1)
                    pool.wait_ge(S["parts_sb"], 2)
                    pool.tensor_tensor(phere[:], pT[:], pnext[:], ALU.subtract).then_inc(S["parts_sb"], 1)
                    for n, f in enumerate((3, 0, 1, 2)):
                        pool.wait_ge(S["G_sb"], n + 1)
                        pool.tensor_tensor(V[:, f, :], G[:, f, :], pnext[:], ALU.mult).then_inc(S["V_sb"], 1)
                    for n, t in enumerate((tq, tk)):
                        pool.wait_ge(S["turned"], n + 1)
                        pool.tensor_tensor(qk[:, n, :], t[:, 0, :], t[:, 1, :], ALU.add).then_inc(S["qk_sb"], 1)
                    pool.wait_ge(S["pool_order"], 1)
                    pool.wait_ge(S["v1_sb"], 2)
                    for c in range(PAIRS):
                        if main:
                            pool.wait_ge(S["pv_ps"], c + 1)
                        for e in TWO:
                            h = 2 * c + e
                            dst = v2[:, :, h * NODES * AUG:(h + 1) * NODES * AUG].rearrange("p i (n d) -> p i n d", n=NODES)
                            pool.tensor_tensor(dst, bcast(probe[:, :, NODES * h:NODES * h + NODES], AUG),
                                               bcast_mid(v1[:, :, h, :], 2, NODES), ALU.mult).then_inc(S["v2_sb"], 1)

            end_turn(nc, S)

        turn(front=0, main=False, tail=None, now=1, ahead=1)
        turn(front=1, main=True, tail=None, now=0, ahead=2 if loops > 2 else None)
        with nc.Fori(0, (loops - 4) // 2) as n:
            for k in TWO:
                turn(front=2 * n + k + 2, main=True, tail=2 * n + k, now=1 - k, ahead=2 * n + k + 3)
        turn(front=loops - 2, main=True, tail=loops - 4, now=1, ahead=loops - 1)
        turn(front=loops - 1, main=True, tail=loops - 3, now=0)
        turn(front=None, main=True, tail=loops - 2, now=1)
        turn(front=None, main=False, tail=loops - 1, now=0)


def end_turn(nc, *stages):
    nums = sorted(s.num for stage in stages for s in stage.all.values())
    starts = [n for n in nums if n - 1 not in nums]
    ends = [n + 1 for n in nums if n + 1 not in nums]
    for a, z in zip(starts, ends):
        nc.all_engine_barrier(sems_to_clear=range(a, z))


PARTS_B = 4
STEPS_B = CHUNKS + 1
PLACES_B = PARTS_B * STEPS_B
MAX_UNITS = 4 * CHUNKS
WHEN_B = {"tile 0": 0, "tile 1": 1, "tile 2": 2, "tile 3": 2, "clamp": 3, "norms": 3, "newton": 4, "turn 0": 5,
          "turn 1": 6, "turn 2": 7, "turn 3": 8, "split maxima": 18, "turn maxima": 19, "project": 0, "mean": 2,
          "variance": 4, "gate 0": 6, "gate 1": 7, "gate 2": 9, "gelu": 9, "gated 0": 11, "gated 1": 12,
          "gated 2": 13, "output": 15}
MAX_FROM, MAX_EACH = 10, 2


def local_attention_layers(nc, io, xs, loops=BATCH, depth=DEPTH):
    ctx = ExitStack()
    with ctx:
        def sb(name, shape, dt=F32):
            return ctx.enter_context(nc.sbuf_tensor("b_" + name, shape, dt))

        def two(name, shape, dt=F32):
            return [sb(f"{name}{u}", shape, dt) for u in TWO]

        ident, ident_b, ones = sb("ident", [P, P]), sb("ident_b", [P, P], BF16), sb("ones", [P, 64])
        mean_w = sb("mean_w", [P, P])
        mask, neg_sel = sb("mask", [P, 3, SPAN], BF16), sb("neg_sel", [P, HEADS_B, P], BF16)
        tab = sb("tab", [P, 2, TILES, 2, HD_B])
        scales = sb("scales", [P, 2, HD_B])
        cols = sb("cols", [P, 3])
        w_qkv, w_o = sb("w_qkv", [P, 3 * INNER]), sb("w_o", [P, CHUNKS, DIM])
        w1, w2 = sb("w1", [P, 2 * HID]), sb("w2", [P, 3, DIM])
        vec = sb("vec", [P, 3])
        b1 = sb("b1", [P, 2, 3])
        hT = sb("hT", [P, SEQ])
        raw, rot, sq = (two(n, [P, 2 * INNER]) for n in ("raw", "rot", "sq"))
        W = sb("W", [P, TILES * 2 * INNER])
        ss, lns, r0, cor, rn = (sb(n, [P, TILES, 2 * HEADS_B]) for n in ("ss", "lns", "r0", "cor", "rn"))
        QTb, KMb = sb("QTb", [P, CHUNKS, SEQ], BF16), sb("KMb", [P, CHUNKS, 2, PAD], BF16)
        mN, mS = sb("mN", [P, TILES, HEADS_B]), sb("mS", [P, TILES, HEADS_B, 2], BF16)
        v = two("v", [P, TILES, INNER])
        QT = two("QT", [P, CHUNKS, PAD])
        KM = two("KM", [P, CHUNKS, 2, PAD])
        mT = two("mT", [P, PAD], BF16)
        E, rd = two("E", [P, 2, TILES, SPAN]), sb("rd", [P, SEQ])
        oT = sb("oT", [P, CHUNKS, SEQ])
        xT, x1, h2, hc, sq2, rs = (sb(n, [P, SEQ]) for n in ("xT", "x1", "h2", "hc", "sq2", "rs"))
        gl = sb("gl", [P, 3, SEQ])
        ps = ctx.enter_context(nc.psum_tensor("b_ps", [P, 8, SEQ], F32))
        FRONT = (0, 1, 2)
        RING_T, NUM, DEN = (3, 4), 5, 6
        TAIL = 7

        ld = ctx.enter_context(nc.semaphore("b_consts_loaded"))
        zeroed = [ctx.enter_context(nc.semaphore(f"b_zeroed{i}")) for i in TWO]
        S = Sems(nc, ctx, """h_loaded h_ahead qkv_ps raw_sb v_sb sq_sb ss_sb U_sb V_sb V2_sb lns_sb r0_sb newton rn_sb W_sb Wn_sb Wk_sb qT_ps kT_ps
            QT_sb KM_sb QTb_sb KMb_sb s_ps max_sb mS_sb mT_ps mT_sb sT_ps E_sb num_ps lnd_sb rd_sb oT_sb x_loaded wo_ps x1_sb h2_sb
            mean_ps hc_sb sq2_sb var_ps lnv_sb rs_sb hn_sb g_ps gb_sb gl_sb a_ps u_sb w2_ps xo_sb stored
            front_w tail_w tabled""", "b")

        def load_front_weights(eng, l):
            eng.dma_start(tab[:].rearrange("p a i t d -> p (a i t d)"), io["xpos"]).then_inc(S["front_w"], 16)
            eng.dma_start(w_qkv[:], io["L0_ffn_wqkv"][l]).then_inc(S["front_w"], 16)
            for n, name in enumerate(("q_scale", "k_scale")):
                eng.dma_start(scales[:, n, :], io["L0_ffn_" + name][l].partition_broadcast(P)).then_inc(S["front_w"], 16)

        def scale_tables(dve):
            dve.wait_ge(S["front_w"], 16 * FRONT_LOADS)
            for i in range(TILES):
                dve.tensor_tensor(tab[:, 0, i, :, :], tab[:, 0, i, :, :], scales[:], ALU.mult).then_inc(S["tabled"], 1)
                for half in range(2):
                    a, o = half * HD_B // 2, (1 - half) * HD_B // 2
                    dve.tensor_tensor(tab[:, 1, i, :, a:a + HD_B // 2], tab[:, 1, i, :, a:a + HD_B // 2],
                                      scales[:, :, o:o + HD_B // 2], ALU.mult).then_inc(S["tabled"], 1)

        def load_tail_weights(eng, l):
            eng.dma_start(w_o[:], io["L0_ffn_wo"][l].rearrange("(c p) m -> p c m", p=P)).then_inc(S["tail_w"], 16)
            eng.dma_start(w1[:], io["L0_ffn_w1"][l]).then_inc(S["tail_w"], 16)
            for c, (o, n) in enumerate(HID_PARTS):
                eng.dma_start(w2[0:n, c, :], io["L0_ffn_w2"][l][o:o + n, :]).then_inc(S["tail_w"], 16)
                for g in range(2):
                    eng.dma_start(b1[0:n, g, c:c + 1], io["L0_ffn_b1"][l][g * HID + o:g * HID + o + n].unsqueeze(1)).then_inc(S["tail_w"], 16)
            for n, name in enumerate(("ln_g", "ln_b", "b2")):
                eng.dma_start(vec[:, n:n + 1], io["L0_ffn_" + name][l].unsqueeze(1)).then_inc(S["tail_w"], 16)

        def turn(front, main, tail, now, ahead=None, next_front=None, next_tail=None):
            nxt = 1 - now

            def due(step, place, part):
                return part is not None and WHEN_B[step] == place

            def max_bank(unit):
                return FRONT[unit % 3]

            def turn_half(eng, i, half, done):
                heads = "p (t h d) -> p t h d"
                a, o = half * HD_B // 2, (1 - half) * HD_B // 2
                eng.tensor_tensor(rot[i % 2][:].rearrange(heads, t=2, d=HD_B)[:, :, :, a:a + HD_B // 2],
                                  raw[i % 2][:].rearrange(heads, t=2, d=HD_B)[:, :, :, o:o + HD_B // 2],
                                  bcast_mid(tab[:, 1, i, :, a:a + HD_B // 2], 2, HEADS_B), ALU.mult).then_inc(S[done], 1)

            with nc.Block() as block:
                @block.sync
                def _(sp):
                    def load_shifted(l, b, done):
                        sp.dma_start(hT[0:64, :], xs[l, b, 0:64, :]).then_inc(S[done], 16)
                        sp.dma_start(hT[64:P, 1:SEQ], xs[l, b, 64:P, 0:SEQ - 1]).then_inc(S[done], 16)

                    if front is not None and not main:
                        load_shifted(*front, "h_loaded")
                    if tail is not None:
                        sp.dma_start(xT[:], xs[tail[0], tail[1]]).then_inc(S["x_loaded"], 16)
                    if next_front is not None:
                        sp.wait_ge(S["qkv_ps"], 3 * TILES)
                        sp.wait_ge(S["U_sb"], TILES)
                        sp.wait_ge(S["V_sb"], TILES)
                        sp.wait_ge(S["V2_sb"], TILES)
                        load_front_weights(sp, next_front)
                    if ahead is not None:
                        sp.wait_ge(S["qkv_ps"], 3 * TILES)
                        load_shifted(*ahead, "h_ahead")
                    if tail is not None:
                        sp.wait_ge(S["xo_sb"], 1)
                        sp.dma_start(xs[tail[0] + 1, tail[1]], xT[:]).then_inc(S["stored"], 16)
                    if next_tail is not None:
                        load_tail_weights(sp, next_tail)
                        sp.wait_ge(S["tail_w"], 16 * TAIL_LOADS)
                    if ahead is not None:
                        sp.wait_ge(S["h_ahead"], 32)
                    if tail is not None:
                        sp.wait_ge(S["stored"], 16)

                @block.tensor
                def _(pe):
                    def front_and_tail(place):
                        for i in range(TILES):
                            if due(f"tile {i}", place, front):
                                if i == 0 and not main:
                                    pe.wait_ge(S["h_loaded"], 32)
                                if i >= 1:
                                    pe.wait_ge(S["raw_sb"], i)
                                for n in range(3):
                                    if i >= 1 and n == 2:
                                        pe.wait_ge(S["v_sb"], i)
                                    pe.matmul(ps[:, FRONT[n], :], hT[:, P * i:P * i + P], w_qkv[:, INNER * n:INNER * n + INNER],
                                              start=True, stop=True).then_inc(S["qkv_ps"], 1)
                            if due(f"turn {i}", place, front):
                                for n, done in enumerate(("qT_ps", "kT_ps")):
                                    if i == 0 and n == 0:
                                        pe.wait_ge(S["raw_sb"], TILES)
                                    if n == 0:
                                        pe.wait_ge(S["Wn_sb"], i + 1)
                                        if i >= 1:
                                            pe.wait_ge(S["QTb_sb"], i)
                                    else:
                                        pe.wait_ge(S["Wk_sb"], i + 1)
                                        if i >= 1:
                                            pe.wait_ge(S["KM_sb"], 2 * i)
                                    for c in range(CHUNKS):
                                        at = 2 * INNER * i + INNER * n + P * c
                                        last = pe.transpose(ps[:, FRONT[n], P * c:P * c + P], W[:, at:at + P], ident[:])
                                    last.then_inc(S[done], 1)
                        if front is not None and MAX_FROM <= place < MAX_FROM + MAX_UNITS // MAX_EACH:
                            for k in range(MAX_EACH):
                                unit = MAX_EACH * (place - MAX_FROM) + k
                                c, half, e = unit // 4, unit // 2 % 2, unit % 2
                                if unit == 0:
                                    pe.wait_ge(S["v_sb"], TILES)
                                    pe.wait_ge(S["KM_sb"], 2 * TILES)
                                    pe.wait_ge(S["QTb_sb"], TILES)
                                    pe.wait_ge(S["KMb_sb"], 2 * TILES)
                                if unit >= 3:
                                    pe.wait_ge(S["max_sb"], unit - 2)
                                for n in TWO:
                                    i = 2 * half + n
                                    o = ps[:, max_bank(unit), SPAN * n:SPAN * n + SPAN]
                                    pe.matmul(o, QTb[:, c, P * i:P * i + P], KMb[:, c, e, P * i:P * i + SPAN], start=True, stop=False)
                                    last = pe.matmul(o, ident_b[:], mask[:, min(i, 1), :], start=False, stop=True)
                                last.then_inc(S["s_ps"], 1)
                        if due("turn maxima", place, front):
                            pe.wait_ge(S["mS_sb"], 2)
                            for i in range(TILES):
                                last = pe.transpose(ps[0:2 * HEADS_B, FRONT[0], :].bitcast(BF16)[:, P * i:P * i + P],
                                                    mS[:, i, :, :].rearrange("p h l -> p (h l)"), ident_b[:])
                            last.then_inc(S["mT_ps"], 1)
                        if due("project", place, tail):
                            for c in range(CHUNKS):
                                last = pe.matmul(ps[:, TAIL, :], w_o[:, c, :], oT[:, c, :], start=c == 0, stop=c == CHUNKS - 1)
                            last.then_inc(S["wo_ps"], 1)
                        if due("mean", place, tail):
                            pe.wait_ge(S["h2_sb"], 2)
                            pe.matmul(ps[:, TAIL, :], mean_w[:], h2[:], start=True, stop=True).then_inc(S["mean_ps"], 1)
                        if due("variance", place, tail):
                            pe.wait_ge(S["sq2_sb"], 1)
                            pe.matmul(ps[:, TAIL, :], mean_w[:], sq2[:], start=True, stop=True).then_inc(S["var_ps"], 1)
                        for c, (o, n) in enumerate(HID_PARTS):
                            if due(f"gate {c}", place, tail):
                                if c == 0:
                                    pe.wait_ge(S["hn_sb"], 2)
                                else:
                                    pe.wait_ge(S["gb_sb"], c)
                                pe.matmul(ps[0:n, TAIL, :], w1[:, HID + o:HID + o + n], h2[:], start=True, stop=True).then_inc(S["g_ps"], 1)
                            if due(f"gated {c}", place, tail):
                                if c == 0:
                                    pe.wait_ge(S["gb_sb"], 3)
                                else:
                                    pe.wait_ge(S["u_sb"], c)
                                pe.matmul(ps[0:n, TAIL, :], w1[:, o:o + n], h2[:], start=True, stop=True).then_inc(S["a_ps"], 1)
                        if due("output", place, tail):
                            pe.wait_ge(S["u_sb"], 3)
                            for c, (o, n) in enumerate(HID_PARTS):
                                last = pe.matmul(ps[:, TAIL, :], w2[0:n, c, :], gl[0:n, c, :], start=c == 0, stop=c == 2)
                            last.then_inc(S["w2_ps"], 1)

                    for place in range(PLACES_B):
                        r, part = place // PARTS_B, place % PARTS_B
                        if main and r < CHUNKS:
                            half, e = part // 2, part % 2
                            t = PARTS_B * r + part
                            if t >= 2:
                                pe.wait_ge(S["E_sb"], t - 1)
                            for n in TWO:
                                j = 2 * half + n
                                o = ps[:, RING_T[t % 2], SPAN * n:SPAN * n + SPAN]
                                pe.matmul(o, KM[now][:, r, e, WINDOW + P * j:WINDOW + P * j + P], QT[now][:, r, P * j:P * j + SPAN],
                                          start=True, stop=False)
                                pe.matmul(o, neg_sel[:, 2 * r + e, :], mT[now][:, P * j:P * j + SPAN], start=False, stop=False)
                                last = pe.matmul(o, ident_b[:], mask[:, 2, :], start=False, stop=True)
                            last.then_inc(S["sT_ps"], 1)
                        if main and r >= 1:
                            c, j = r - 1, part
                            if j == 0 and c >= 1:
                                pe.wait_ge(S["oT_sb"], c)
                            pe.wait_ge(S["E_sb"], PARTS_B * c + 2 * (j // 2) + 2)
                            n = min(SPAN, SEQ - P * j)
                            for bank in (NUM, DEN):
                                for e in TWO:
                                    h = 2 * c + e
                                    lhs = v[now][:, j, HD_B * h:HD_B * h + HD_B] if bank == NUM else ones[:]
                                    last = pe.matmul(ps[64 * e:64 * e + 64, bank, P * j:P * j + n], lhs, E[c % 2][:, e, j, 0:n],
                                                     start=j == 0, stop=j == TILES - 1, skip_group_check=True)
                            if j == TILES - 1:
                                last.then_inc(S["num_ps"], 1)
                        front_and_tail(place)

                @block.vector
                def _(dve):
                    heads = "p (t h d) -> p t h d"

                    def front_and_tail(place):
                        if due("newton", place, front):
                            dve.wait_ge(S["r0_sb"], 1)
                            link = chain(dve, S["newton"])
                            link(dve.tensor_tensor(cor[:], r0[:], r0[:], ALU.mult))
                            link(dve.tensor_tensor(cor[:], cor[:], ss[:], ALU.mult))
                            link(dve.tensor_scalar(cor[:], cor[:], -0.5, 1.5, ALU.mult, ALU.add))
                            dve.tensor_tensor(rn[:], r0[:], cor[:], ALU.mult).then_inc(S["rn_sb"], 1)
                        for i in range(TILES):
                            if due(f"tile {i}", place, front):
                                at = 2 * INNER * i
                                src = raw[i % 2][:].rearrange(heads, t=2, d=HD_B)
                                dve.wait_ge(S["raw_sb"], i + 1)
                                dve.tensor_tensor(W[:, at:at + 2 * INNER].rearrange(heads, t=2, d=HD_B), src,
                                                  bcast_mid(tab[:, 0, i, :, :], 2, HEADS_B), ALU.mult).then_inc(S["U_sb"], 1)
                                if i >= 2:
                                    dve.wait_ge(S["W_sb"], i - 1)
                                turn_half(dve, i, 0, "V_sb")
                                dve.wait_ge(S["sq_sb"], i + 1)
                                dve.tensor_reduce(ss[:, i, :], sq[i % 2][:].rearrange("p (h d) -> p h d", d=HD_B), AX_X, ALU.add).then_inc(S["ss_sb"], 1)
                            if due(f"turn {i}", place, front):
                                if i == 0:
                                    normalise(0)
                                if i + 1 < TILES:
                                    normalise(i + 1)
                                dve.wait_ge(S["kT_ps"], i + 1)
                                src = ps[:, FRONT[1], :].rearrange("p (c n) -> p c n", c=CHUNKS)
                                for e in TWO:
                                    rows = slice(64 * e, 64 * e + 64)
                                    dve.tensor_copy(KM[nxt][rows, :, e, WINDOW + P * i:WINDOW + P * i + P], src[rows]).then_inc(S["KM_sb"], 1)
                        if due("clamp", place, front):
                            dve.wait_ge(S["ss_sb"], TILES)
                            dve.tensor_scalar(ss[:], ss[:], NORM_MIN ** 2, None, ALU.max).then_inc(S["ss_sb"], 1)
                        if front is not None and MAX_FROM <= place < MAX_FROM + MAX_UNITS // MAX_EACH:
                            for k in range(MAX_EACH):
                                unit = MAX_EACH * (place - MAX_FROM) + k
                                c, half, e = unit // 4, unit // 2 % 2, unit % 2
                                dve.wait_ge(S["s_ps"], unit + 1)
                                dve.tensor_reduce(mN[:, 2 * half:2 * half + 2, 2 * c + e],
                                                  ps[:, max_bank(unit), 0:2 * SPAN].rearrange("p (n s) -> p n s", n=2), AX_X, ALU.max).then_inc(S["max_sb"], 1)
                        if due("split maxima", place, front):
                            dve.wait_ge(S["max_sb"], MAX_UNITS)
                            dve.tensor_copy(mS[:, :, :, 0], mN[:]).then_inc(S["mS_sb"], 1)
                            dve.wait_ge(S["mS_sb"], 1)
                            dve.tensor_tensor(mS[:, :, :, 1], mN[:], mS[:, :, :, 0], ALU.subtract).then_inc(S["mS_sb"], 1)
                        if due("project", place, tail):
                            dve.wait_ge(S["wo_ps"], 1)
                            dve.wait_ge(S["x_loaded"], 16)
                            dve.tensor_tensor(x1[:], ps[:, TAIL, :], xT[:], ALU.add).then_inc(S["x1_sb"], 1)
                            dve.wait_ge(S["x1_sb"], 1)
                            dve.tensor_copy(h2[0:64, :], x1[0:64, :]).then_inc(S["h2_sb"], 1)
                            dve.tensor_copy(h2[64:P, 1:SEQ], x1[64:P, 0:SEQ - 1]).then_inc(S["h2_sb"], 1)
                        if due("mean", place, tail):
                            dve.wait_ge(S["h2_sb"], 2)
                            dve.wait_ge(S["mean_ps"], 1)
                            dve.tensor_tensor(hc[:], h2[:], ps[:, TAIL, :], ALU.subtract).then_inc(S["hc_sb"], 1)
                        if due("variance", place, tail):
                            dve.wait_ge(S["hc_sb"], 1)
                            dve.wait_ge(S["rs_sb"], 1)
                            dve.tensor_tensor(hc[:], hc[:], rs[:], ALU.mult).then_inc(S["hn_sb"], 1)
                            dve.wait_ge(S["hn_sb"], 1)
                            dve.tensor_scalar(h2[:], hc[:], vec[:, 0:1], vec[:, 1:2], ALU.mult, ALU.add).then_inc(S["hn_sb"], 1)
                        for c, (o, n) in enumerate(HID_PARTS):
                            if due(f"gate {c}", place, tail):
                                dve.wait_ge(S["g_ps"], c + 1)
                                dve.tensor_scalar(gl[0:n, c, :], ps[0:n, TAIL, :], b1[0:n, 1, c:c + 1], None, ALU.add).then_inc(S["gb_sb"], 1)
                            if due(f"gated {c}", place, tail):
                                dve.wait_ge(S["gl_sb"], 2)
                                dve.wait_ge(S["a_ps"], c + 1)
                                dve.scalar_tensor_tensor(gl[0:n, c, :], ps[0:n, TAIL, :], b1[0:n, 0, c:c + 1], gl[0:n, c, :],
                                                         ALU.add, ALU.mult).then_inc(S["u_sb"], 1)
                        if due("output", place, tail):
                            dve.wait_ge(S["w2_ps"], 1)
                            dve.scalar_tensor_tensor(xT[:], ps[:, TAIL, :], vec[:, 2:3], x1[:], ALU.add, ALU.add).then_inc(S["xo_sb"], 1)
                            dve.memset(h2[64:P, 0:1], 0.0).then_inc(S["xo_sb"], 1)

                    def normalise(i):
                        dve.wait_ge(S["rn_sb"], 1)
                        dve.wait_ge(S["W_sb"], i + 1)
                        w = W[:, 2 * INNER * i:2 * INNER * i + INNER].rearrange("p (h d) -> p h d", d=HD_B)
                        dve.tensor_tensor(w, w, bcast(rn[:, i, 0:HEADS_B], HD_B), ALU.mult).then_inc(S["Wn_sb"], 1)

                    for place in range(PLACES_B):
                        r, part = place // PARTS_B, place % PARTS_B
                        if main and r >= 1 and part == PARTS_B - 1:
                            c = r - 1
                            if c == 0 and tail is not None:
                                dve.wait_ge(S["wo_ps"], 1)
                            dve.wait_ge(S["num_ps"], c + 1)
                            dve.wait_ge(S["rd_sb"], c + 1)
                            dve.tensor_tensor(oT[:, c, :], ps[:, NUM, :], rd[:], ALU.mult).then_inc(S["oT_sb"], 1)
                        front_and_tail(place)
                    if next_front is not None:
                        scale_tables(dve)

                @block.scalar
                def _(act):
                    def front_and_tail(place):
                        for i in range(TILES):
                            if due(f"tile {i}", place, front):
                                if i >= 2:
                                    act.wait_ge(S["U_sb"], i - 1)
                                    act.wait_ge(S["V_sb"], i - 1)
                                    act.wait_ge(S["V2_sb"], i - 1)
                                    act.wait_ge(S["ss_sb"], i - 1)
                                act.wait_ge(S["qkv_ps"], 3 * i + 2)
                                act.activation(raw[i % 2][:].rearrange("p (t n) -> p t n", t=2), ps[:, FRONT[0]:FRONT[1] + 1, :], ACT.Copy).then_inc(S["raw_sb"], 1)
                                act.wait_ge(S["qkv_ps"], 3 * i + 3)
                                act.activation(v[nxt][:, i, :], ps[:, FRONT[2], :], ACT.Copy).then_inc(S["v_sb"], 1)
                                act.wait_ge(S["raw_sb"], i + 1)
                                act.activation(sq[i % 2][:], raw[i % 2][:], ACT.Square).then_inc(S["sq_sb"], 1)
                            if due(f"turn {i}", place, front):
                                act.wait_ge(S["qT_ps"], i + 1)
                                src = ps[:, FRONT[0], :].rearrange("p (c n) -> p c n", c=CHUNKS)
                                act.activation(QT[nxt][:, :, P * i:P * i + P], src, ACT.Copy).then_inc(S["QT_sb"], 1)
                                act.activation(QTb[:, :, P * i:P * i + P], src, ACT.Copy).then_inc(S["QTb_sb"], 1)
                                act.wait_ge(S["KM_sb"], 2 * (i + 1))
                                for e in TWO:
                                    rows, cs = slice(64 * e, 64 * e + 64), slice(WINDOW + P * i, WINDOW + P * i + P)
                                    act.activation(KMb[rows, :, e, cs], KM[nxt][rows, :, e, cs], ACT.Copy).then_inc(S["KMb_sb"], 1)
                        if due("norms", place, front):
                            act.wait_ge(S["ss_sb"], TILES + 1)
                            act.activation(lns[:], ss[:], ACT.Ln).then_inc(S["lns_sb"], 1)
                            act.wait_ge(S["lns_sb"], 1)
                            act.activation(r0[:], lns[:], ACT.Exp, scale=-0.5).then_inc(S["r0_sb"], 1)
                        if due("turn maxima", place, front):
                            act.wait_ge(S["mT_ps"], 1)
                            act.activation(mT[nxt][0:2 * HEADS_B, 0:SEQ], ps[0:2 * HEADS_B, FRONT[0], :].bitcast(BF16)[:, 0:SEQ], ACT.Copy).then_inc(S["mT_sb"], 1)
                        if due("mean", place, tail):
                            act.wait_ge(S["hc_sb"], 1)
                            act.activation(sq2[:], hc[:], ACT.Square).then_inc(S["sq2_sb"], 1)
                        if due("variance", place, tail):
                            act.wait_ge(S["var_ps"], 1)
                            act.activation(rs[:], ps[:, TAIL, :], ACT.Ln, bias=cols[:, 2:3]).then_inc(S["lnv_sb"], 1)
                            act.wait_ge(S["lnv_sb"], 1)
                            act.activation(rs[:], rs[:], ACT.Exp, scale=-0.5).then_inc(S["rs_sb"], 1)
                        if due("gelu", place, tail):
                            act.wait_ge(S["gb_sb"], 3)
                            n = HID_PARTS[2][1]
                            act.activation(gl[:, 0:2, :], gl[:, 0:2, :], ACT.Gelu).then_inc(S["gl_sb"], 1)
                            act.activation(gl[0:n, 2, :], gl[0:n, 2, :], ACT.Gelu).then_inc(S["gl_sb"], 1)
                            nc.scalar.preload_act_table_set("natural_log_exp_and_others")

                    nc.scalar.preload_act_table_set("natural_log_exp_and_others")
                    for place in range(PLACES_B):
                        r, part = place // PARTS_B, place % PARTS_B
                        if main and r < CHUNKS:
                            half, e = part // 2, part % 2
                            t = PARTS_B * r + part
                            if part == 0 and r >= 2:
                                act.wait_ge(S["num_ps"], r - 1)
                            act.wait_ge(S["sT_ps"], t + 1)
                            act.activation(E[r % 2][:, e, 2 * half:2 * half + 2, :], ps[:, RING_T[t % 2], 0:2 * SPAN].rearrange("p (n s) -> p n s", n=2),
                                           ACT.Exp, scale=QK_SCALE).then_inc(S["E_sb"], 1)
                        if main and r >= 1 and part == PARTS_B - 1:
                            c = r - 1
                            act.wait_ge(S["num_ps"], c + 1)
                            if c >= 1:
                                act.wait_ge(S["oT_sb"], c)
                            act.activation(rd[:], ps[:, DEN, :], ACT.Ln).then_inc(S["lnd_sb"], 1)
                            act.wait_ge(S["lnd_sb"], c + 1)
                            act.activation(rd[:], rd[:], ACT.Exp, scale=-1.0).then_inc(S["rd_sb"], 1)
                        front_and_tail(place)

                @block.gpsimd
                def _(pool):
                    if front is None:
                        return
                    for i in range(TILES):
                        w = W[:, 2 * INNER * i:2 * INNER * (i + 1)]
                        pool.wait_ge(S["raw_sb"], i + 1)
                        turn_half(pool, i, 1, "V2_sb")
                        pool.wait_ge(S["U_sb"], i + 1)
                        pool.wait_ge(S["V_sb"], i + 1)
                        pool.wait_ge(S["V2_sb"], i + 1)
                        pool.tensor_tensor(w, w, rot[i % 2][:], ALU.add).then_inc(S["W_sb"], 1)
                    for i in range(TILES):
                        w = W[:, 2 * INNER * i + INNER:2 * INNER * (i + 1)].rearrange("p (h d) -> p h d", d=HD_B)
                        pool.wait_ge(S["rn_sb"], 1)
                        pool.wait_ge(S["W_sb"], i + 1)
                        pool.tensor_tensor(w, w, bcast(rn[:, i, HEADS_B:], HD_B), ALU.mult).then_inc(S["Wk_sb"], 1)

            end_turn(nc, S)

        with nc.Block() as block:
            @block.sync
            def _(sp):
                load_front_weights(sp, 0)
                sp.dma_start(ident[:], io["ident"]).then_inc(ld, 16)
                sp.dma_start(ident_b[:], io["ident_b"]).then_inc(ld, 16)
                sp.dma_start(mask[:], io["mask_b"]).then_inc(ld, 16)
                sp.dma_start(neg_sel[:], io["neg_sel"]).then_inc(ld, 16)
                sp.dma_start(cols[:], io["cols"]).then_inc(ld, 16)
                sp.wait_ge(ld, 80)

            @block.scalar
            def _(act):
                load_tail_weights(act, 0)
                act.wait_ge(S["tail_w"], 16 * TAIL_LOADS)

            @block.gpsimd
            def _(pool):
                for buf in (KM[0], QT[0], mT[0], hT, h2):
                    pool.memset(buf[:], 0.0).then_inc(zeroed[0], 1)
                pool.memset(ones[:], 1.0).then_inc(zeroed[0], 1)
                pool.memset(mean_w[:], 1.0 / DIM).then_inc(zeroed[0], 1)

            @block.vector
            def _(dve):
                for buf in (KM[1], KMb, QT[1], mT[1]):
                    dve.memset(buf[:], 0.0).then_inc(zeroed[1], 1)
                scale_tables(dve)

        end_turn(nc, S)

        def middle(l, ahead, next_front):
            with nc.Fori(0, (loops - 4) // 2) as n:
                for k in TWO:
                    turn(front=(l, 2 * n + k + 2), main=True, tail=(l, 2 * n + k), now=1 - k, ahead=(l, 2 * n + k + 3))
            turn(front=(l, loops - 2), main=True, tail=(l, loops - 4), now=1, ahead=(l, loops - 1))
            turn(front=(l, loops - 1), main=True, tail=(l, loops - 3), now=0, ahead=ahead, next_front=next_front)

        turn(front=(0, 0), main=False, tail=None, now=1, ahead=(0, 1))
        turn(front=(0, 1), main=True, tail=None, now=0, ahead=(0, 2))
        with nc.Fori(0, depth - 1) as l:
            middle(l, ahead=(l + 1, 0), next_front=l + 1)
            turn(front=(l + 1, 0), main=True, tail=(l, loops - 2), now=1, ahead=(l + 1, 1))
            turn(front=(l + 1, 1), main=True, tail=(l, loops - 1), now=0, ahead=(l + 1, 2), next_tail=l + 1)
        middle(depth - 1, ahead=None, next_front=None)
        turn(front=None, main=True, tail=(depth - 1, loops - 2), now=1)
        turn(front=None, main=False, tail=(depth - 1, loops - 1), now=0)


def final_layernorm(nc, io, xs, out, loops=BATCH):
    GROUP = 4
    with ExitStack() as ctx:
        def sb(name, shape, dt=F32):
            return ctx.enter_context(nc.sbuf_tensor("c_" + name, shape, dt))

        ident, cols = sb("ident", [P, P]), sb("cols", [P, 3])
        xa, xb, xsum = (sb(n, [P, GROUP, SEQ]) for n in ("xa", "xb", "xsum"))
        st, mv = sb("st", [P, GROUP, TILES, 6]), sb("mv", [P, GROUP, TILES, 2])
        nrm, rstd = sb("nrm", [P, GROUP, TILES]), sb("rstd", [P, GROUP, TILES])
        y = sb("y", [P, GROUP, TILES, DIM])
        ps = ctx.enter_context(nc.psum_tensor("c_ps", [P, GROUP, SEQ], F32))
        ld = ctx.enter_context(nc.semaphore("c_consts_loaded"))
        S = Sems(nc, ctx, " ".join(f"a_loaded{u} b_loaded{u}" for u in range(GROUP)) + " sum_sb y_ps st_sb mv_sb nrm_sb rstd_sb y_sb stored", "c")

        with nc.Block() as block:
            @block.sync
            def _(sp):
                sp.dma_start(ident[:], io["ident"]).then_inc(ld, 16)
                sp.dma_start(cols[:], io["cols"]).then_inc(ld, 16)
                sp.wait_ge(ld, 32)

        xs2 = xs.rearrange("l (b u) p n -> l b u p n", u=GROUP)
        out2 = out.rearrange("(b u) (i p) e -> b u p i e", u=GROUP, p=P)
        with nc.Fori(0, loops // GROUP) as b:
            with nc.Block() as block:
                @block.sync
                def _(sp):
                    for u in range(GROUP):
                        sp.dma_start(xa[:, u, :], xs2[0, b, u]).then_inc(S[f"a_loaded{u}"], 16)
                    for u in range(GROUP):
                        sp.wait_ge(S["y_sb"], TILES * (u + 1))
                        sp.dma_start(out2[b, u], y[:, u, :, :]).then_inc(S["stored"], 16)
                    sp.wait_ge(S["stored"], 16 * GROUP)

                @block.tensor
                def _(pe):
                    for u in range(GROUP):
                        pe.wait_ge(S["sum_sb"], u + 1)
                        for i in range(TILES):
                            last = pe.transpose(ps[:, u, P * i:P * i + P], xsum[:, u, P * i:P * i + P], ident[:])
                        last.then_inc(S["y_ps"], 1)

                @block.vector
                def _(dve):
                    def total(u):
                        dve.wait_ge(S[f"a_loaded{u}"], 16)
                        dve.wait_ge(S[f"b_loaded{u}"], 16)
                        dve.tensor_tensor(xsum[:, u, :], xa[:, u, :], xb[:, u, :], ALU.add).then_inc(S["sum_sb"], 1)

                    def statistics(u):
                        dve.wait_ge(S["y_ps"], u + 1)
                        for i in range(TILES):
                            dve.bn_stats(st[:, u, i, :], ps[:, u, P * i:P * i + P]).then_inc(S["st_sb"], 1)
                        dve.wait_ge(S["st_sb"], TILES * (u + 1))
                        for i in range(TILES):
                            dve.bn_aggr(mv[:, u, i, :], st[:, u, i, :]).then_inc(S["mv_sb"], 1)

                    def normalise(u):
                        dve.wait_ge(S["mv_sb"], TILES * (u + 1))
                        dve.wait_ge(S["nrm_sb"], u + 1)
                        dve.reciprocal(rstd[:, u, :], nrm[:, u, :]).then_inc(S["rstd_sb"], 1)
                        dve.wait_ge(S["rstd_sb"], u + 1)
                        for i in range(TILES):
                            dve.tensor_scalar(y[:, u, i, :], ps[:, u, P * i:P * i + P], mv[:, u, i, 0:1], rstd[:, u, i:i + 1],
                                              ALU.subtract, ALU.mult).then_inc(S["y_sb"], 1)

                    for u in range(GROUP + 2):
                        if u < GROUP:
                            total(u)
                        if 1 <= u <= GROUP:
                            statistics(u - 1)
                        if u >= 2:
                            normalise(u - 2)

                @block.scalar
                def _(act):
                    for u in range(GROUP):
                        act.dma_start(xb[:, u, :], xs2[DEPTH, b, u]).then_inc(S[f"b_loaded{u}"], 16)
                    for u in range(GROUP):
                        act.wait_ge(S["mv_sb"], TILES * (u + 1))
                        act.activation(nrm[:, u, :], mv[:, u, :, 1], ACT.Sqrt, bias=cols[:, 2:3]).then_inc(S["nrm_sb"], 1)

            end_turn(nc, S)


DIRECT = ["L0_attn_x"] + ["L0_ffn_" + n for n in ("wqkv", "q_scale", "k_scale", "wo", "ln_g", "ln_b", "w1", "b1", "w2", "b2")]


def lay_out(inputs):
    arrays = {n: np.ascontiguousarray(inputs[n]) for n in DIRECT}
    wq, wk, wv, wr, wo = (np.asarray(inputs["L0_attn_W" + n]) for n in "qkvro")
    other_half = np.arange(DIM).reshape(HEADS_A, 2, FREQS)[:, ::-1].reshape(DIM)
    arrays["w_vr"] = np.concatenate([wv, wr], 1)
    arrays["w_qk"] = np.stack([wq, wq[:, other_half], wk, wk[:, other_half]])
    arrays["w_o"] = np.ascontiguousarray(wo)
    arrays.update(constants())
    return arrays


def build(nc, io, out):
    xs = nc.dram_tensor("xs", [DEPTH + 1, BATCH, DIM, SEQ], F32).ap()
    scratch = nc.dram_tensor("split_qk", [3, 2, HEADS_A, HD_A, SEQ], BF16).ap()
    soft_rope_attention(nc, io, xs, scratch)
    local_attention_layers(nc, io, xs)
    final_layernorm(nc, io, xs, out)


def kernel(**inputs):
    import concourse.bacc as bacc
    from concourse.bass_utils import run_bass_kernel_spmd

    nc = bacc.Bacc("TRN2", target_bir_lowering=False, num_devices=1)
    arrays = lay_out(inputs)
    io = {n: nc.dram_tensor(f"in_{n}_dram", a.shape, mybir.dt.from_np(a.dtype), kind="ExternalInput").ap() for n, a in arrays.items()}
    out = nc.dram_tensor("out_0_dram", (BATCH, SEQ, DIM), F32, kind="ExternalOutput").ap()
    build(nc, io, out)
    r = run_bass_kernel_spmd(nc, [{f"in_{n}_dram": a for n, a in arrays.items()}], core_ids=[0])
    return r.results[0]["out_0_dram"]
```
